# Optimizing a Trainium2 kernel written in Bass

```python
import numpy as np
import jax
import jax.numpy as jnp

def _softmax(x, axis=-1):
    return jax.nn.softmax(x, axis=axis)

def _gelu(x):
    return jax.nn.gelu(x, approximate=True)

def _silu(x):
    return jax.nn.silu(x)

def _sigmoid(x):
    return jax.nn.sigmoid(x)

def _layernorm(x, axis=-1, eps=1e-05):
    m = jnp.mean(x, axis=axis, keepdims=True)
    v = jnp.var(x, axis=axis, keepdims=True)
    return (x - m) / jnp.sqrt(v + eps)

def _scatter_add(tgt, idx, src, axis=0):
    return tgt.at[idx].add(src)

def _segment_sum(src, seg, n):
    return jax.ops.segment_sum(src, seg, n)
kernel_name = 'mk_vit_tower_cls_d2_tok_img256_r4_eb1afe'

def setup_inputs(seed: int=0):
    np.random.seed(seed)
    _w = jnp.asarray

    def _rec_inputs():
        import jax
        import jax.numpy as jnp
        _rk = jax.random.key(seed)
        x = -0.000222058 + 0.999998 * jax.random.normal(jax.random.fold_in(_rk, 1), (64, 3, 96, 96), jnp.float32)
        cls_tok = 0.02 * jax.random.normal(jax.random.fold_in(_rk, 5), (1, 1, 64), jnp.float32)
        return (x, cls_tok)
    x, cls_tok = _rec_inputs()

    def _L0_tok_setup():
        import jax, jax.numpy as jnp
        import numpy as np
        IMAGE_SIZE = 64
        PATCH = 16
        EMBED_DIM = 64
        IN_CH = 3
        BATCH = 128
        IN_DIM = IN_CH * PATCH * PATCH

        def _patchify(x, p):
            B, C, H, Wd = x.shape
            x = x.reshape(B, C, H // p, p, Wd // p, p)
            x = x.transpose(0, 2, 4, 1, 3, 5)
            return x.reshape(B, H // p * (Wd // p), C * p * p)
        key = jax.random.key(seed)
        kx, kw, kb = jax.random.split(key, 3)
        x = jax.random.normal(kx, (BATCH, IN_CH, IMAGE_SIZE, IMAGE_SIZE), dtype=jnp.float32)
        W = jax.random.normal(kw, (EMBED_DIM, IN_DIM), dtype=jnp.float32) * (1.0 / np.sqrt(IN_DIM))
        b = jax.random.normal(kb, (EMBED_DIM,), dtype=jnp.float32) * 0.01
        return {'x': x, 'W': W, 'b': b}
    _L0_tok_all = _L0_tok_setup()
    _L0_tok_in = {k: v for k, v in _L0_tok_all.items() if k in ('W', 'b')}
    del _L0_tok_all

    def _L0_attn_setup():
        import jax, jax.numpy as jnp
        import numpy as np
        D_ATT = 64
        D_GROUP = 32
        N_GROUP = D_ATT // D_GROUP
        key = jax.random.key(seed)
        ks = jax.random.split(key, 6)
        B, L = (4, 128)
        import math
        s = 1.0 / math.sqrt(D_ATT)
        return {'x': jax.random.normal(ks[0], (B, L, D_ATT), dtype=jnp.float32), 'Wq': jax.random.normal(ks[1], (D_ATT, D_ATT), dtype=jnp.float32) * s * 0.06, 'Wk': jax.random.normal(ks[2], (D_ATT, D_ATT), dtype=jnp.float32) * s * 0.06, 'Wv': jax.random.normal(ks[3], (D_ATT, D_ATT), dtype=jnp.float32) * s * 0.06, 'w_mlp': jax.random.normal(ks[4], (D_GROUP,), dtype=jnp.float32) * 0.1, 'b_mlp': jax.random.normal(ks[5], (1,), dtype=jnp.float32) * 0.1}
    _L0_attn_all = _L0_attn_setup()
    _L0_attn_in = {k: v for k, v in _L0_attn_all.items() if k in ('Wq', 'Wk', 'Wv', 'w_mlp', 'b_mlp')}
    del _L0_attn_all

    def _L0_ffn_setup():
        import jax, jax.numpy as jnp
        import numpy as np
        B, T, C = (64, 96, 64)
        NH, NKV = (4, 2)
        HD = C // NH
        NREP = NH // NKV
        NE, TOPK = (8, 2)
        HID = int(8 / 3 * C)
        EPS_RMS = 1e-06

        def _rope_tables(t_len):
            inv_freq = 1.0 / 10000.0 ** (np.arange(0, HD, 2, dtype=np.float32) / HD)
            t = np.arange(t_len, dtype=np.float32)
            freqs = np.outer(t, inv_freq)
            emb = np.concatenate([freqs, freqs], axis=-1)
            return (jnp.asarray(np.cos(emb)), jnp.asarray(np.sin(emb)))

        def _rotate_half(x):
            h = x.shape[-1] // 2
            return jnp.concatenate([-x[..., h:], x[..., :h]], axis=-1)

        def _rmsnorm(v, w):
            return v * jax.lax.rsqrt(jnp.mean(v * v, axis=-1, keepdims=True) + EPS_RMS) * w
        key = jax.random.key(seed)
        ks = jax.random.split(key, 10)
        s = lambda k, shape: jax.random.normal(k, shape, jnp.float32) * 0.02
        return {'x': jax.random.normal(ks[0], (B, T, C), jnp.float32), 'ln1_w': jnp.ones((C,), jnp.float32), 'ln2_w': jnp.ones((C,), jnp.float32), 'wq': s(ks[1], (NH * HD, C)), 'wk': s(ks[2], (NKV * HD, C)), 'wv': s(ks[3], (NKV * HD, C)), 'wo': s(ks[4], (C, C)), 'router_w': s(ks[5], (NE, C)), 'w1': s(ks[6], (NE, HID, C)), 'w2': s(ks[7], (NE, C, HID)), 'w3': s(ks[8], (NE, HID, C))}
    _L0_ffn_all = _L0_ffn_setup()
    _L0_ffn_in = {k: v for k, v in _L0_ffn_all.items() if k in ('ln1_w', 'ln2_w', 'wq', 'wk', 'wv', 'wo', 'router_w', 'w1', 'w2', 'w3')}
    del _L0_ffn_all

    def _L1_attn_setup():
        import jax, jax.numpy as jnp
        import numpy as np
        N_HEADS, EMB, KQ = (8, 64, 64)
        BATCH, SEQ = (4, 512)
        key = jax.random.key(seed)
        ks = jax.random.split(key, 5)
        x = jax.random.normal(ks[0], (BATCH, SEQ, EMB), dtype=jnp.float32)
        key_matrices = 0.1 * jax.random.normal(ks[1], (N_HEADS, EMB, KQ), dtype=jnp.float32)
        query_matrices = 0.1 * jax.random.normal(ks[2], (N_HEADS, EMB, KQ), dtype=jnp.float32)
        value_in_matrices = 0.1 * jax.random.normal(ks[3], (N_HEADS, EMB, KQ), dtype=jnp.float32)
        value_out_matrices = 0.1 * jax.random.normal(ks[4], (N_HEADS, KQ, EMB), dtype=jnp.float32)
        return {'x': x, 'key_matrices': key_matrices, 'query_matrices': query_matrices, 'value_in_matrices': value_in_matrices, 'value_out_matrices': value_out_matrices}
    _L1_attn_all = _L1_attn_setup()
    _L1_attn_in = {k: v for k, v in _L1_attn_all.items() if k in ('key_matrices', 'query_matrices', 'value_in_matrices', 'value_out_matrices')}
    del _L1_attn_all

    def _L1_ffn_setup():
        import jax, jax.numpy as jnp
        import numpy as np
        DIM = 64
        HEADS = 8
        NUM_KEYS = 64
        NUM_KV = NUM_KEYS ** 2
        PK_TOPK = 16
        FINAL_TOPK = 16
        DIM_KEY = DIM // 2
        P = 2

        def _pk(x, Wq_pk, pk_keys):
            b, n, _ = x.shape
            q = (x @ Wq_pk).reshape(b, n, P, HEADS, DIM_KEY).transpose(2, 0, 1, 3, 4)
            sim = jnp.einsum('pbnhd,pkhd->pbnhk', q, pk_keys)
            scores, idx = jax.lax.top_k(sim, PK_TOPK)
            idx0 = idx[0]
            idx1 = idx[1] * NUM_KEYS
            index = (idx0[..., :, None] + idx1[..., None, :]).reshape(b, n, HEADS, PK_TOPK * PK_TOPK)
            score = (scores[0][..., :, None] + scores[1][..., None, :]).reshape(b, n, HEADS, PK_TOPK * PK_TOPK)
            final_scores, pk_idx = jax.lax.top_k(score, FINAL_TOPK)
            final_indices = jnp.take_along_axis(index, pk_idx, axis=-1)
            final_scores = jax.nn.softmax(final_scores, axis=-1)
            return (final_scores, final_indices)
        key = jax.random.key(seed)
        ks = jax.random.split(key, 7)
        b, n = (2, 256)
        std = 0.02
        x = jax.random.normal(ks[0], (b, n, DIM), dtype=jnp.float32)
        Wq_pk = jax.random.normal(ks[1], (DIM, P * HEADS * DIM_KEY), dtype=jnp.float32) * std
        pk_keys = jax.random.normal(ks[2], (P, NUM_KEYS, HEADS, DIM_KEY), dtype=jnp.float32) * std
        Wq = jax.random.normal(ks[3], (DIM, HEADS * DIM), dtype=jnp.float32) * std
        keys_table = jax.random.normal(ks[4], (NUM_KV * HEADS, DIM), dtype=jnp.float32) * std
        values_table = jax.random.normal(ks[5], (NUM_KV * HEADS, DIM), dtype=jnp.float32) * std
        Wo = jax.random.normal(ks[6], (DIM * HEADS, DIM), dtype=jnp.float32) * std
        return {'x': x, 'Wq_pk': Wq_pk, 'pk_keys': pk_keys, 'Wq': Wq, 'keys_table': keys_table, 'values_table': values_table, 'Wo': Wo}
    _L1_ffn_all = _L1_ffn_setup()
    _L1_ffn_in = {k: v for k, v in _L1_ffn_all.items() if k in ('Wq_pk', 'pk_keys', 'Wq', 'keys_table', 'values_table', 'Wo')}
    del _L1_ffn_all
    return {'x': x, 'cls_tok': cls_tok, 'L0_tok_W': _L0_tok_in['W'], 'L0_tok_b': _L0_tok_in['b'], 'L0_attn_Wq': _L0_attn_in['Wq'], 'L0_attn_Wk': _L0_attn_in['Wk'], 'L0_attn_Wv': _L0_attn_in['Wv'], 'L0_attn_w_mlp': _L0_attn_in['w_mlp'], 'L0_attn_b_mlp': _L0_attn_in['b_mlp'], 'L0_ffn_ln1_w': _L0_ffn_in['ln1_w'], 'L0_ffn_ln2_w': _L0_ffn_in['ln2_w'], 'L0_ffn_wq': _L0_ffn_in['wq'], 'L0_ffn_wk': _L0_ffn_in['wk'], 'L0_ffn_wv': _L0_ffn_in['wv'], 'L0_ffn_wo': _L0_ffn_in['wo'], 'L0_ffn_router_w': _L0_ffn_in['router_w'], 'L0_ffn_w1': _L0_ffn_in['w1'], 'L0_ffn_w2': _L0_ffn_in['w2'], 'L0_ffn_w3': _L0_ffn_in['w3'], 'L1_attn_key_matrices': _L1_attn_in['key_matrices'], 'L1_attn_query_matrices': _L1_attn_in['query_matrices'], 'L1_attn_value_in_matrices': _L1_attn_in['value_in_matrices'], 'L1_attn_value_out_matrices': _L1_attn_in['value_out_matrices'], 'L1_ffn_Wq_pk': _L1_ffn_in['Wq_pk'], 'L1_ffn_pk_keys': _L1_ffn_in['pk_keys'], 'L1_ffn_Wq': _L1_ffn_in['Wq'], 'L1_ffn_keys_table': _L1_ffn_in['keys_table'], 'L1_ffn_values_table': _L1_ffn_in['values_table'], 'L1_ffn_Wo': _L1_ffn_in['Wo']}

def reference(x, cls_tok, L0_tok_W, L0_tok_b, L0_attn_Wq, L0_attn_Wk, L0_attn_Wv, L0_attn_w_mlp, L0_attn_b_mlp, L0_ffn_ln1_w, L0_ffn_ln2_w, L0_ffn_wq, L0_ffn_wk, L0_ffn_wv, L0_ffn_wo, L0_ffn_router_w, L0_ffn_w1, L0_ffn_w2, L0_ffn_w3, L1_attn_key_matrices, L1_attn_query_matrices, L1_attn_value_in_matrices, L1_attn_value_out_matrices, L1_ffn_Wq_pk, L1_ffn_pk_keys, L1_ffn_Wq, L1_ffn_keys_table, L1_ffn_values_table, L1_ffn_Wo):
    import jax
    import jax.numpy as jnp

    def _L0_tok_ref(x, W, b):
        import jax, jax.numpy as jnp
        import numpy as np
        IMAGE_SIZE = 64
        PATCH = 16
        EMBED_DIM = 64
        IN_CH = 3
        BATCH = 128
        IN_DIM = IN_CH * PATCH * PATCH

        def _patchify(x, p):
            B, C, H, Wd = x.shape
            x = x.reshape(B, C, H // p, p, Wd // p, p)
            x = x.transpose(0, 2, 4, 1, 3, 5)
            return x.reshape(B, H // p * (Wd // p), C * p * p)
        patches = _patchify(x, PATCH)
        return jnp.einsum('bnk,ek->bne', patches, W) + b

    def _L0_attn_ref(x, Wq, Wk, Wv, w_mlp, b_mlp):
        import jax, jax.numpy as jnp
        import numpy as np
        D_ATT = 64
        D_GROUP = 32
        N_GROUP = D_ATT // D_GROUP
        B, L, d_att = x.shape
        G, Dg = (N_GROUP, D_GROUP)
        Q = x @ Wq.T
        K = x @ Wk.T
        V = x @ Wv.T
        Qg = Q.reshape(B, L, 1, G, Dg)
        Kg = K.reshape(B, 1, L, G, Dg)
        diff = Qg - Kg
        attn = jnp.einsum('bqkgd,d->bqkg', jax.nn.relu(diff), w_mlp) + b_mlp[0]
        attn = jax.nn.relu(attn)
        attn = jax.nn.softmax(attn, axis=2)
        Vg = V.reshape(B, L, Dg, G)
        out = jnp.einsum('bqkg,bkdg->bqdg', attn, Vg)
        return out.reshape(B, L, d_att)

    def _L0_ffn_ref(x, ln1_w, ln2_w, wq, wk, wv, wo, router_w, w1, w2, w3):
        import jax, jax.numpy as jnp
        import numpy as np
        B, T, C = (64, 96, 64)
        NH, NKV = (4, 2)
        HD = C // NH
        NREP = NH // NKV
        NE, TOPK = (8, 2)
        HID = int(8 / 3 * C)
        EPS_RMS = 1e-06

        def _rope_tables(t_len):
            inv_freq = 1.0 / 10000.0 ** (np.arange(0, HD, 2, dtype=np.float32) / HD)
            t = np.arange(t_len, dtype=np.float32)
            freqs = np.outer(t, inv_freq)
            emb = np.concatenate([freqs, freqs], axis=-1)
            return (jnp.asarray(np.cos(emb)), jnp.asarray(np.sin(emb)))

        def _rotate_half(x):
            h = x.shape[-1] // 2
            return jnp.concatenate([-x[..., h:], x[..., :h]], axis=-1)

        def _rmsnorm(v, w):
            return v * jax.lax.rsqrt(jnp.mean(v * v, axis=-1, keepdims=True) + EPS_RMS) * w
        Bx, Tx, Cx = x.shape
        h = _rmsnorm(x, ln1_w)
        q = (h @ wq.T).reshape(Bx, Tx, NH, HD).transpose(0, 2, 1, 3)
        k = (h @ wk.T).reshape(Bx, Tx, NKV, HD).transpose(0, 2, 1, 3)
        v = (h @ wv.T).reshape(Bx, Tx, NKV, HD).transpose(0, 2, 1, 3)
        cos, sin = _rope_tables(Tx)
        cos, sin = (cos[None, None], sin[None, None])
        q = q * cos + _rotate_half(q) * sin
        k = k * cos + _rotate_half(k) * sin
        k = jnp.repeat(k, NREP, axis=1)
        v = jnp.repeat(v, NREP, axis=1)
        scores = jnp.einsum('bhtd,bhsd->bhts', q, k) / jnp.sqrt(jnp.float32(HD))
        causal = jnp.tril(jnp.ones((Tx, Tx), dtype=bool))
        scores = jnp.where(causal[None, None], scores, jnp.float32(-1e+30))
        att = jax.nn.softmax(scores, axis=-1)
        y = jnp.einsum('bhts,bhsd->bhtd', att, v).transpose(0, 2, 1, 3).reshape(Bx, Tx, Cx)
        x = x + y @ wo.T
        flat = _rmsnorm(x, ln2_w).reshape(-1, Cx)
        probs = jax.nn.softmax(flat @ router_w.T, axis=-1)
        tp, ti = jax.lax.top_k(probs, TOPK)
        tp = tp / (jnp.sum(tp, axis=-1, keepdims=True) + 1e-09)
        weights = jnp.sum(tp[..., None] * jax.nn.one_hot(ti, NE, dtype=flat.dtype), axis=1)
        out = jnp.zeros_like(flat)
        for e in range(NE):
            hh = jax.nn.silu(flat @ w1[e].T) * (flat @ w3[e].T)
            out = out + weights[:, e:e + 1] * (hh @ w2[e].T)
        return x + out.reshape(Bx, Tx, Cx)

    def _L1_attn_ref(x, key_matrices, query_matrices, value_in_matrices, value_out_matrices):
        import jax, jax.numpy as jnp
        import numpy as np
        N_HEADS, EMB, KQ = (8, 64, 64)
        BATCH, SEQ = (4, 512)
        seq_len = x.shape[1]
        queries = jnp.einsum('ned,bse->nbsd', query_matrices, x)
        keys = jnp.einsum('ned,bse->nbsd', key_matrices, x)
        kq = jnp.einsum('nbjd,nbkd->nbjk', keys, queries)
        mask = jnp.triu(jnp.ones((seq_len, seq_len), dtype=bool), k=1)
        kq = jnp.where(mask, -jnp.inf, kq)
        attention_pattern = jax.nn.softmax(kq, axis=3)
        v = jnp.einsum('bjp,npd->nbjd', x, value_in_matrices)
        ctx = jnp.einsum('nbsj,nbjd->nbsd', attention_pattern, v)
        return jnp.einsum('nbsd,nde->bse', ctx, value_out_matrices)

    def _L1_ffn_ref(x, Wq_pk, pk_keys, Wq, keys_table, values_table, Wo):
        import jax, jax.numpy as jnp
        import numpy as np
        DIM = 64
        HEADS = 8
        NUM_KEYS = 64
        NUM_KV = NUM_KEYS ** 2
        PK_TOPK = 16
        FINAL_TOPK = 16
        DIM_KEY = DIM // 2
        P = 2

        def _pk(x, Wq_pk, pk_keys):
            b, n, _ = x.shape
            q = (x @ Wq_pk).reshape(b, n, P, HEADS, DIM_KEY).transpose(2, 0, 1, 3, 4)
            sim = jnp.einsum('pbnhd,pkhd->pbnhk', q, pk_keys)
            scores, idx = jax.lax.top_k(sim, PK_TOPK)
            idx0 = idx[0]
            idx1 = idx[1] * NUM_KEYS
            index = (idx0[..., :, None] + idx1[..., None, :]).reshape(b, n, HEADS, PK_TOPK * PK_TOPK)
            score = (scores[0][..., :, None] + scores[1][..., None, :]).reshape(b, n, HEADS, PK_TOPK * PK_TOPK)
            final_scores, pk_idx = jax.lax.top_k(score, FINAL_TOPK)
            final_indices = jnp.take_along_axis(index, pk_idx, axis=-1)
            final_scores = jax.nn.softmax(final_scores, axis=-1)
            return (final_scores, final_indices)
        b, n, d = x.shape
        q = (x @ Wq).reshape(b, n, HEADS, DIM) * DIM ** (-0.5)
        kv_scores, indices = _pk(x, Wq_pk, pk_keys)
        offsets = jnp.arange(HEADS, dtype=indices.dtype) * NUM_KV
        ind = indices + offsets[None, None, :, None]
        k = jnp.einsum('bnhk,bnhkd->bnhd', kv_scores, keys_table[ind])
        v = jnp.einsum('bnhk,bnhkd->bnhd', kv_scores, values_table[ind])
        sim = jnp.einsum('bihd,bjhd->bhij', q, k)
        neg = -jnp.finfo(sim.dtype).max
        causal = jnp.tril(jnp.ones((n, n), dtype=bool))
        sim = jnp.where(causal, sim, neg)
        attn = jax.nn.softmax(sim, axis=-1)
        out = jnp.einsum('bhij,bjhd->bhid', attn, v)
        out = out.transpose(0, 2, 1, 3).reshape(b, n, HEADS * DIM)
        return out @ Wo
    h = _L0_tok_ref(x, L0_tok_W, L0_tok_b)
    h = jnp.concatenate([jnp.broadcast_to(cls_tok, (h.shape[0], 1, h.shape[2])), h], axis=1)
    h = h + _L0_attn_ref(_layernorm(h, axis=-1), L0_attn_Wq, L0_attn_Wk, L0_attn_Wv, L0_attn_w_mlp, L0_attn_b_mlp)
    h = h + _L0_ffn_ref(_layernorm(h, axis=-1), L0_ffn_ln1_w, L0_ffn_ln2_w, L0_ffn_wq, L0_ffn_wk, L0_ffn_wv, L0_ffn_wo, L0_ffn_router_w, L0_ffn_w1, L0_ffn_w2, L0_ffn_w3)
    h = h + _L1_attn_ref(_layernorm(h, axis=-1), L1_attn_key_matrices, L1_attn_query_matrices, L1_attn_value_in_matrices, L1_attn_value_out_matrices)
    h = h + _L1_ffn_ref(_layernorm(h, axis=-1), L1_ffn_Wq_pk, L1_ffn_pk_keys, L1_ffn_Wq, L1_ffn_keys_table, L1_ffn_values_table, L1_ffn_Wo)
    return h

_drawn_inputs = setup_inputs


def setup_inputs(seed=0):
    import zlib

    import numpy as np

    out = dict(_drawn_inputs(seed))
    spreads = {'L0_ffn_ln1_w': (1.0, 0.6), 'L0_ffn_ln2_w': (1.0, 0.6)}
    factors = {'L0_tok_b': 3.409,
     'L0_attn_Wq': 8.0,
     'L0_attn_Wk': 8.0,
     'L0_attn_w_mlp': 8.0,
     'L0_ffn_wq': 8.0,
     'L0_ffn_wk': 8.0,
     'L0_ffn_wv': 4.936,
     'L0_ffn_wo': 5.454,
     'L0_ffn_router_w': 8.0,
     'L0_ffn_w1': 8.0,
     'L0_ffn_w2': 8.0,
     'L0_ffn_w3': 8.0,
     'L1_ffn_Wq_pk': 51.299,
     'L1_ffn_pk_keys': 51.576,
     'L1_ffn_Wq': 64.0,
     'L1_ffn_keys_table': 64.0,
     'L1_ffn_values_table': 50.066,
     'L1_ffn_Wo': 49.988}
    for name, (base, spread) in spreads.items():
        noise = np.random.default_rng([zlib.crc32(name.encode()), seed]).standard_normal(out[name].shape)
        drawn = base * np.exp(spread * noise) if base else spread * noise
        out[name] = jnp.asarray(drawn.astype(out[name].dtype))
    for name, factor in factors.items():
        out[name] = (out[name] * factor).astype(out[name].dtype)
    return out
```

```python
from contextlib import ExitStack

import numpy as np

import concourse.bass as bass
from concourse import mybir

F32 = mybir.dt.float32
ALU = mybir.AluOpType
ACT = mybir.ActivationFunctionType
AX = mybir.AxisListType

C = 64
IMAGES, TOK = 64, 37
PER = 3
ROWS = PER * TOK
GROUPS = 22
COLS = ROWS * GROUPS
KCH = 6
BANK = 512
NEXP, HID = 8, 170
HH = HID // 2
HEADS = 8
KEYS = 64
TOPK = 16
ENT = KEYS * KEYS
CHUNKS = ENT // 128
TILES = -(-IMAGES * TOK // 128)
UNITS = HEADS * TILES
PADT = TILES * 128
KVT = 128 + HEADS * PADT + COLS
NEG = -3.0e38
LOAN = 1


class Scope:

    spent = []

    def __init__(self, nc, tag):
        self.nc, self.tag = nc, tag
        self.ctx, self.sem_ctx, self.sems, self.old = ExitStack(), ExitStack(), [], []

    def __enter__(self):
        return self

    def __exit__(self, *a):
        self.ctx.close()
        for ctx, _ in self.old:
            ctx.close()
        if self.sems:
            Scope.spent.append((self.sem_ctx, self.sems))

    def sb(self, name, shape, dt=F32):
        return self.ctx.enter_context(self.nc.sbuf_tensor(f"{self.tag}_{name}", shape, dt))

    def bank(self, name):
        return self.ctx.enter_context(self.nc.psum_tensor(f"{self.tag}_{name}", [128, BANK], F32))

    def sem(self, name):
        self.sems.append(self.sem_ctx.enter_context(self.nc.semaphore(f"{self.tag}_{name}")))
        return self.sems[-1]

    def block(self):
        block = self.ctx.enter_context(self.nc.Block())
        self.old, Scope.spent = Scope.spent, []

        @block.sync
        def _(sp):
            for _, sems in self.old:
                for sem in sems:
                    sp.sem_clear(sem)
        return block


class Chain:

    def __init__(self, eng, sem, base=0):
        self.eng, self.sem, self.base, self.n = eng, sem, base, 0

    def step(self, ins):
        ins.then_inc(self.sem, 1)
        self.n += 1

    def wait(self):
        self.eng.wait_ge(self.sem, self.base + self.n)


def spread(ap, axis, n):
    a = ap.unsqueeze(axis)
    shape = list(a.shape)
    shape[axis] = n
    return a.broadcast_to(shape)


def embed(nc, hid, x_img, w_tokT, cls_tok, b_tok):
    with Scope(nc, "tok") as s:
        patches = [s.sb(f"patches{i}", [128, KCH * ROWS]) for i in range(2)]
        w = s.sb("w", [128, KCH * C])
        add = s.sb("add", [ROWS, C])
        acc = [s.bank(f"acc{i}") for i in range(2)]
        w_in, bias_in, cls_in = s.sem("w_in"), s.sem("bias_in"), s.sem("cls_in")
        patches_in = [s.sem(f"patches_in{i}") for i in range(2)]
        product_done, row_done = s.sem("product_done"), s.sem("row_done")
        block = s.block()

        @block.sync
        def _(sp):
            sp.dma_start(w[:, :], w_tokT).then_inc(w_in, 16)
            with sp.Fori(0, GROUPS // 2) as i:
                for k in range(2):
                    sp.wait_ge(product_done, 2 * i + LOAN)
                    sp.dma_start(patches[k][:, :], x_img[bass.ds(2 * i + k, 1), :, :].rearrange("g p n -> (g p) n")).then_inc(patches_in[k], 16)

        @block.scalar
        def _(act):
            act.dma_start(add[:, :], b_tok.rearrange("(o c) -> o c", o=1).broadcast_to([ROWS, C])).then_inc(bias_in, 16)
            act.wait_ge(bias_in, 16)
            for m in range(PER):
                act.dma_start(add[m * TOK:m * TOK + 1, :], cls_tok).then_inc(cls_in, 16)

        @block.tensor
        def _(pe):
            pe.sem_inc(product_done, LOAN)
            pe.wait_ge(w_in, 16)
            with pe.Fori(0, GROUPS // 2) as i:
                for k in range(2):
                    pe.wait_ge(patches_in[k], 16 * i + 16)
                    pe.wait_ge(row_done, 2 * i + LOAN)
                    for c in range(KCH):
                        last = nc.tensor.matmul(acc[k][0:ROWS, 0:C], patches[k][:, c * ROWS:(c + 1) * ROWS],
                                                w[:, c * C:(c + 1) * C], start=c == 0, stop=c == KCH - 1)
                    last.then_inc(product_done, 1)

        @block.vector
        def _(dve):
            dve.sem_inc(row_done, LOAN)
            dve.wait_ge(bias_in, 16)
            dve.wait_ge(cls_in, 16 * PER)
            with dve.Fori(0, GROUPS // 2) as i:
                for k in range(2):
                    dve.wait_ge(product_done, 2 * i + (k + 1 + LOAN))
                    nc.vector.tensor_tensor(hid[:, bass.ds(2 * i + k, 1), :].rearrange("p g c -> p (g c)"),
                                            acc[k][0:ROWS, 0:C], add[:, :], ALU.add).then_inc(row_done, 1)


def normalize(nc, tag, src, dst, xT, ident, center, eps, weight=None):
    with Scope(nc, tag) as s:
        row = [ROWS, GROUPS]
        work = s.sb("work", [ROWS, GROUPS, C])
        mean, power, rstd = s.sb("mean", row), s.sb("power", row), s.sb("rstd", row)
        flip = [s.bank(f"flip{i}") for i in range(6)]
        centered_ok, square_ok, power_ok, rstd_ok = (s.sem(n) for n in ("centered", "square", "power", "rstd"))
        out_ok, flip_ok, dve_own = s.sem("out"), s.sem("flip"), s.sem("dve_own")
        w_in = s.sem("w_in")
        xc = dst if center else src
        if weight is not None:
            wrow = s.sb("wrow", [ROWS, C])
        block = s.block()
        quads = [(n, min(4, GROUPS - 4 * n)) for n in range(6)]

        @block.sync
        def _(sp):
            if weight is not None:
                sp.dma_start(wrow[:, :], weight.rearrange("(o c) -> o c", o=1).broadcast_to([ROWS, C])).then_inc(w_in, 16)

        @block.vector
        def _(dve):
            own = Chain(dve, dve_own)
            if center:
                own.step(nc.vector.tensor_reduce(mean[:, :], src[:, :, :], AX.X, ALU.add))
                own.wait()
                own.step(nc.vector.tensor_scalar(mean[:, :], mean[:, :], 1.0 / C, None, ALU.mult))
                own.wait()
                nc.vector.tensor_tensor(dst[:, :, :], src[:, :, :], spread(mean[:, :], 2, C),
                                        ALU.subtract).then_inc(centered_ok, 1)
            dve.wait_ge(square_ok, 1)
            own.step(nc.vector.tensor_reduce(power[:, :], work[:, :, :], AX.X, ALU.add))
            own.wait()
            nc.vector.tensor_scalar(power[:, :], power[:, :], eps, None, ALU.add).then_inc(power_ok, 1)
            dve.wait_ge(rstd_ok, 1)
            own.step(nc.vector.reciprocal(rstd[:, :], rstd[:, :]))
            own.wait()
            if center:
                dve.wait_ge(centered_ok, 1)
            last = nc.vector.tensor_tensor(dst[:, :, :], xc[:, :, :], spread(rstd[:, :], 2, C), ALU.mult)
            if weight is not None:
                own.step(last)
                own.wait()
                dve.wait_ge(w_in, 16)
                last = nc.vector.tensor_tensor(dst[:, :, :], dst[:, :, :], spread(wrow[:, :], 1, GROUPS), ALU.mult)
            last.then_inc(out_ok, 1)
            for n, m in quads[1::2]:
                dve.wait_ge(flip_ok, n + 1)
                nc.vector.tensor_copy(xT[:, 4 * n * ROWS:(4 * n + m) * ROWS], flip[n][0:C, 0:m * ROWS])

        @block.scalar
        def _(act):
            if center:
                act.wait_ge(centered_ok, 1)
            nc.scalar.activation(work[:, :, :], xc[:, :, :], ACT.Square, scale=C ** -0.5).then_inc(square_ok, 1)
            act.wait_ge(power_ok, 1)
            nc.scalar.activation(rstd[:, :], power[:, :], ACT.Sqrt).then_inc(rstd_ok, 1)
            for n, m in quads[0::2]:
                act.wait_ge(flip_ok, n + 1)
                nc.scalar.copy(xT[:, 4 * n * ROWS:(4 * n + m) * ROWS], flip[n][0:C, 0:m * ROWS])

        @block.tensor
        def _(pe):
            pe.wait_ge(out_ok, 1)
            for n, m in quads:
                for j in range(m):
                    last = nc.tensor.transpose(flip[n][0:C, j * ROWS:(j + 1) * ROWS], dst[:, 4 * n + j, :],
                                               ident[0:ROWS, 0:ROWS])
                last.then_inc(flip_ok, 1)


def relu_attention(nc, hid, xT, ident, wqT, wkT, wvT, w_mlp, b_mlp, unmix):
    HALF = IMAGES // 2
    D = 32
    with Scope(nc, "rat") as s:
        q, k = s.sb("q", [128, HALF, TOK]), s.sb("k", [128, HALF, TOK])
        w3 = s.sb("w3", [C, 3 * C])
        window = s.sb("window", [128, 252])
        b_sb = s.sb("b_sb", [1, 1])
        zrow = s.sb("zrow", [1, BANK])
        ones = s.sb("ones", [1, 128])
        brow = s.sb("brow", [1, BANK])
        wst = [s.sb(f"wst{i}", [128, 128]) for i in range(2)]
        diff = [s.sb(f"diff{i}", [128, TOK, TOK]) for i in range(2)]
        logit = s.sb("logit", [128, TOK, TOK])
        top, tot = s.sb("top", [128, TOK]), s.sb("tot", [128, TOK])
        prob_t = s.sb("prob_t", [TOK, TOK, 128])
        x8 = s.sb("x8", [C, 7 * TOK + 128])
        v8 = s.sb("v8", [TOK, 9 * C])
        out_t = s.sb("out_t", [C, COLS])
        unmix_sb = s.sb("unmix", [C, C])
        bank = [s.bank(f"b{i}") for i in range(8)]
        w_in, win_in, zero_ok, ones_ok, b_ok = (s.sem(n) for n in ("w_in", "win_in", "zero", "ones", "b"))
        qk_done, q_out, k_out = s.sem("qk_done"), s.sem("q_out"), s.sem("k_out")
        win_ok, diff_ok, relu_ok, pair_done = (s.sem(n) for n in ("win", "diff", "relu", "pair_done"))
        logits_done, logit_ok, own, exp_ok, prob_ok = (s.sem(n) for n in ("logits_done", "logit", "dve_own", "exp", "prob"))
        flip_ok, flip_a, flip_d = s.sem("flip"), s.sem("flip_a"), s.sem("flip_d")
        x8_ok, v_done, v8_ok, mix_done, mix_out = (s.sem(n) for n in ("x8", "v_done", "v8", "mix_done", "mix_out"))
        back_ok, centered = s.sem("back"), s.sem("sub")
        block = s.block()
        PARTS = ((0, 13), (13, 12), (25, 12))
        FLIPS = -(-TOK // 4)

        @block.sync
        def _(sp):
            sp.dma_start(w3[:, 0:C], wqT).then_inc(w_in, 16)
            sp.dma_start(w3[:, C:2 * C], wkT).then_inc(w_in, 16)
            sp.dma_start(w3[:, 2 * C:3 * C], wvT).then_inc(w_in, 16)
            sp.dma_start(unmix_sb[:, :], unmix).then_inc(w_in, 16)
            sp.dma_start(b_sb[:, :], b_mlp.rearrange("(o c) -> o c", o=1)).then_inc(w_in, 16)
            sp.wait_ge(zero_ok, 1)
            for m in range(4):
                sp.dma_start(window[m * D:(m + 1) * D, 124 + m:125 + m],
                             w_mlp.rearrange("(d o) -> d o", o=1)).then_inc(win_in, 16)

        @block.gpsimd
        def _(pool):
            nc.gpsimd.memset(window[:, :], 0.0).then_inc(zero_ok, 1)
            nc.gpsimd.memset(out_t[:, :], 0.0).then_inc(zero_ok, 1)
            nc.gpsimd.memset(zrow[:, :], 0.0).then_inc(ones_ok, 1)
            nc.gpsimd.memset(ones[:, :], 1.0).then_inc(ones_ok, 1)
            nc.gpsimd.memset(v8[:, :], 0.0).then_inc(ones_ok, 1)
            nc.gpsimd.memset(x8[:, :], 0.0).then_inc(ones_ok, 1)
            pool.wait_ge(w_in, 80)
            pool.wait_ge(ones_ok, 1)
            nc.gpsimd.tensor_scalar(brow[:, :], zrow[:, :], b_sb[0:1, 0:1], None, ALU.add).then_inc(b_ok, 1)
            pool.wait_ge(win_in, 64)
            with pool.Fori(0, HALF // 2) as i:
                for m in range(2):
                    at = pool.snap(i * -8 + (124 - 4 * m))
                    pool.wait_ge(pair_done, 2 * i + LOAN)
                    nc.gpsimd.tensor_copy(wst[m][:, :], window[:, bass.ds(at, 128)]).then_inc(win_ok, 1)
            for hf in range(2):
                with pool.Fori(0, 4) as c:
                    pool.wait_ge(v_done, c + (4 * hf + LOAN))
                    nc.gpsimd.tensor_copy(x8[:, 0:8 * TOK], xT[:, bass.ds((4 * hf * 8 * TOK) + c * (8 * TOK), 8 * TOK)]).then_inc(x8_ok, 1)

        @block.tensor
        def _(pe):
            pe.sem_inc(pair_done, LOAN)
            pe.sem_inc(v_done, LOAN)
            pe.wait_ge(w_in, 80)
            for n in range(4):
                for j in range(2):
                    for hf in range(2):
                        at = (hf * 4 + n) * 8 * TOK
                        last = nc.tensor.matmul(bank[2 * n + j][C * hf:C * hf + C, 0:8 * TOK], w3[:, j * C:(j + 1) * C],
                                                xT[:, at:at + 8 * TOK], start=True, stop=True)
                last.then_inc(qk_done, 1)
            pe.wait_ge(ones_ok, 4)
            pe.wait_ge(q_out, 2)
            pe.wait_ge(k_out, 2)
            for b, (r, n) in enumerate(PARTS):
                nc.tensor.matmul(bank[b][:, 0:n * TOK], ones[:, :], zrow[:, 0:n * TOK], start=True, stop=False)
            with pe.Fori(0, HALF // 2) as i:
                for m in range(2):
                    pe.wait_ge(win_ok, 2 * i + m + 1)
                    pe.wait_ge(relu_ok, 2 * i + m + 1)
                    for b, (r, n) in enumerate(PARTS):
                        last = nc.tensor.matmul(bank[b][:, 0:n * TOK], wst[m][:, :], diff[m][:, r:r + n, :],
                                                start=False, stop=False)
                    last.then_inc(pair_done, 1)
            pe.wait_ge(b_ok, 1)
            for b, (r, n) in enumerate(PARTS):
                nc.tensor.matmul(bank[b][:, 0:n * TOK], ones[:, :], brow[:, 0:n * TOK],
                                 start=False, stop=True).then_inc(logits_done, 1)
            pe.wait_ge(prob_ok, 1)
            for n in range(FLIPS):
                if n >= 4:
                    pe.wait_ge((flip_a, flip_d)[n % 2], (n - 4) // 2 + 1)
                for r in range(4 * n, min(4 * n + 4, TOK)):
                    last = nc.tensor.transpose(bank[3 + n % 4][0:TOK, (r % 4) * 128:(r % 4 + 1) * 128], logit[:, r, :],
                                               ident[:, :])
                last.then_inc(flip_ok, 1)
            pe.wait_ge(flip_a, FLIPS // 2)
            pe.wait_ge(flip_d, FLIPS // 2)
            for hf in range(2):
                with pe.Fori(0, 4) as c:
                    pe.wait_ge(x8_ok, c + 4 * hf + 1)
                    for j in range(8):
                        last = nc.tensor.matmul(bank[7][:, j * C:(j + 1) * C], x8[:, j * TOK:j * TOK + 128],
                                                w3[:, 2 * C:3 * C], start=True, stop=True)
                    last.then_inc(v_done, 1)
                    pe.wait_ge(v8_ok, c + 4 * hf + 1)
                    pe.wait_ge(mix_out, 4 * c + (16 * hf + LOAN))
                    for j in range(8):
                        last = nc.tensor.matmul(bank[j // 4][:, (j % 4) * 2 * TOK:(j % 4 + 1) * 2 * TOK],
                                                v8[:, j * C:j * C + 128],
                                                prob_t[:, :, bass.ds(4 * j + 2 * hf + c * 32, 2)], start=True, stop=True)
                    last.then_inc(mix_done, 1)
            pe.wait_ge(mix_out, 32 + LOAN)
            for g in range(GROUPS):
                last = nc.tensor.matmul(bank[3 + g // 8][0:ROWS, (g % 8) * C:(g % 8 + 1) * C],
                                        out_t[:, g * ROWS:(g + 1) * ROWS], unmix_sb[:, :], start=True, stop=True)
                if g % 8 == 7 or g == GROUPS - 1:
                    last.then_inc(back_ok, 1)

        @block.scalar
        def _(act):
            for n in range(4):
                act.wait_ge(qk_done, n + 1)
                nc.scalar.copy(q[:, n * 8:(n + 1) * 8, :].rearrange("p i t -> p (i t)"), bank[2 * n][:, 0:8 * TOK]).then_inc(q_out, 1)
            with act.Fori(0, HALF // 2) as i:
                for m in range(2):
                    act.wait_ge(diff_ok, 2 * i + m + 1)
                    nc.scalar.activation(diff[m][:, :, :], diff[m][:, :, :], ACT.Relu).then_inc(relu_ok, 1)
            for b, (r, n) in enumerate(PARTS):
                act.wait_ge(logits_done, 3)
                nc.scalar.activation(logit[:, r:r + n, :].rearrange("p a b -> p (a b)"), bank[b][:, 0:n * TOK], ACT.Relu).then_inc(logit_ok, 1)
            act.wait_ge(centered, 1)
            nc.scalar.activation(logit[:, :, :], logit[:, :, :], ACT.Exp).then_inc(exp_ok, 1)
            for n in range(0, FLIPS, 2):
                act.wait_ge(flip_ok, n + 1)
                m = min(4, TOK - 4 * n)
                nc.scalar.copy(prob_t[:, 4 * n:4 * n + m, :].rearrange("p a b -> p (a b)"),
                               bank[3 + n % 4][0:TOK, 0:128 * m]).then_inc(flip_a, 1)
            for hf in range(2):
                with act.Fori(0, 4) as c:
                    act.wait_ge(v_done, c + (4 * hf + 1 + LOAN))
                    nc.scalar.copy(v8[:, 0:8 * C], bank[7][0:TOK, :]).then_inc(v8_ok, 1)

        @block.vector
        def _(dve):
            dve.sem_inc(mix_out, LOAN)
            for n in range(4):
                dve.wait_ge(qk_done, n + 1)
                nc.vector.tensor_copy(k[:, n * 8:(n + 1) * 8, :].rearrange("p i t -> p (i t)"), bank[2 * n + 1][:, 0:8 * TOK]).then_inc(k_out, 1)
            dve.wait_ge(q_out, 4)
            dve.wait_ge(k_out, 4)
            with dve.Fori(0, HALF // 2) as i:
                for m in range(2):
                    dve.wait_ge(pair_done, 2 * i + LOAN)
                    one = bass.ds(2 * i + m, 1)
                    nc.vector.tensor_tensor(diff[m][:, :, :], q[:, one, :].rearrange("p o t -> p t o").broadcast_to([128, TOK, TOK]),
                                            k[:, one, :].broadcast_to([128, TOK, TOK]), ALU.subtract).then_inc(diff_ok, 1)
            dve.wait_ge(logit_ok, 3)
            chain = Chain(dve, own)
            chain.step(nc.vector.tensor_reduce(top[:, :], logit[:, :, :], AX.X, ALU.max))
            chain.wait()
            nc.vector.tensor_tensor(logit[:, :, :], logit[:, :, :], spread(top[:, :], 2, TOK), ALU.subtract).then_inc(centered, 1)
            dve.wait_ge(exp_ok, 1)
            chain.step(nc.vector.tensor_reduce(tot[:, :], logit[:, :, :], AX.X, ALU.add))
            chain.wait()
            chain.step(nc.vector.reciprocal(tot[:, :], tot[:, :]))
            chain.wait()
            nc.vector.tensor_tensor(logit[:, :, :], logit[:, :, :], spread(tot[:, :], 2, TOK), ALU.mult).then_inc(prob_ok, 1)
            for n in range(1, FLIPS, 2):
                dve.wait_ge(flip_ok, n + 1)
                m = min(4, TOK - 4 * n)
                nc.vector.tensor_copy(prob_t[:, 4 * n:4 * n + m, :].rearrange("p a b -> p (a b)"),
                                      bank[3 + n % 4][0:TOK, 0:128 * m]).then_inc(flip_d, 1)
            dve.wait_ge(zero_ok, 2)
            for hf in range(2):
                with dve.Fori(0, 4) as c:
                    dve.wait_ge(mix_done, c + 4 * hf + 1)
                    for h4 in range(2):
                        for g in range(2):
                            src = bank[h4][g * D:(g + 1) * D, 0:8 * TOK].rearrange("p (j t g) -> p j t g", j=4, g=2)
                            at = bass.ds((4 * hf * 8 + 4 * h4) * TOK + c * (8 * TOK), 4 * TOK)
                            nc.vector.tensor_copy(out_t[g * D:(g + 1) * D, at].rearrange("p (j t) -> p j t", j=4),
                                                  src[:, :, :, g]).then_inc(mix_out, 1)
            for n in range(3):
                m = min(8, GROUPS - 8 * n)
                dve.wait_ge(back_ok, n + 1)
                nc.vector.tensor_tensor(hid[:, 8 * n:8 * n + m, :].rearrange("p g c -> p (g c)"),
                                        hid[:, 8 * n:8 * n + m, :].rearrange("p g c -> p (g c)"),
                                        bank[3 + n][0:ROWS, 0:m * C], ALU.add)


def merge(nc, tag, pairs, spots):
    with Scope(nc, tag) as s:
        banks = [s.bank(f"m{i}") for i in range(-(-len(pairs) // 8))]
        bank_ok = s.sem("bank")
        block = s.block()

        @block.tensor
        def _(pe):
            for n, (left, right) in enumerate(pairs):
                last = nc.tensor.matmul(banks[n // 8][0:C, (n % 8) * C:(n % 8 + 1) * C], left, right, start=True, stop=True)
                if n % 8 == 7:
                    last.then_inc(bank_ok, 1)

        @block.vector
        def _(dve):
            for n, spot in enumerate(spots):
                dve.wait_ge(bank_ok, n + 1)
                nc.vector.tensor_copy(spot, banks[n][0:C, :])


def load(nc, tag, pairs):
    with Scope(nc, tag) as s:
        arrived = s.sem("arrived")
        block = s.block()

        @block.sync
        def _(sp):
            for dst, src in pairs:
                sp.dma_start(dst, src).then_inc(arrived, 16)
            sp.wait_ge(arrived, 16 * len(pairs))


def head_attention(nc, tag, hid, xT, ident, mask, wq, wv, scale, kv=None):
    HALF = 4 * ROWS
    NH = HEADS
    with Scope(nc, tag) as s:
        def two(name, shape):
            return [s.sb(f"{name}{i}", shape) for i in range(2)]
        x_g = two("x_g", [C, ROWS])
        q_t = two("q_t", [C, NH * ROWS])
        v_g = two("v_g", [ROWS, NH * C])
        score = two("score", [ROWS, NH, ROWS])
        prob_t = two("prob_t", [ROWS, NH * ROWS])
        top, tot = two("top", [ROWS, NH]), two("tot", [ROWS, NH])
        if kv is not None:
            kv_g = two("kv_g", [128, NH, ROWS])
        bank = [[s.bank(f"b{k}{n}") for n in range(3)] for k in range(2)]
        x_ok, q_done, v_done, q_a, q_d, v_ok = (s.sem(n) for n in ("x", "q_done", "v_done", "q_a", "q_d", "v"))
        score_done, masked, top_ok, centered, exp_ok, prob_ok = (s.sem(n) for n in ("score_done", "masked", "top", "sub", "exp", "prob"))
        sum_ok, recip_ok = s.sem("sum"), s.sem("recip")
        flip_done, flip_a, flip_d, mix_done, hid_ok = (s.sem(n) for n in ("flip_done", "flip_a", "flip_d", "mix_done", "hid"))
        block = s.block()

        @block.gpsimd
        def _(pool):
            with pool.Fori(0, GROUPS // 2) as i:
                for k in range(2):
                    pool.wait_ge(mix_done, 2 * i + LOAN)
                    at = bass.ds((2 * i + k) * ROWS, ROWS)
                    last = nc.gpsimd.tensor_copy(x_g[k][:, :], xT[:, at])
                    if kv is not None:
                        last.then_inc(x_ok, 1)
                        last = nc.gpsimd.tensor_copy(
                            kv_g[k][:, :, :],
                            kv[:, bass.ds((2 * i + k) * ROWS + 128, NH * PADT)].rearrange("p (h t) -> p h t", h=NH)[:, :, 0:ROWS])
                    last.then_inc(x_ok, 1)

        staged = 1 if kv is None else 2

        @block.tensor
        def _(pe):
            pe.sem_inc(mix_done, LOAN)
            with pe.Fori(0, GROUPS // 2) as i:
                for k in range(2):
                    b = bank[k]
                    pe.wait_ge(x_ok, staged * (2 * i + k + 1))
                    pe.wait_ge(flip_a, 2 * i + LOAN)
                    pe.wait_ge(flip_d, 2 * i + LOAN)
                    pe.wait_ge(hid_ok, 2 * i + LOAN)
                    for h in range(NH):
                        m = 2 if h == 0 else 1
                        last = nc.tensor.matmul(b[h // 4][0:m * C, (h % 4) * ROWS:(h % 4 + 1) * ROWS],
                                                wq[:, h:h + m, :].rearrange("p h c -> p (h c)"), x_g[k][:, :],
                                                start=True, stop=True)
                        if h % 4 == 3:
                            last.then_inc(q_done, 1)
                    if kv is None:
                        nc.tensor.matmul(b[2][0:ROWS, :], x_g[k][:, :], wv[:, :, :].rearrange("p h c -> p (h c)"),
                                         start=True, stop=True).then_inc(v_done, 1)
                    else:
                        for h in range(NH):
                            last = nc.tensor.matmul(b[2][0:ROWS, h * C:(h + 1) * C], kv_g[k][:, h, :], wv[:, h, :],
                                                    start=True, stop=True)
                        last.then_inc(v_done, 1)
                for k in range(2):
                    b = bank[k]
                    for h in range(NH):
                        if h == 0:
                            pe.wait_ge(q_a, 2 * i + k + 1)
                        if h == 4:
                            pe.wait_ge(q_d, 2 * i + k + 1)
                        keys = x_g[k][:, :] if kv is None else kv_g[k][0:C, h, :]
                        last = nc.tensor.matmul(b[h // 4][0:ROWS, (h % 4) * ROWS:(h % 4 + 1) * ROWS],
                                                q_t[k][:, h * ROWS:(h + 1) * ROWS], keys, start=True, stop=True)
                        if h % 4 == 3:
                            last.then_inc(score_done, 1)
                for k in range(2):
                    b = bank[k]
                    pe.wait_ge(prob_ok, 2 * i + k + 1)
                    for h in range(NH):
                        last = nc.tensor.transpose(b[h // 4][0:ROWS, (h % 4) * ROWS:(h % 4 + 1) * ROWS],
                                                   score[k][:, h, :], ident[0:ROWS, 0:ROWS])
                        if h % 4 == 3:
                            last.then_inc(flip_done, 1)
                for k in range(2):
                    b = bank[k]
                    pe.wait_ge(v_ok, 2 * i + k + 1)
                    pe.wait_ge(flip_a, 2 * i + (k + 1 + LOAN))
                    pe.wait_ge(flip_d, 2 * i + (k + 1 + LOAN))
                    for h in range(NH):
                        last = nc.tensor.matmul(b[2][0:ROWS, 0:C], prob_t[k][:, h * ROWS:(h + 1) * ROWS],
                                                v_g[k][:, h * C:(h + 1) * C], start=h == 0, stop=h == NH - 1)
                    last.then_inc(mix_done, 1)

        @block.scalar
        def _(act):
            act.sem_inc(flip_a, LOAN)
            with act.Fori(0, GROUPS // 2) as i:
                for k in range(2):
                    act.wait_ge(q_done, 4 * i + 2 * k + 1)
                    nc.scalar.copy(q_t[k][:, 0:HALF], bank[k][0][0:C, 0:HALF]).then_inc(q_a, 1)
                    act.wait_ge(v_done, 2 * i + k + 1)
                    nc.scalar.copy(v_g[k][:, :], bank[k][2][0:ROWS, :]).then_inc(v_ok, 1)
                for k in range(2):
                    act.wait_ge(centered, 2 * i + k + 1)
                    nc.scalar.activation(score[k][:, :, :], score[k][:, :, :], ACT.Exp, scale=scale).then_inc(exp_ok, 1)
                for k in range(2):
                    act.wait_ge(flip_done, 4 * i + 2 * k + 1)
                    nc.scalar.copy(prob_t[k][:, 0:HALF], bank[k][0][0:ROWS, 0:HALF]).then_inc(flip_a, 1)

        @block.vector
        def _(dve):
            dve.sem_inc(flip_d, LOAN)
            dve.sem_inc(hid_ok, LOAN)
            with dve.Fori(0, GROUPS // 2) as i:
                for k in range(2):
                    dve.wait_ge(q_done, 4 * i + 2 * k + 2)
                    nc.vector.tensor_copy(q_t[k][:, HALF:2 * HALF], bank[k][1][0:C, 0:HALF]).then_inc(q_d, 1)
                for k in range(2):
                    for j in range(2):
                        dve.wait_ge(score_done, 4 * i + 2 * k + j + 1)
                        nc.vector.tensor_tensor(score[k][:, 4 * j:4 * j + 4, :],
                                                bank[k][j][0:ROWS, 0:HALF].rearrange("p (h t) -> p h t", h=4),
                                                spread(mask[:, :], 1, 4), ALU.add).then_inc(masked, 1)
                for k in range(2):
                    dve.wait_ge(masked, 4 * i + 2 * k + 2)
                    nc.vector.tensor_reduce(top[k][:, :], score[k][:, :, :], AX.X, ALU.max).then_inc(top_ok, 1)
                for k in range(2):
                    dve.wait_ge(top_ok, 2 * i + k + 1)
                    nc.vector.tensor_tensor(score[k][:, :, :], score[k][:, :, :], spread(top[k][:, :], 2, ROWS),
                                            ALU.subtract).then_inc(centered, 1)
                for k in range(2):
                    dve.wait_ge(exp_ok, 2 * i + k + 1)
                    nc.vector.tensor_reduce(tot[k][:, :], score[k][:, :, :], AX.X, ALU.add).then_inc(sum_ok, 1)
                    dve.wait_ge(sum_ok, 2 * i + k + 1)
                    nc.vector.reciprocal(tot[k][:, :], tot[k][:, :]).then_inc(recip_ok, 1)
                    dve.wait_ge(recip_ok, 2 * i + k + 1)
                    nc.vector.tensor_tensor(score[k][:, :, :], score[k][:, :, :], spread(tot[k][:, :], 2, ROWS),
                                            ALU.mult).then_inc(prob_ok, 1)
                for k in range(2):
                    dve.wait_ge(flip_done, 4 * i + 2 * k + 2)
                    nc.vector.tensor_copy(prob_t[k][:, HALF:2 * HALF], bank[k][1][0:ROWS, 0:HALF]).then_inc(flip_d, 1)
                for k in range(2):
                    dve.wait_ge(mix_done, 2 * i + (k + 1 + LOAN))
                    row = hid[:, bass.ds(2 * i + k, 1), :].rearrange("p g c -> p (g c)")
                    nc.vector.tensor_tensor(row, row, bank[k][2][0:ROWS, 0:C], ALU.add).then_inc(hid_ok, 1)


def product_keys(nc, xT, ident, side_w, table, kv_t):
    Q = 4
    QN = ENT // Q
    SIDE = KEYS // Q
    TURNS = ENT // BANK
    PARTS = ((0, 16, 0, 2), (0, 2, 2, 16), (2, 5, 2, 5))
    CAND = sum((a1 - a0) * (b1 - b0) for a0, a1, b0, b1 in PARTS)
    PICKS = 13
    with Scope(nc, "pk") as s:
        x_st, w_st = s.sb("x_st", [C, 128]), s.sb("w_st", [C, 128])
        sim_sel, sim_sum = s.sb("sim_sel", [128, 128]), s.sb("sim_sum", [128, 128])
        total = [s.sb(f"total{q}", [128, SIDE, KEYS]) for q in range(Q)]
        weight = [s.sb(f"weight{q}", [128, QN]) for q in range(Q)]
        turned = [s.sb(f"turned{i}", [128, BANK]) for i in range(4)]
        tab = s.sb("tab", [128, CHUNKS, 128])
        best = [s.sb(f"best{p}", [128, TOPK]) for p in range(2)]
        rest = [s.sb(f"rest{p}", [128, KEYS]) for p in range(2)]
        cand, cand2, chosen = s.sb("cand", [128, CAND]), s.sb("cand2", [128, CAND]), s.sb("chosen", [128, TOPK])
        cut = s.sb("cut", [128, 2])
        zpart, zinv = s.sb("zpart", [128, Q]), s.sb("zinv", [128, 1])
        kv_sb = s.sb("kv_sb", [128, 128])
        expo = [s.ctx.enter_context(nc.psum_tensor(f"pk_expo{i}", [128, QN], F32)) for i in range(2)]
        turn = [s.bank(f"turn{i}") for i in range(2)]
        out, misc = s.bank("out"), s.bank("misc")
        zero_ok, staged, sims_done, sel_ok, sum_in = (s.sem(n) for n in ("zero", "staged", "sims_done", "sel", "sum_in"))
        pool_sum, dve_sum, exp_ok, masked, cut_ok = (s.sem(n) for n in ("pool_sum", "dve_sum", "exp", "masked", "cut"))
        turn_done, turned_ok, mul_done = s.sem("turn_done"), s.sem("turned"), s.sem("mul_done")
        pick, z_ok, zinv_ok, kv_ok, flip_done, flip_out = (s.sem(n) for n in ("pick", "z", "zinv", "kv", "flip_done", "flip_out"))
        tab_in = [s.sem(f"tab_in{q}") for q in range(Q)]
        ready = s.sem("ready")
        block = s.block()
        TURNED0, MUL0, MASKED0, TURN0 = 1 + LOAN, 3 + LOAN, 3 + LOAN, 6 + LOAN

        def sum_quarter(eng, q):
            return eng.tensor_tensor(total[q][:, :, :], spread(sim_sum[:, 0:KEYS], 1, SIDE),
                                     spread(sim_sum[:, KEYS + q * SIDE:KEYS + (q + 1) * SIDE], 2, KEYS), ALU.add)

        @block.sync
        def _(sp):
            per = CHUNKS // Q
            for q in range(Q):
                sp.dma_start(tab[:, q * per:(q + 1) * per, :], table[0, :, q * per:(q + 1) * per, :]).then_inc(tab_in[q], 16)
            with sp.Fori(1, HEADS) as h:
                for q in range(Q):
                    sp.wait_ge(mul_done, h * (TURNS * TILES) + (MUL0 - TURNS + 2 * q + 2))
                    sp.dma_start(tab[:, q * per:(q + 1) * per, :],
                                 table[bass.ds(h, 1), :, q * per:(q + 1) * per, :].rearrange("h p c n -> (h p) c n")).then_inc(tab_in[q], 16)

        @block.gpsimd
        def _(pool):
            nc.gpsimd.memset(kv_sb[:, :], 0.0).then_inc(zero_ok, 1)
            nc.gpsimd.tensor_copy(w_st[:, :], side_w[:, 0, :]).then_inc(ready, 1)
            nc.gpsimd.tensor_copy(x_st[:, :], xT[:, 0:128]).then_inc(staged, 1)

            def unit(u, at, head):
                pool.wait_ge(sims_done, u + 1)
                if head is not None:
                    nc.gpsimd.tensor_copy(w_st[:, :], side_w[:, bass.ds(head, 1), :].rearrange("p h n -> p (h n)")).then_inc(ready, 1)
                nc.gpsimd.tensor_copy(x_st[:, :], xT[:, at]).then_inc(staged, 1)
                pool.wait_ge(sum_in, u + 1)
                for q in range(Q - 1):
                    pool.wait_ge(masked, u * Q + q + MASKED0 - 3)
                    sum_quarter(nc.gpsimd, q).then_inc(pool_sum, 1)

            with pool.Fori(0, HEADS) as h:
                with pool.Fori(0, TILES - 1) as t:
                    unit(h * TILES + t, bass.ds(t * 128 + 128, 128), None)
                unit(h * TILES + (TILES - 1), slice(0, 128), h + 1)

        @block.tensor
        def _(pe):
            pe.wait_ge(zero_ok, 1)
            pe.sem_inc(mul_done, MUL0)
            pe.sem_inc(turn_done, TURN0)
            pe.wait_ge(ready, 1)
            pe.wait_ge(staged, 1)
            nc.tensor.matmul(misc[:, 0:128], x_st[:, :], w_st[:, :], start=True, stop=True).then_inc(sims_done, 1)

            def turn_bank(u, k):
                if k % 2 == 0:
                    pe.wait_ge(masked, u * Q + (k // 2 + 1 + MASKED0))
                pe.wait_ge(turned_ok, u * TURNS + (k - 1 + TURNED0))
                for j in range(4):
                    at = ((4 * k + j) % (QN // 128)) * 128
                    last = nc.tensor.transpose(turn[k % 2][:, j * 128:(j + 1) * 128],
                                               weight[k // 2][:, at:at + 128], ident[:, :])
                last.then_inc(turn_done, 1)

            def multiply(u, h, k):
                if k == 0:
                    pe.wait_ge(kv_ok, u + LOAN)
                if k % 2 == 0:
                    pe.wait_ge(tab_in[k // 2], h * 16 + 16)
                pe.wait_ge(turned_ok, u * TURNS + (k + 1 + TURNED0))
                for j in range(4):
                    last = nc.tensor.matmul(out[:, 0:128], turned[k % 4][:, j * 128:(j + 1) * 128], tab[:, 4 * k + j, :],
                                            start=k == 0 and j == 0, stop=k == TURNS - 1 and j == 3)
                last.then_inc(mul_done, 1)

            def flip(u):
                pe.wait_ge(kv_ok, u + LOAN)
                pe.wait_ge(flip_out, u + LOAN)
                pe.wait_ge(sum_in, u + 1)
                nc.tensor.transpose(misc[:, 128:256], kv_sb[:, :], ident[:, :]).then_inc(flip_done, 1)

            with pe.Fori(0, HEADS) as h:
                with pe.Fori(0, TILES) as t:
                    u = h * TILES + t
                    turn_bank(u, 0)
                    for k in range(TURNS):
                        if k + 1 < TURNS:
                            turn_bank(u, k + 1)
                        multiply(u, h, k)
                        if k == 0:
                            flip(u)
                        if k == 1:
                            pe.wait_ge(flip_out, u + (1 + LOAN))
                            pe.wait_ge(staged, u + 2)
                            pe.wait_ge(ready, h + 1)
                            pe.wait_ge(sum_in, u + 1)
                            nc.tensor.matmul(misc[:, 0:128], x_st[:, :], w_st[:, :], start=True, stop=True).then_inc(sims_done, 1)
            flip(UNITS)

        @block.scalar
        def _(act):
            act.sem_inc(kv_ok, LOAN)
            act.sem_inc(flip_out, LOAN)
            act.sem_inc(turned_ok, TURNED0)

            def exp(u, q):
                if q < Q - 1:
                    act.wait_ge(pool_sum, u * (Q - 1) + (q + 1))
                else:
                    act.wait_ge(dve_sum, u + 1)
                act.wait_ge(cut_ok, u + 1)
                act.wait_ge(masked, u * Q + (q - 1 + MASKED0))
                nc.scalar.activation(expo[q % 2][:, :], total[q][:, :, :].rearrange("p j i -> p (j i)"), ACT.Exp,
                                     bias=cut[:, 1:2]).then_inc(exp_ok, 1)

            def copy_turned(u, k):
                act.wait_ge(turn_done, u * TURNS + (k + 1 + TURN0))
                act.wait_ge(mul_done, u * TURNS + (k - 3 + MUL0))
                nc.scalar.copy(turned[k % 4][:, :], turn[k % 2][:, :]).then_inc(turned_ok, 1)

            def scores_for_sums(u, first=False):
                if not first:
                    act.wait_ge(pool_sum, u * (Q - 1))
                    act.wait_ge(dve_sum, u)
                act.wait_ge(sel_ok, u + 1)
                nc.scalar.copy(sim_sum[:, :], misc[:, 0:128]).then_inc(sum_in, 1)

            def flipped(u):
                act.wait_ge(flip_done, u + 1)
                nc.scalar.copy(kv_t[:, bass.ds(u * 128, 128)], misc[:, 128:256]).then_inc(flip_out, 1)

            def unit(u, last):
                exp(u, 1)
                copy_turned(u, 0)
                copy_turned(u, 1)
                flipped(u)
                exp(u, 2)
                copy_turned(u, 2)
                copy_turned(u, 3)
                exp(u, 3)
                copy_turned(u, 4)
                copy_turned(u, 5)
                scores_for_sums(u + 1)
                copy_turned(u, 6)
                if not last:
                    exp(u + 1, 0)
                copy_turned(u, 7)
                act.wait_ge(mul_done, u * TURNS + (TURNS + MUL0))
                act.wait_ge(zinv_ok, u + 1)
                act.wait_ge(flip_done, u + 1)
                nc.scalar.activation(kv_sb[:, :], out[:, 0:128], ACT.Copy, scale=zinv[:, 0:1]).then_inc(kv_ok, 1)

            scores_for_sums(0, first=True)
            exp(0, 0)
            with act.Fori(0, UNITS - 1) as u:
                unit(u, False)
            unit(UNITS - 1, True)
            flipped(UNITS)

        @block.vector
        def _(dve):
            dve.sem_inc(masked, MASKED0)

            def select(v):
                own = Chain(dve, pick)
                side = [sim_sel[:, p * KEYS:(p + 1) * KEYS] for p in range(2)]
                dve.sem_clear(pick)
                dve.wait_ge(sims_done, v + 1)
                own.step(nc.vector.tensor_copy(sim_sel[:, :], misc[:, 0:128]))
                own.wait()
                dve.sem_inc(sel_ok, 1)
                for p in range(2):
                    own.step(nc.vector.max(best[p][:, 0:8], side[p]))
                own.wait()
                for p in range(2):
                    own.step(nc.vector.match_replace(rest[p][:, :], best[p][:, 0:8], side[p], NEG))
                own.wait()
                for p in range(2):
                    own.step(nc.vector.max(best[p][:, 8:16], rest[p][:, :]))
                own.wait()
                at = 0
                for a0, a1, b0, b1 in PARTS:
                    n = (a1 - a0) * (b1 - b0)
                    own.step(nc.vector.tensor_tensor(
                        cand[:, at:at + n].rearrange("p (b a) -> p b a", a=a1 - a0),
                        spread(best[0][:, a0:a1], 1, b1 - b0), spread(best[1][:, b0:b1], 2, a1 - a0), ALU.add))
                    at += n
                own.wait()
                own.step(nc.vector.max(chosen[:, 0:8], cand[:, :]))
                own.wait()
                own.step(nc.vector.match_replace(cand2[:, :], chosen[:, 0:8], cand[:, :], NEG))
                own.wait()
                own.step(nc.vector.max(chosen[:, 8:16], cand2[:, :]))
                assert own.n == PICKS

            def set_cut(v):
                dve.wait_ge(pick, PICKS)
                nc.vector.tensor_copy(cut[:, 0:1], chosen[:, 15:16])
                nc.vector.tensor_scalar(cut[:, 1:2], chosen[:, 0:1], -1.0, None, ALU.mult).then_inc(cut_ok, 1)

            def mask(u, q):
                dve.wait_ge(exp_ok, u * Q + (q + 1))
                dve.wait_ge(cut_ok, u + 1)
                dve.wait_ge(turn_done, u * TURNS + (2 * q - 6 + TURN0))
                nc.vector.scalar_tensor_tensor(weight[q][:, :], total[q][:, :, :].rearrange("p j i -> p (j i)"),
                                               cut[:, 0:1], expo[q % 2][:, :], ALU.is_ge, ALU.mult,
                                               accum_out=zpart[:, q:q + 1]).then_inc(masked, 1)

            select(0)
            set_cut(0)
            with dve.Fori(0, UNITS) as u:
                dve.wait_ge(sum_in, u + 1)
                sum_quarter(nc.vector, 3).then_inc(dve_sum, 1)
                mask(u, 0)
                mask(u, 1)
                select(u + 1)
                mask(u, 2)
                mask(u, 3)
                dve.wait_ge(masked, u * Q + (Q + MASKED0))
                dve.wait_ge(kv_ok, u + LOAN)
                nc.vector.tensor_reduce(zinv[:, :], zpart[:, :], AX.X, ALU.add).then_inc(z_ok, 1)
                set_cut(u + 1)
                dve.wait_ge(z_ok, u + 1)
                nc.vector.reciprocal(zinv[:, :], zinv[:, :]).then_inc(zinv_ok, 1)


def clear(nc, tag, spots):
    with Scope(nc, tag) as s:
        block = s.block()

        @block.gpsimd
        def _(pool):
            for spot in spots:
                nc.gpsimd.memset(spot, 0.0)


def rotary_attention(nc, x, xT, ident, mask, wqkvT, woT, rope):
    NQ, NKV, HD = 4, 2, 16
    QK = (NQ + NKV) * HD
    with Scope(nc, "gqa") as s:
        def two(name, shape):
            return [s.sb(f"{name}{i}", shape) for i in range(2)]
        w_in, w_o = s.sb("w_in", [C, 128]), s.sb("w_o", [C, C])
        cos_sin = s.sb("cos_sin", [ROWS, 2, HD])
        x_g = two("x_g", [C, ROWS])
        part, turn = two("part", [ROWS, QK]), two("turn", [ROWS, QK])
        v_g = two("v_g", [ROWS, NKV * HD])
        q_t, k_t = two("q_t", [HD, NQ * ROWS]), two("k_t", [HD, NKV * ROWS])
        score, prob_t = two("score", [ROWS, NQ, ROWS]), two("prob_t", [ROWS, NQ * ROWS])
        top, tot = two("top", [ROWS, NQ]), two("tot", [ROWS, NQ])
        y, y_t = two("y", [ROWS, 128]), two("y_t", [C, ROWS])
        pad_ok = s.sem("pad")
        bank = [[s.bank(f"b{k}{n}") for n in range(3)] for k in range(2)]
        arrived, x_ok, qkv_done, part_ok, rope_ok, v_ok = (s.sem(n) for n in ("arrived", "x", "qkv", "part", "rope", "v"))
        flip_q, flip_k, q_ok, k_ok, score_done, masked = (s.sem(n) for n in ("flip_q", "flip_k", "q", "k", "score", "masked"))
        top_ok, centered, exp_ok, sum_ok, recip_ok = (s.sem(n) for n in ("top", "sub", "exp", "sum", "recip"))
        flip_p, p_ok, mix_done, y_ok, flip_y, yt_ok, out_done, x_new = (
            s.sem(n) for n in ("flip_p", "p", "mix", "y", "flip_y", "yt", "out", "x_new"))
        block = s.block()

        @block.sync
        def _(sp):
            for dst, src in ((w_in[:, :], wqkvT), (w_o[:, :], woT), (cos_sin[:, :, :], rope)):
                sp.dma_start(dst, src).then_inc(arrived, 16)

        @block.gpsimd
        def _(pool):
            for k in range(2):
                nc.gpsimd.memset(y[k][:, :], 0.0).then_inc(pad_ok, 1)
            with pool.Fori(0, GROUPS // 2) as i:
                for k in range(2):
                    pool.wait_ge(qkv_done, 2 * i + LOAN)
                    nc.gpsimd.tensor_copy(x_g[k][:, :], xT[:, bass.ds((2 * i + k) * ROWS, ROWS)]).then_inc(x_ok, 1)

        @block.tensor
        def _(pe):
            pe.sem_inc(qkv_done, LOAN)
            pe.wait_ge(arrived, 48)
            pe.wait_ge(pad_ok, 2)
            with pe.Fori(0, GROUPS // 2) as i:
                def turn_of(k):
                    return 2 * i + k + 1
                for k in range(2):
                    pe.wait_ge(x_ok, turn_of(k))
                    pe.wait_ge(x_new, 2 * i + LOAN)
                    nc.tensor.matmul(bank[k][0][0:ROWS, 0:128], x_g[k][:, :], w_in[:, :], start=True, stop=True).then_inc(qkv_done, 1)
                for k in range(2):
                    pe.wait_ge(rope_ok, turn_of(k))
                    for h in range(NQ):
                        last = nc.tensor.transpose(bank[k][1][0:HD, h * ROWS:(h + 1) * ROWS],
                                                   part[k][:, h * HD:(h + 1) * HD], ident[0:ROWS, 0:ROWS])
                    last.then_inc(flip_q, 1)
                    for h in range(NKV):
                        last = nc.tensor.transpose(bank[k][2][0:HD, h * ROWS:(h + 1) * ROWS],
                                                   part[k][:, (NQ + h) * HD:(NQ + h + 1) * HD], ident[0:ROWS, 0:ROWS])
                    last.then_inc(flip_k, 1)
                for k in range(2):
                    pe.wait_ge(q_ok, turn_of(k))
                    pe.wait_ge(k_ok, turn_of(k))
                    for h in range(NQ):
                        last = nc.tensor.matmul(bank[k][1][0:ROWS, h * ROWS:(h + 1) * ROWS], q_t[k][:, h * ROWS:(h + 1) * ROWS],
                                                k_t[k][:, (h // 2) * ROWS:(h // 2 + 1) * ROWS], start=True, stop=True)
                    last.then_inc(score_done, 1)
                for k in range(2):
                    pe.wait_ge(exp_ok, turn_of(k))
                    for h in range(NQ):
                        last = nc.tensor.transpose(bank[k][1][0:ROWS, h * ROWS:(h + 1) * ROWS], score[k][:, h, :],
                                                   ident[0:ROWS, 0:ROWS])
                    last.then_inc(flip_p, 1)
                for k in range(2):
                    pe.wait_ge(p_ok, turn_of(k))
                    for h in range(NQ):
                        last = nc.tensor.matmul(bank[k][0][0:ROWS, h * HD:(h + 1) * HD], prob_t[k][:, h * ROWS:(h + 1) * ROWS],
                                                v_g[k][:, (h // 2) * HD:(h // 2 + 1) * HD], start=True, stop=True)
                    last.then_inc(mix_done, 1)
                for k in range(2):
                    pe.wait_ge(y_ok, turn_of(k))
                    nc.tensor.transpose(bank[k][2][:, 0:ROWS], y[k][:, :], ident[0:ROWS, 0:ROWS]).then_inc(flip_y, 1)
                for k in range(2):
                    pe.wait_ge(yt_ok, turn_of(k))
                    nc.tensor.matmul(bank[k][0][0:ROWS, 0:C], y_t[k][:, :], w_o[:, :], start=True, stop=True).then_inc(out_done, 1)

        @block.scalar
        def _(act):
            with act.Fori(0, GROUPS // 2) as i:
                for k in range(2):
                    act.wait_ge(flip_q, 2 * i + k + 1)
                    nc.scalar.copy(q_t[k][:, :], bank[k][1][0:HD, 0:NQ * ROWS]).then_inc(q_ok, 1)
                for k in range(2):
                    act.wait_ge(centered, 2 * i + k + 1)
                    nc.scalar.activation(score[k][:, :, :], score[k][:, :, :], ACT.Exp, scale=HD ** -0.5).then_inc(exp_ok, 1)
                for k in range(2):
                    act.wait_ge(flip_p, 2 * i + k + 1)
                    nc.scalar.copy(prob_t[k][:, :], bank[k][1][0:ROWS, 0:NQ * ROWS]).then_inc(p_ok, 1)
                for k in range(2):
                    act.wait_ge(flip_y, 2 * i + k + 1)
                    nc.scalar.copy(y_t[k][:, :], bank[k][2][0:C, 0:ROWS]).then_inc(yt_ok, 1)

        @block.vector
        def _(dve):
            dve.sem_inc(x_new, LOAN)
            dve.wait_ge(arrived, 48)
            dve.wait_ge(pad_ok, 2)
            with dve.Fori(0, GROUPS // 2) as i:
                for k in range(2):
                    dve.wait_ge(qkv_done, 2 * i + (k + 1 + LOAN))
                    b = bank[k][0]
                    halves = [a[0:ROWS, 0:QK].rearrange("p (h s d) -> p h s d", s=2, d=HD // 2) for a in (b, turn[k])]
                    nc.vector.tensor_tensor(part[k][:, :].rearrange("p (h d) -> p h d", d=HD), b[0:ROWS, 0:QK].rearrange("p (h d) -> p h d", d=HD),
                                            spread(cos_sin[:, 0, :], 1, NQ + NKV), ALU.mult).then_inc(part_ok, 1)
                    for d in range(2):
                        nc.vector.tensor_tensor(halves[1][:, :, d, :], halves[0][:, :, 1 - d, :],
                                                spread(cos_sin[:, 1, d * 8:d * 8 + 8], 1, NQ + NKV), ALU.mult).then_inc(part_ok, 1)
                    nc.vector.tensor_copy(v_g[k][:, :], b[0:ROWS, QK:128]).then_inc(v_ok, 1)
                for k in range(2):
                    dve.wait_ge(part_ok, 6 * i + 3 * k + 3)
                    dve.wait_ge(v_ok, 2 * i + k + 1)
                    nc.vector.tensor_tensor(part[k][:, :], part[k][:, :], turn[k][:, :], ALU.add).then_inc(rope_ok, 1)
                for k in range(2):
                    dve.wait_ge(flip_k, 2 * i + k + 1)
                    nc.vector.tensor_copy(k_t[k][:, :], bank[k][2][0:HD, 0:NKV * ROWS]).then_inc(k_ok, 1)
                for k in range(2):
                    dve.wait_ge(score_done, 2 * i + k + 1)
                    nc.vector.tensor_tensor(score[k][:, :, :], bank[k][1][0:ROWS, 0:NQ * ROWS].rearrange("p (h t) -> p h t", h=NQ),
                                            spread(mask[:, :], 1, NQ), ALU.add).then_inc(masked, 1)
                for k in range(2):
                    dve.wait_ge(masked, 2 * i + k + 1)
                    nc.vector.tensor_reduce(top[k][:, :], score[k][:, :, :], AX.X, ALU.max).then_inc(top_ok, 1)
                for k in range(2):
                    dve.wait_ge(top_ok, 2 * i + k + 1)
                    nc.vector.tensor_tensor(score[k][:, :, :], score[k][:, :, :], spread(top[k][:, :], 2, ROWS),
                                            ALU.subtract).then_inc(centered, 1)
                for k in range(2):
                    dve.wait_ge(exp_ok, 2 * i + k + 1)
                    nc.vector.tensor_reduce(tot[k][:, :], score[k][:, :, :], AX.X, ALU.add).then_inc(sum_ok, 1)
                    dve.wait_ge(sum_ok, 2 * i + k + 1)
                    nc.vector.reciprocal(tot[k][:, :], tot[k][:, :]).then_inc(recip_ok, 1)
                for k in range(2):
                    dve.wait_ge(recip_ok, 2 * i + k + 1)
                    dve.wait_ge(mix_done, 2 * i + k + 1)
                    nc.vector.tensor_tensor(y[k][:, 0:C].rearrange("p (h d) -> p h d", h=NQ),
                                            bank[k][0][0:ROWS, 0:C].rearrange("p (h d) -> p h d", h=NQ),
                                            spread(tot[k][:, :], 2, HD), ALU.mult).then_inc(y_ok, 1)
                for k in range(2):
                    dve.wait_ge(out_done, 2 * i + k + 1)
                    row = x[:, bass.ds(2 * i + k, 1), :].rearrange("p g c -> p (g c)")
                    nc.vector.tensor_tensor(row, row, bank[k][0][0:ROWS, 0:C], ALU.add).then_inc(x_new, 1)


def gates(nc, xT, routerT, gate):
    with Scope(nc, "gate") as s:
        w = s.sb("w", [C, NEXP])
        prob, best = s.sb("prob", [ROWS, GROUPS, NEXP]), s.sb("best", [ROWS, GROUPS, 8])
        red = s.sb("red", [ROWS, GROUPS])
        logits = s.bank("logits")
        w_in, logits_done, centered, exp_ok, own_sem = (s.sem(n) for n in ("w_in", "logits", "sub", "exp", "own"))
        block = s.block()

        @block.sync
        def _(sp):
            sp.dma_start(w[:, :], routerT).then_inc(w_in, 16)

        @block.tensor
        def _(pe):
            pe.wait_ge(w_in, 16)
            for g in range(GROUPS):
                last = nc.tensor.matmul(logits[0:ROWS, g * NEXP:(g + 1) * NEXP], xT[:, g * ROWS:(g + 1) * ROWS], w[:, :],
                                        start=True, stop=True)
            last.then_inc(logits_done, 1)

        @block.scalar
        def _(act):
            act.wait_ge(centered, 1)
            nc.scalar.activation(prob[:, :, :], prob[:, :, :], ACT.Exp).then_inc(exp_ok, 1)

        @block.vector
        def _(dve):
            own = Chain(dve, own_sem)

            def then(ins):
                own.step(ins)
                own.wait()

            dve.wait_ge(logits_done, 1)
            then(nc.vector.tensor_reduce(red[:, :], logits[0:ROWS, 0:GROUPS * NEXP].rearrange("p (g e) -> p g e", g=GROUPS), AX.X, ALU.max))
            nc.vector.tensor_tensor(prob[:, :, :], logits[0:ROWS, 0:GROUPS * NEXP].rearrange("p (g e) -> p g e", g=GROUPS),
                                    spread(red[:, :], 2, NEXP), ALU.subtract).then_inc(centered, 1)
            dve.wait_ge(exp_ok, 1)
            then(nc.vector.tensor_reduce(red[:, :], prob[:, :, :], AX.X, ALU.add))
            then(nc.vector.reciprocal(red[:, :], red[:, :]))
            then(nc.vector.tensor_tensor(prob[:, :, :], prob[:, :, :], spread(red[:, :], 2, NEXP), ALU.mult))
            for g in range(GROUPS):
                own.step(nc.vector.max(best[:, g, :], prob[:, g, :]))
            own.wait()
            then(nc.vector.tensor_tensor(red[:, :], best[:, :, 0], best[:, :, 1], ALU.add))
            then(nc.vector.tensor_scalar(red[:, :], red[:, :], 1e-9, None, ALU.add))
            then(nc.vector.reciprocal(red[:, :], red[:, :]))
            then(nc.vector.tensor_tensor(gate[:, :, :], prob[:, :, :], best[:, :, 1:2].broadcast_to([ROWS, GROUPS, NEXP]), ALU.is_ge))
            then(nc.vector.tensor_tensor(gate[:, :, :], gate[:, :, :], prob[:, :, :], ALU.mult))
            nc.vector.tensor_tensor(gate[:, :, :], gate[:, :, :], spread(red[:, :], 2, NEXP), ALU.mult)


def experts(nc, hid, x, xT, gate, w1T, w3T, w2T):
    PAIR = 2 * ROWS
    HALVES = 2 * NEXP
    with Scope(nc, "moe") as s:
        w1, w3 = s.sb("w1", [C, NEXP * HID]), s.sb("w3", [C, NEXP * HID])
        w2 = s.sb("w2", [HH, HALVES, C])
        x_p = s.sb("x_p", [C, PAIR])
        silu = [s.sb(f"silu{i}", [HH, PAIR]) for i in range(3)]
        hidden = s.sb("hidden", [HH, HALVES, PAIR])
        gated = [s.sb(f"gated{i}", [ROWS, NEXP, C]) for i in range(2)]
        mixed = [s.sb(f"mixed{i}", [ROWS, C]) for i in range(2)]
        up = [s.bank(f"up{i}") for i in range(3)]
        down = [s.bank(f"down{i}") for i in range(2)]
        arrived, x_ok, up_done, silu_ok, hidden_ok = (s.sem(n) for n in ("arrived", "x", "up", "silu", "hidden"))
        down_done, gated_ok, mixed_ok, hid_x = s.sem("down"), s.sem("gated"), s.sem("mixed"), s.sem("hid_x")
        block = s.block()
        HIDDEN0 = 2 + LOAN

        @block.sync
        def _(sp):
            for dst, src in ((w1[:, :], w1T), (w3[:, :], w3T), (w2[:, :, :], w2T)):
                sp.dma_start(dst, src).then_inc(arrived, 16)

        @block.gpsimd
        def _(pool):
            with pool.Fori(0, GROUPS // 2) as i:
                pool.wait_ge(up_done, HALVES * i + LOAN)
                nc.gpsimd.tensor_copy(x_p[:, :], xT[:, bass.ds(i * PAIR, PAIR)]).then_inc(x_ok, 1)

        @block.tensor
        def _(pe):
            pe.sem_inc(up_done, LOAN)
            pe.sem_inc(down_done, LOAN)
            pe.wait_ge(arrived, 48)
            with pe.Fori(0, GROUPS // 2) as i:
                pe.wait_ge(x_ok, i + 1)
                for c in range(HALVES):
                    pe.wait_ge(hidden_ok, HALVES * i + (c - 2 + HIDDEN0))
                    nc.tensor.matmul(up[c % 3][0:HH, 0:PAIR], w1[:, c * HH:(c + 1) * HH], x_p[:, :], start=True, stop=True)
                    nc.tensor.matmul(up[c % 3][0:HH, 256:256 + PAIR], w3[:, c * HH:(c + 1) * HH], x_p[:, :],
                                     start=True, stop=True).then_inc(up_done, 1)
                pe.wait_ge(hidden_ok, HALVES * i + (HALVES + HIDDEN0))
                pe.wait_ge(gated_ok, 2 * i + LOAN)
                for k in range(2):
                    for c in range(HALVES):
                        last = nc.tensor.matmul(down[k][0:ROWS, (c // 2) * C:(c // 2 + 1) * C], hidden[:, c, k * ROWS:(k + 1) * ROWS],
                                                w2[:, c, :], start=c % 2 == 0, stop=c % 2 == 1)
                    last.then_inc(down_done, 1)

        @block.scalar
        def _(act):
            with act.Fori(0, GROUPS // 2) as i:
                for c in range(HALVES):
                    act.wait_ge(up_done, HALVES * i + (c + 1 + LOAN))
                    act.wait_ge(hidden_ok, HALVES * i + (c - 2 + HIDDEN0))
                    nc.scalar.activation(silu[c % 3][:, :], up[c % 3][0:HH, 0:PAIR], ACT.Silu).then_inc(silu_ok, 1)

        @block.vector
        def _(dve):
            dve.sem_inc(gated_ok, LOAN)
            dve.sem_inc(hidden_ok, HIDDEN0)
            nc.vector.tensor_tensor(hid[:, :, :], hid[:, :, :], x[:, :, :], ALU.add).then_inc(hid_x, 1)
            dve.wait_ge(hid_x, 1)
            with dve.Fori(0, GROUPS // 2) as i:
                dve.wait_ge(down_done, 2 * i + LOAN)
                for c in range(HALVES):
                    dve.wait_ge(silu_ok, HALVES * i + (c + 1))
                    nc.vector.tensor_tensor(hidden[:, c, :], silu[c % 3][:, :], up[c % 3][0:HH, 256:256 + PAIR],
                                            ALU.mult).then_inc(hidden_ok, 1)
                for k in range(2):
                    dve.wait_ge(down_done, 2 * i + (k + 1 + LOAN))
                    one = bass.ds(2 * i + k, 1)
                    nc.vector.tensor_tensor(gated[k][:, :, :], down[k][0:ROWS, :].rearrange("p (e c) -> p e c", e=NEXP),
                                            gate[:, one, :].rearrange("p o e -> p e o").broadcast_to([ROWS, NEXP, C]), ALU.mult).then_inc(gated_ok, 1)
                for k in range(2):
                    dve.wait_ge(gated_ok, 2 * i + (k + 1 + LOAN))
                    nc.vector.tensor_reduce(mixed[k][:, :], gated[k][:, :, :].rearrange("p e c -> p c e"), AX.X, ALU.add).then_inc(mixed_ok, 1)
                for k in range(2):
                    dve.wait_ge(mixed_ok, 2 * i + k + 1)
                    row = hid[:, bass.ds(2 * i + k, 1), :].rearrange("p g c -> p (g c)")
                    nc.vector.tensor_tensor(row, row, mixed[k][:, :], ALU.add)


def vision_tower(nc, x_img, cls_tok, tok_w, tok_b, a_wq, a_wk, a_wv, a_mlp, a_b, unmix,
                 ln1, ln2, wqkv, wo, router, w1, w2, w3, rope,
                 key_m, query_m, value_in, value_out, pk_w, pk_k, mem_wq, table, mem_wo, ident_in, mask_in, out):
    Scope.spent = []
    with Scope(nc, "all") as s:
        hid = s.sb("hid", [ROWS, GROUPS, C])
        x = s.sb("x", [ROWS, GROUPS, C])
        xT = s.sb("xT", [C, COLS])
        ident, mask = s.sb("ident", [128, 128]), s.sb("mask", [ROWS, ROWS])

        load(nc, "consts", [(ident[:, :], ident_in), (mask[:, :], mask_in)])
        embed(nc, hid, x_img, tok_w, cls_tok, tok_b)
        normalize(nc, "ln_a", hid, x, xT, ident, True, 1e-5)
        relu_attention(nc, hid, xT, ident, a_wq, a_wk, a_wv, a_mlp, a_b, unmix)
        normalize(nc, "ln_b", hid, x, xT, ident, True, 1e-5)
        with Scope(nc, "first") as f:
            scaled = f.sb("scaled", [ROWS, GROUPS, C])
            gate = f.sb("gate", [ROWS, GROUPS, NEXP])
            normalize(nc, "rms_a", x, scaled, xT, ident, False, 1e-6, ln1)
            rotary_attention(nc, x, xT, ident, mask, wqkv, wo, rope)
            normalize(nc, "rms_b", x, scaled, xT, ident, False, 1e-6, ln2)
            gates(nc, xT, router, gate)
            experts(nc, hid, x, xT, gate, w1, w3, w2)

        normalize(nc, "ln_c", hid, x, xT, ident, True, 1e-5)
        with Scope(nc, "second") as f:
            raw = [f.sb(f"raw{n}", [C, HEADS, C]) for n in range(4)]
            score_w, value_w = f.sb("score_w", [C, HEADS, C]), f.sb("value_w", [C, HEADS, C])
            load(nc, "raw", [(r[:, :, :], a) for r, a in zip(raw, (key_m, query_m, value_in, value_out))])
            merge(nc, "merge", [(raw[2 * m][:, h, :], raw[2 * m + 1][:, h, :]) for m in range(2) for h in range(HEADS)],
                  [w[:, :, :].rearrange("p h c -> p (h c)") for w in (score_w, value_w)])
            head_attention(nc, "mha", hid, xT, ident, mask, score_w, value_w, 1.0)

        normalize(nc, "ln_d", hid, x, xT, ident, True, 1e-5)
        with Scope(nc, "third") as f:
            kv_t = f.sb("kv_t", [128, KVT])
            with Scope(nc, "keys") as g:
                side_w = g.sb("side_w", [C, HEADS + 1, 128])
                a, b = g.sb("a", [32, 2 * HEADS, C]), g.sb("b", [32, 2 * HEADS, C])
                load(nc, "pk_in", [(a[:, :, :], pk_w), (b[:, :, :], pk_k)])
                clear(nc, "clear", [side_w[:, HEADS, :], kv_t[:, 128 + HEADS * PADT:]])
                merge(nc, "merge2", [(a[:, n, :], b[:, n, :]) for n in range(2 * HEADS)],
                      [side_w[:, 4 * m:4 * m + 4, :].rearrange("p h c -> p (h c)") for m in range(2)])
                product_keys(nc, xT, ident, side_w, table, kv_t)
            wq, wv = f.sb("wq", [C, HEADS, C]), f.sb("wv", [128, HEADS, C])
            clear(nc, "clear2", [wv[0:C, :, :]])
            load(nc, "wo", [(wq[:, :, :], mem_wq), (wv[C:128, :, :], mem_wo)])
            head_attention(nc, "mem", hid, xT, ident, mask, wq, wv, C ** -0.5, kv_t)
        load(nc, "store", [(out, hid[:, :, :])])


def _constants():
    mask = np.full((ROWS, ROWS), -1e30, np.float32)
    for m in range(PER):
        for i in range(TOK):
            mask[m * TOK + i, m * TOK:m * TOK + i + 1] = 0
    unmix = np.zeros((C, C), np.float32)
    for g in range(2):
        for d in range(32):
            unmix[g * 32 + d, d * 2 + g] = 1
    hd = 16
    inv = 1.0 / 10000.0 ** (np.arange(0, hd, 2, dtype=np.float32) / hd)
    angle = np.outer(np.arange(TOK, dtype=np.float32), inv)
    sin, cos = np.sin(angle), np.cos(angle)
    table = np.stack([np.concatenate([cos, cos], 1), np.concatenate([-sin, sin], 1)], 1)
    return {"unmix": unmix, "rope": np.tile(table, (PER, 1, 1)).astype(np.float32),
            "ident_in": np.eye(128, dtype=np.float32), "mask_in": mask}


def kernel(x, cls_tok, L0_tok_W, L0_tok_b, L0_attn_Wq, L0_attn_Wk, L0_attn_Wv, L0_attn_w_mlp, L0_attn_b_mlp,
           L0_ffn_ln1_w, L0_ffn_ln2_w, L0_ffn_wq, L0_ffn_wk, L0_ffn_wv, L0_ffn_wo, L0_ffn_router_w, L0_ffn_w1,
           L0_ffn_w2, L0_ffn_w3, L1_attn_key_matrices, L1_attn_query_matrices, L1_attn_value_in_matrices,
           L1_attn_value_out_matrices, L1_ffn_Wq_pk, L1_ffn_pk_keys, L1_ffn_Wq, L1_ffn_keys_table,
           L1_ffn_values_table, L1_ffn_Wo):
    import concourse.bacc as bacc
    from concourse.bass_utils import run_bass_kernel_spmd

    patches = np.asarray(x).reshape(IMAGES, 3, 6, 16, 6, 16).transpose(0, 2, 4, 1, 3, 5).reshape(IMAGES, 36, 768)
    tokens = np.zeros((GROUPS * PER, TOK, 768), np.float32)
    tokens[:IMAGES, 1:] = patches
    consts = _constants()
    table = np.concatenate([L1_ffn_keys_table, L1_ffn_values_table], 1)
    arrays = {
        "x_img": tokens.reshape(GROUPS, ROWS, KCH, 128).transpose(0, 3, 2, 1).reshape(GROUPS, 128, KCH * ROWS),
        "cls_tok": np.asarray(cls_tok).reshape(1, C),
        "tok_w": np.asarray(L0_tok_W).T.reshape(KCH, 128, C).transpose(1, 0, 2).reshape(128, KCH * C),
        "tok_b": L0_tok_b,
        "a_wq": np.asarray(L0_attn_Wq).T, "a_wk": np.asarray(L0_attn_Wk).T,
        "a_wv": np.asarray(L0_attn_Wv).reshape(32, 2, C).transpose(1, 0, 2).reshape(C, C).T,
        "a_mlp": L0_attn_w_mlp, "a_b": L0_attn_b_mlp, "unmix": consts["unmix"],
        "ln1": L0_ffn_ln1_w, "ln2": L0_ffn_ln2_w,
        "wqkv": np.concatenate([L0_ffn_wq, L0_ffn_wk, L0_ffn_wv]).T, "wo": np.asarray(L0_ffn_wo).T,
        "router": np.asarray(L0_ffn_router_w).T,
        "w1": np.asarray(L0_ffn_w1).transpose(2, 0, 1).reshape(C, NEXP * HID),
        "w2": np.asarray(L0_ffn_w2).reshape(NEXP, C, 2, HH).transpose(3, 0, 2, 1).reshape(HH, 2 * NEXP, C),
        "w3": np.asarray(L0_ffn_w3).transpose(2, 0, 1).reshape(C, NEXP * HID),
        "rope": consts["rope"],
        "key_m": np.asarray(L1_attn_key_matrices).transpose(2, 0, 1),
        "query_m": np.asarray(L1_attn_query_matrices).transpose(2, 0, 1),
        "value_in": np.asarray(L1_attn_value_in_matrices).transpose(2, 0, 1),
        "value_out": np.asarray(L1_attn_value_out_matrices).transpose(1, 0, 2),
        "pk_w": np.asarray(L1_ffn_Wq_pk).reshape(C, 2, HEADS, 32).transpose(3, 2, 1, 0).reshape(32, 2 * HEADS, C),
        "pk_k": np.asarray(L1_ffn_pk_keys).transpose(3, 2, 0, 1).reshape(32, 2 * HEADS, KEYS),
        "mem_wq": np.asarray(L1_ffn_Wq).reshape(C, HEADS, C),
        "table": table.reshape(HEADS, CHUNKS, 128, 128).transpose(0, 2, 1, 3),
        "mem_wo": np.asarray(L1_ffn_Wo).reshape(HEADS, C, C).transpose(1, 0, 2),
        "ident_in": consts["ident_in"], "mask_in": consts["mask_in"],
    }
    nc = bacc.Bacc("TRN2", target_bir_lowering=False, num_devices=1)
    arrays = {f"in_{n}": np.ascontiguousarray(a) for n, a in arrays.items()}
    args = {n[3:]: nc.dram_tensor(n, a.shape, mybir.dt.from_np(a.dtype), kind="ExternalInput").ap() for n, a in arrays.items()}
    out = nc.dram_tensor("out", (ROWS, GROUPS, C), F32, kind="ExternalOutput").ap()
    vision_tower(nc, **args, out=out)
    got = run_bass_kernel_spmd(nc, [arrays], core_ids=[0]).results[0]["out"]
    return got.transpose(1, 0, 2).reshape(GROUPS * PER, TOK, C)[:IMAGES]
```

```python
from contextlib import ExitStack

import numpy as np

import concourse.bass as bass
from concourse import mybir

F32 = mybir.dt.float32
ALU = mybir.AluOpType
ACT = mybir.ActivationFunctionType
AX = mybir.AxisListType

C = 64
IMAGES, TOK = 64, 37
PER = 3
ROWS = PER * TOK
GROUPS = 22
COLS = ROWS * GROUPS
KCH = 6
BANK = 512
NEXP, HID = 8, 170
HH = HID // 2
HEADS = 8
KEYS = 64
TOPK = 16
ENT = KEYS * KEYS
CHUNKS = ENT // 128
TILES = -(-IMAGES * TOK // 128)
UNITS = HEADS * TILES
PADT = TILES * 128
KVT = 128 + HEADS * PADT + COLS
NEG = -3.0e38
LOAN = 1


class Scope:

    spent = []

    def __init__(self, nc, tag):
        self.nc, self.tag = nc, tag
        self.ctx, self.sem_ctx, self.sems, self.old = ExitStack(), ExitStack(), [], []

    def __enter__(self):
        return self

    def __exit__(self, *a):
        self.ctx.close()
        for ctx, _ in self.old:
            ctx.close()
        if self.sems:
            Scope.spent.append((self.sem_ctx, self.sems))

    def sb(self, name, shape, dt=F32):
        return self.ctx.enter_context(self.nc.sbuf_tensor(f"{self.tag}_{name}", shape, dt))

    def bank(self, name):
        return self.ctx.enter_context(self.nc.psum_tensor(f"{self.tag}_{name}", [128, BANK], F32))

    def sem(self, name):
        self.sems.append(self.sem_ctx.enter_context(self.nc.semaphore(f"{self.tag}_{name}")))
        return self.sems[-1]

    def block(self):
        block = self.ctx.enter_context(self.nc.Block())
        self.old, Scope.spent = Scope.spent, []

        @block.sync
        def _(sp):
            for _, sems in self.old:
                for sem in sems:
                    sp.sem_clear(sem)
        return block


class Chain:

    def __init__(self, eng, sem, base=0):
        self.eng, self.sem, self.base, self.n = eng, sem, base, 0

    def step(self, ins):
        ins.then_inc(self.sem, 1)
        self.n += 1

    def wait(self):
        self.eng.wait_ge(self.sem, self.base + self.n)


def spread(ap, axis, n):
    a = ap.unsqueeze(axis)
    shape = list(a.shape)
    shape[axis] = n
    return a.broadcast_to(shape)


def embed(nc, hid, x_img, w_tokT, cls_tok, b_tok):
    with Scope(nc, "tok") as s:
        patches = [s.sb(f"patches{i}", [128, KCH * ROWS]) for i in range(2)]
        w = s.sb("w", [128, KCH * C])
        add = s.sb("add", [ROWS, C])
        acc = [s.bank(f"acc{i}") for i in range(2)]
        w_in, bias_in, cls_in = s.sem("w_in"), s.sem("bias_in"), s.sem("cls_in")
        patches_in = [s.sem(f"patches_in{i}") for i in range(2)]
        product_done, row_done = s.sem("product_done"), s.sem("row_done")
        block = s.block()

        @block.sync
        def _(sp):
            sp.dma_start(w[:, :], w_tokT).then_inc(w_in, 16)
            with sp.Fori(0, GROUPS // 2) as i:
                for k in range(2):
                    sp.wait_ge(product_done, 2 * i + LOAN)
                    sp.dma_start(patches[k][:, :], x_img[bass.ds(2 * i + k, 1), :, :].rearrange("g p n -> (g p) n")).then_inc(patches_in[k], 16)

        @block.scalar
        def _(act):
            act.dma_start(add[:, :], b_tok.rearrange("(o c) -> o c", o=1).broadcast_to([ROWS, C])).then_inc(bias_in, 16)
            act.wait_ge(bias_in, 16)
            for m in range(PER):
                act.dma_start(add[m * TOK:m * TOK + 1, :], cls_tok).then_inc(cls_in, 16)

        @block.tensor
        def _(pe):
            pe.sem_inc(product_done, LOAN)
            pe.wait_ge(w_in, 16)
            with pe.Fori(0, GROUPS // 2) as i:
                for k in range(2):
                    pe.wait_ge(patches_in[k], 16 * i + 16)
                    pe.wait_ge(row_done, 2 * i + LOAN)
                    for c in range(KCH):
                        last = nc.tensor.matmul(acc[k][0:ROWS, 0:C], patches[k][:, c * ROWS:(c + 1) * ROWS],
                                                w[:, c * C:(c + 1) * C], start=c == 0, stop=c == KCH - 1)
                    last.then_inc(product_done, 1)

        @block.vector
        def _(dve):
            dve.sem_inc(row_done, LOAN)
            dve.wait_ge(bias_in, 16)
            dve.wait_ge(cls_in, 16 * PER)
            with dve.Fori(0, GROUPS // 2) as i:
                for k in range(2):
                    dve.wait_ge(product_done, 2 * i + (k + 1 + LOAN))
                    nc.vector.tensor_tensor(hid[:, bass.ds(2 * i + k, 1), :].rearrange("p g c -> p (g c)"),
                                            acc[k][0:ROWS, 0:C], add[:, :], ALU.add).then_inc(row_done, 1)


def normalize(nc, tag, src, dst, xT, ident, center, eps, weight=None):
    with Scope(nc, tag) as s:
        row = [ROWS, GROUPS]
        work = s.sb("work", [ROWS, GROUPS, C])
        mean, power, rstd = s.sb("mean", row), s.sb("power", row), s.sb("rstd", row)
        flip = [s.bank(f"flip{i}") for i in range(6)]
        centered_ok, square_ok, power_ok, rstd_ok = (s.sem(n) for n in ("centered", "square", "power", "rstd"))
        out_ok, flip_ok, dve_own = s.sem("out"), s.sem("flip"), s.sem("dve_own")
        w_in = s.sem("w_in")
        xc = dst if center else src
        if weight is not None:
            wrow = s.sb("wrow", [ROWS, C])
        block = s.block()
        quads = [(n, min(4, GROUPS - 4 * n)) for n in range(6)]

        @block.sync
        def _(sp):
            if weight is not None:
                sp.dma_start(wrow[:, :], weight.rearrange("(o c) -> o c", o=1).broadcast_to([ROWS, C])).then_inc(w_in, 16)

        @block.vector
        def _(dve):
            own = Chain(dve, dve_own)
            if center:
                own.step(nc.vector.tensor_reduce(mean[:, :], src[:, :, :], AX.X, ALU.add))
                own.wait()
                own.step(nc.vector.tensor_scalar(mean[:, :], mean[:, :], 1.0 / C, None, ALU.mult))
                own.wait()
                nc.vector.tensor_tensor(dst[:, :, :], src[:, :, :], spread(mean[:, :], 2, C),
                                        ALU.subtract).then_inc(centered_ok, 1)
            dve.wait_ge(square_ok, 1)
            own.step(nc.vector.tensor_reduce(power[:, :], work[:, :, :], AX.X, ALU.add))
            own.wait()
            nc.vector.tensor_scalar(power[:, :], power[:, :], eps, None, ALU.add).then_inc(power_ok, 1)
            dve.wait_ge(rstd_ok, 1)
            own.step(nc.vector.reciprocal(rstd[:, :], rstd[:, :]))
            own.wait()
            if center:
                dve.wait_ge(centered_ok, 1)
            last = nc.vector.tensor_tensor(dst[:, :, :], xc[:, :, :], spread(rstd[:, :], 2, C), ALU.mult)
            if weight is not None:
                own.step(last)
                own.wait()
                dve.wait_ge(w_in, 16)
                last = nc.vector.tensor_tensor(dst[:, :, :], dst[:, :, :], spread(wrow[:, :], 1, GROUPS), ALU.mult)
            last.then_inc(out_ok, 1)
            for n, m in quads[1::2]:
                dve.wait_ge(flip_ok, n + 1)
                nc.vector.tensor_copy(xT[:, 4 * n * ROWS:(4 * n + m) * ROWS], flip[n][0:C, 0:m * ROWS])

        @block.scalar
        def _(act):
            if center:
                act.wait_ge(centered_ok, 1)
            nc.scalar.activation(work[:, :, :], xc[:, :, :], ACT.Square, scale=C ** -0.5).then_inc(square_ok, 1)
            act.wait_ge(power_ok, 1)
            nc.scalar.activation(rstd[:, :], power[:, :], ACT.Sqrt).then_inc(rstd_ok, 1)
            for n, m in quads[0::2]:
                act.wait_ge(flip_ok, n + 1)
                nc.scalar.copy(xT[:, 4 * n * ROWS:(4 * n + m) * ROWS], flip[n][0:C, 0:m * ROWS])

        @block.tensor
        def _(pe):
            pe.wait_ge(out_ok, 1)
            for n, m in quads:
                for j in range(m):
                    last = nc.tensor.transpose(flip[n][0:C, j * ROWS:(j + 1) * ROWS], dst[:, 4 * n + j, :],
                                               ident[0:ROWS, 0:ROWS])
                last.then_inc(flip_ok, 1)


def relu_attention(nc, hid, xT, ident, wqT, wkT, wvT, w_mlp, b_mlp, unmix):
    HALF = IMAGES // 2
    D = 32
    with Scope(nc, "rat") as s:
        q, k = s.sb("q", [128, HALF, TOK]), s.sb("k", [128, HALF, TOK])
        w3 = s.sb("w3", [C, 3 * C])
        window = s.sb("window", [128, 252])
        b_sb = s.sb("b_sb", [1, 1])
        zrow = s.sb("zrow", [1, BANK])
        ones = s.sb("ones", [1, 128])
        brow = s.sb("brow", [1, BANK])
        wst = [s.sb(f"wst{i}", [128, 128]) for i in range(2)]
        diff = [s.sb(f"diff{i}", [128, TOK, TOK]) for i in range(2)]
        logit = s.sb("logit", [128, TOK, TOK])
        top, tot = s.sb("top", [128, TOK]), s.sb("tot", [128, TOK])
        prob_t = s.sb("prob_t", [TOK, TOK, 128])
        x8 = s.sb("x8", [C, 7 * TOK + 128])
        v8 = s.sb("v8", [TOK, 9 * C])
        out_t = s.sb("out_t", [C, COLS])
        unmix_sb = s.sb("unmix", [C, C])
        bank = [s.bank(f"b{i}") for i in range(8)]
        w_in, win_in, zero_ok, ones_ok, b_ok = (s.sem(n) for n in ("w_in", "win_in", "zero", "ones", "b"))
        qk_done, q_out, k_out = s.sem("qk_done"), s.sem("q_out"), s.sem("k_out")
        win_ok, diff_ok, relu_ok, pair_done = (s.sem(n) for n in ("win", "diff", "relu", "pair_done"))
        logits_done, logit_ok, own, exp_ok, prob_ok = (s.sem(n) for n in ("logits_done", "logit", "dve_own", "exp", "prob"))
        flip_ok, flip_a, flip_d = s.sem("flip"), s.sem("flip_a"), s.sem("flip_d")
        x8_ok, v_done, v8_ok, mix_done, mix_out = (s.sem(n) for n in ("x8", "v_done", "v8", "mix_done", "mix_out"))
        back_ok, centered = s.sem("back"), s.sem("sub")
        block = s.block()
        PARTS = ((0, 13), (13, 12), (25, 12))
        FLIPS = -(-TOK // 4)

        @block.sync
        def _(sp):
            sp.dma_start(w3[:, 0:C], wqT).then_inc(w_in, 16)
            sp.dma_start(w3[:, C:2 * C], wkT).then_inc(w_in, 16)
            sp.dma_start(w3[:, 2 * C:3 * C], wvT).then_inc(w_in, 16)
            sp.dma_start(unmix_sb[:, :], unmix).then_inc(w_in, 16)
            sp.dma_start(b_sb[:, :], b_mlp.rearrange("(o c) -> o c", o=1)).then_inc(w_in, 16)
            sp.wait_ge(zero_ok, 1)
            for m in range(4):
                sp.dma_start(window[m * D:(m + 1) * D, 124 + m:125 + m],
                             w_mlp.rearrange("(d o) -> d o", o=1)).then_inc(win_in, 16)

        @block.gpsimd
        def _(pool):
            nc.gpsimd.memset(window[:, :], 0.0).then_inc(zero_ok, 1)
            nc.gpsimd.memset(out_t[:, :], 0.0).then_inc(zero_ok, 1)
            nc.gpsimd.memset(zrow[:, :], 0.0).then_inc(ones_ok, 1)
            nc.gpsimd.memset(ones[:, :], 1.0).then_inc(ones_ok, 1)
            nc.gpsimd.memset(v8[:, :], 0.0).then_inc(ones_ok, 1)
            nc.gpsimd.memset(x8[:, :], 0.0).then_inc(ones_ok, 1)
            pool.wait_ge(w_in, 80)
            pool.wait_ge(ones_ok, 1)
            nc.gpsimd.tensor_scalar(brow[:, :], zrow[:, :], b_sb[0:1, 0:1], None, ALU.add).then_inc(b_ok, 1)
            pool.wait_ge(win_in, 64)
            with pool.Fori(0, HALF // 2) as i:
                for m in range(2):
                    at = pool.snap(i * -8 + (124 - 4 * m))
                    pool.wait_ge(pair_done, 2 * i + LOAN)
                    nc.gpsimd.tensor_copy(wst[m][:, :], window[:, bass.ds(at, 128)]).then_inc(win_ok, 1)
            for hf in range(2):
                with pool.Fori(0, 4) as c:
                    pool.wait_ge(v_done, c + (4 * hf + LOAN))
                    nc.gpsimd.tensor_copy(x8[:, 0:8 * TOK], xT[:, bass.ds((4 * hf * 8 * TOK) + c * (8 * TOK), 8 * TOK)]).then_inc(x8_ok, 1)

        @block.tensor
        def _(pe):
            pe.sem_inc(pair_done, LOAN)
            pe.sem_inc(v_done, LOAN)
            pe.wait_ge(w_in, 80)
            for n in range(4):
                for j in range(2):
                    for hf in range(2):
                        at = (hf * 4 + n) * 8 * TOK
                        last = nc.tensor.matmul(bank[2 * n + j][C * hf:C * hf + C, 0:8 * TOK], w3[:, j * C:(j + 1) * C],
                                                xT[:, at:at + 8 * TOK], start=True, stop=True)
                last.then_inc(qk_done, 1)
            pe.wait_ge(ones_ok, 4)
            pe.wait_ge(q_out, 2)
            pe.wait_ge(k_out, 2)
            for b, (r, n) in enumerate(PARTS):
                nc.tensor.matmul(bank[b][:, 0:n * TOK], ones[:, :], zrow[:, 0:n * TOK], start=True, stop=False)
            with pe.Fori(0, HALF // 2) as i:
                for m in range(2):
                    pe.wait_ge(win_ok, 2 * i + m + 1)
                    pe.wait_ge(relu_ok, 2 * i + m + 1)
                    for b, (r, n) in enumerate(PARTS):
                        last = nc.tensor.matmul(bank[b][:, 0:n * TOK], wst[m][:, :], diff[m][:, r:r + n, :],
                                                start=False, stop=False)
                    last.then_inc(pair_done, 1)
            pe.wait_ge(b_ok, 1)
            for b, (r, n) in enumerate(PARTS):
                nc.tensor.matmul(bank[b][:, 0:n * TOK], ones[:, :], brow[:, 0:n * TOK],
                                 start=False, stop=True).then_inc(logits_done, 1)
            pe.wait_ge(prob_ok, 1)
            for n in range(FLIPS):
                if n >= 4:
                    pe.wait_ge((flip_a, flip_d)[n % 2], (n - 4) // 2 + 1)
                for r in range(4 * n, min(4 * n + 4, TOK)):
                    last = nc.tensor.transpose(bank[3 + n % 4][0:TOK, (r % 4) * 128:(r % 4 + 1) * 128], logit[:, r, :],
                                               ident[:, :])
                last.then_inc(flip_ok, 1)
            pe.wait_ge(flip_a, FLIPS // 2)
            pe.wait_ge(flip_d, FLIPS // 2)
            for hf in range(2):
                with pe.Fori(0, 4) as c:
                    pe.wait_ge(x8_ok, c + 4 * hf + 1)
                    for j in range(8):
                        last = nc.tensor.matmul(bank[7][:, j * C:(j + 1) * C], x8[:, j * TOK:j * TOK + 128],
                                                w3[:, 2 * C:3 * C], start=True, stop=True)
                    last.then_inc(v_done, 1)
                    pe.wait_ge(v8_ok, c + 4 * hf + 1)
                    pe.wait_ge(mix_out, 4 * c + (16 * hf + LOAN))
                    for j in range(8):
                        last = nc.tensor.matmul(bank[j // 4][:, (j % 4) * 2 * TOK:(j % 4 + 1) * 2 * TOK],
                                                v8[:, j * C:j * C + 128],
                                                prob_t[:, :, bass.ds(4 * j + 2 * hf + c * 32, 2)], start=True, stop=True)
                    last.then_inc(mix_done, 1)
            pe.wait_ge(mix_out, 32 + LOAN)
            for g in range(GROUPS):
                last = nc.tensor.matmul(bank[3 + g // 8][0:ROWS, (g % 8) * C:(g % 8 + 1) * C],
                                        out_t[:, g * ROWS:(g + 1) * ROWS], unmix_sb[:, :], start=True, stop=True)
                if g % 8 == 7 or g == GROUPS - 1:
                    last.then_inc(back_ok, 1)

        @block.scalar
        def _(act):
            for n in range(4):
                act.wait_ge(qk_done, n + 1)
                nc.scalar.copy(q[:, n * 8:(n + 1) * 8, :].rearrange("p i t -> p (i t)"), bank[2 * n][:, 0:8 * TOK]).then_inc(q_out, 1)
            with act.Fori(0, HALF // 2) as i:
                for m in range(2):
                    act.wait_ge(diff_ok, 2 * i + m + 1)
                    nc.scalar.activation(diff[m][:, :, :], diff[m][:, :, :], ACT.Relu).then_inc(relu_ok, 1)
            for b, (r, n) in enumerate(PARTS):
                act.wait_ge(logits_done, 3)
                nc.scalar.activation(logit[:, r:r + n, :].rearrange("p a b -> p (a b)"), bank[b][:, 0:n * TOK], ACT.Relu).then_inc(logit_ok, 1)
            act.wait_ge(centered, 1)
            nc.scalar.activation(logit[:, :, :], logit[:, :, :], ACT.Exp).then_inc(exp_ok, 1)
            for n in range(0, FLIPS, 2):
                act.wait_ge(flip_ok, n + 1)
                m = min(4, TOK - 4 * n)
                nc.scalar.copy(prob_t[:, 4 * n:4 * n + m, :].rearrange("p a b -> p (a b)"),
                               bank[3 + n % 4][0:TOK, 0:128 * m]).then_inc(flip_a, 1)
            for hf in range(2):
                with act.Fori(0, 4) as c:
                    act.wait_ge(v_done, c + (4 * hf + 1 + LOAN))
                    nc.scalar.copy(v8[:, 0:8 * C], bank[7][0:TOK, :]).then_inc(v8_ok, 1)

        @block.vector
        def _(dve):
            dve.sem_inc(mix_out, LOAN)
            for n in range(4):
                dve.wait_ge(qk_done, n + 1)
                nc.vector.tensor_copy(k[:, n * 8:(n + 1) * 8, :].rearrange("p i t -> p (i t)"), bank[2 * n + 1][:, 0:8 * TOK]).then_inc(k_out, 1)
            dve.wait_ge(q_out, 4)
            dve.wait_ge(k_out, 4)
            with dve.Fori(0, HALF // 2) as i:
                for m in range(2):
                    dve.wait_ge(pair_done, 2 * i + LOAN)
                    one = bass.ds(2 * i + m, 1)
                    nc.vector.tensor_tensor(diff[m][:, :, :], q[:, one, :].rearrange("p o t -> p t o").broadcast_to([128, TOK, TOK]),
                                            k[:, one, :].broadcast_to([128, TOK, TOK]), ALU.subtract).then_inc(diff_ok, 1)
            dve.wait_ge(logit_ok, 3)
            chain = Chain(dve, own)
            chain.step(nc.vector.tensor_reduce(top[:, :], logit[:, :, :], AX.X, ALU.max))
            chain.wait()
            nc.vector.tensor_tensor(logit[:, :, :], logit[:, :, :], spread(top[:, :], 2, TOK), ALU.subtract).then_inc(centered, 1)
            dve.wait_ge(exp_ok, 1)
            chain.step(nc.vector.tensor_reduce(tot[:, :], logit[:, :, :], AX.X, ALU.add))
            chain.wait()
            chain.step(nc.vector.reciprocal(tot[:, :], tot[:, :]))
            chain.wait()
            nc.vector.tensor_tensor(logit[:, :, :], logit[:, :, :], spread(tot[:, :], 2, TOK), ALU.mult).then_inc(prob_ok, 1)
            for n in range(1, FLIPS, 2):
                dve.wait_ge(flip_ok, n + 1)
                m = min(4, TOK - 4 * n)
                nc.vector.tensor_copy(prob_t[:, 4 * n:4 * n + m, :].rearrange("p a b -> p (a b)"),
                                      bank[3 + n % 4][0:TOK, 0:128 * m]).then_inc(flip_d, 1)
            dve.wait_ge(zero_ok, 2)
            for hf in range(2):
                with dve.Fori(0, 4) as c:
                    dve.wait_ge(mix_done, c + 4 * hf + 1)
                    for h4 in range(2):
                        for g in range(2):
                            src = bank[h4][g * D:(g + 1) * D, 0:8 * TOK].rearrange("p (j t g) -> p j t g", j=4, g=2)
                            at = bass.ds((4 * hf * 8 + 4 * h4) * TOK + c * (8 * TOK), 4 * TOK)
                            nc.vector.tensor_copy(out_t[g * D:(g + 1) * D, at].rearrange("p (j t) -> p j t", j=4),
                                                  src[:, :, :, g]).then_inc(mix_out, 1)
            for n in range(3):
                m = min(8, GROUPS - 8 * n)
                dve.wait_ge(back_ok, n + 1)
                nc.vector.tensor_tensor(hid[:, 8 * n:8 * n + m, :].rearrange("p g c -> p (g c)"),
                                        hid[:, 8 * n:8 * n + m, :].rearrange("p g c -> p (g c)"),
                                        bank[3 + n][0:ROWS, 0:m * C], ALU.add)


def merge(nc, tag, pairs, spots):
    with Scope(nc, tag) as s:
        banks = [s.bank(f"m{i}") for i in range(-(-len(pairs) // 8))]
        bank_ok = s.sem("bank")
        block = s.block()

        @block.tensor
        def _(pe):
            for n, (left, right) in enumerate(pairs):
                last = nc.tensor.matmul(banks[n // 8][0:C, (n % 8) * C:(n % 8 + 1) * C], left, right, start=True, stop=True)
                if n % 8 == 7:
                    last.then_inc(bank_ok, 1)

        @block.vector
        def _(dve):
            for n, spot in enumerate(spots):
                dve.wait_ge(bank_ok, n + 1)
                nc.vector.tensor_copy(spot, banks[n][0:C, :])


def load(nc, tag, pairs):
    with Scope(nc, tag) as s:
        arrived = s.sem("arrived")
        block = s.block()

        @block.sync
        def _(sp):
            for dst, src in pairs:
                sp.dma_start(dst, src).then_inc(arrived, 16)
            sp.wait_ge(arrived, 16 * len(pairs))


def await_count(eng, sem, count):
    if not isinstance(count, int) or count > 0:
        eng.wait_ge(sem, count)


def skewed(eng, step, before, after):
    lo, hi = after, GROUPS - before
    lo += lo % 2
    hi -= hi % 2
    for i in range(-before, lo):
        step(i, i % 2)
    with eng.Fori(0, (hi - lo) // 2) as j:
        for k in range(2):
            step(2 * j + (lo + k), k)
    for i in range(hi, GROUPS + after):
        step(i, i % 2)


def live(i, shift=0):
    return not isinstance(i, int) or 0 <= i + shift < GROUPS


def head_attention(nc, tag, hid, xT, ident, mask, wq, wv, scale, kv=None):
    HALF = 4 * ROWS
    NH = HEADS
    with Scope(nc, tag) as s:
        def two(name, shape):
            return [s.sb(f"{name}{i}", shape) for i in range(2)]
        x_g = two("x_g", [C, ROWS])
        q_t = two("q_t", [C, NH * ROWS])
        v_g = two("v_g", [ROWS, NH * C])
        score = two("score", [ROWS, NH, ROWS])
        prob_t = two("prob_t", [ROWS, NH * ROWS])
        top, shift, tot = two("top", [ROWS, NH]), two("shift", [ROWS, NH]), two("tot", [ROWS, NH])
        if kv is not None:
            kv_g = two("kv_g", [128, NH, ROWS])
        q_bank, s_bank, t_bank = ([s.bank(f"{n}{j}") for j in range(2)] for n in ("q", "s", "t"))
        v_bank, o_bank = s.bank("v"), s.bank("o")
        x_ok, kv_ok, q_done, v_done, q_a, q_d, v_ok = (s.sem(n) for n in ("x", "kv", "q_done", "v_done", "q_a", "q_d", "v"))
        score_done, masked, top_ok, shift_ok, exp_ok, prob_ok = (
            s.sem(n) for n in ("score_done", "masked", "top", "shift", "exp", "prob"))
        recip_ok = s.sem("recip")
        flip_done, flip_a, flip_d, mix_done, hid_ok = (s.sem(n) for n in ("flip_done", "flip_a", "flip_d", "mix_done", "hid"))
        block = s.block()

        @block.gpsimd
        def _(pool):
            def step(g, k):
                if not live(g):
                    return
                await_count(pool, v_done, g - 1)
                nc.gpsimd.tensor_copy(x_g[k][:, :], xT[:, bass.ds(g * ROWS, ROWS)]).then_inc(x_ok, 1)
                if kv is not None:
                    nc.gpsimd.tensor_copy(
                        kv_g[k][:, :, :],
                        kv[:, bass.ds(g * ROWS + 128, NH * PADT)].rearrange("p (h t) -> p h t", h=NH)[:, :, 0:ROWS]).then_inc(kv_ok, 1)
            skewed(pool, step, 0, 2)

        @block.tensor
        def _(pe):
            def turn(g, k):
                await_count(pe, prob_ok, g + 1)
                await_count(pe, flip_a, g)
                await_count(pe, flip_d, g)
                for h in range(NH):
                    last = nc.tensor.transpose(t_bank[h // 4][0:ROWS, (h % 4) * ROWS:(h % 4 + 1) * ROWS],
                                               score[k][:, h, :], ident[0:ROWS, 0:ROWS])
                    if h % 4 == 3:
                        last.then_inc(flip_done, 1)

            def make_scores(g, k):
                if kv is not None:
                    await_count(pe, kv_ok, g + 1)
                await_count(pe, masked, 2 * g)
                await_count(pe, q_d, g + 1)
                await_count(pe, q_a, g + 1)
                for h in range(NH):
                    keys = x_g[k][:, :] if kv is None else kv_g[k][0:C, h, :]
                    last = nc.tensor.matmul(s_bank[h // 4][0:ROWS, (h % 4) * ROWS:(h % 4 + 1) * ROWS],
                                            q_t[k][:, h * ROWS:(h + 1) * ROWS], keys, start=True, stop=True)
                    if h % 4 == 3:
                        last.then_inc(score_done, 1)

            def make_queries(g, k):
                await_count(pe, q_a, g)
                await_count(pe, q_d, g)
                await_count(pe, x_ok, g + 1)
                for h in range(NH):
                    m = 2 if h == 0 else 1
                    last = nc.tensor.matmul(q_bank[h // 4][0:m * C, (h % 4) * ROWS:(h % 4 + 1) * ROWS],
                                            wq[:, h:h + m, :].rearrange("p h c -> p (h c)"), x_g[k][:, :],
                                            start=True, stop=True)
                    if h % 4 == 3:
                        last.then_inc(q_done, 1)

            def mix(g, k):
                await_count(pe, hid_ok, g)
                await_count(pe, v_ok, g + 1)
                await_count(pe, flip_a, g + 1)
                await_count(pe, flip_d, g + 1)
                for h in range(NH):
                    last = nc.tensor.matmul(o_bank[0:ROWS, 0:C], prob_t[k][:, h * ROWS:(h + 1) * ROWS],
                                            v_g[k][:, h * C:(h + 1) * C], start=h == 0, stop=h == NH - 1)
                last.then_inc(mix_done, 1)

            def make_values(g, k):
                await_count(pe, v_ok, g)
                if kv is None:
                    nc.tensor.matmul(v_bank[0:ROWS, :], x_g[k][:, :], wv[:, :, :].rearrange("p h c -> p (h c)"),
                                     start=True, stop=True).then_inc(v_done, 1)
                else:
                    for h in range(NH):
                        last = nc.tensor.matmul(v_bank[0:ROWS, h * C:(h + 1) * C], kv_g[k][:, h, :], wv[:, h, :],
                                                start=True, stop=True)
                    last.then_inc(v_done, 1)

            def step(i, k):
                if live(i, -2):
                    turn(i - 2, k)
                if live(i):
                    make_scores(i, k)
                if live(i, 1):
                    make_queries(i + 1, 1 - k)
                if live(i, -2):
                    mix(i - 2, k)
                if live(i):
                    make_values(i, k)
            skewed(pe, step, 1, 2)

        @block.scalar
        def _(act):
            def step(i, k):
                if live(i, -2):
                    act.wait_ge(flip_done, 2 * i - 3)
                    nc.scalar.copy(prob_t[k][:, 0:HALF], t_bank[0][0:ROWS, 0:HALF]).then_inc(flip_a, 1)
                if live(i, 1):
                    act.wait_ge(q_done, 2 * i + 3)
                    nc.scalar.copy(q_t[1 - k][:, 0:HALF], q_bank[0][0:C, 0:HALF]).then_inc(q_a, 1)
                if live(i):
                    act.wait_ge(shift_ok, i + 1)
                    for h in range(NH):
                        last = nc.scalar.activation(score[k][:, h, :], score[k][:, h, :], ACT.Exp, scale=scale,
                                                    bias=shift[k][:, h:h + 1], accum_out=tot[k][:, h:h + 1])
                    last.then_inc(exp_ok, 1)
                    act.wait_ge(v_done, i + 1)
                    nc.scalar.copy(v_g[k][:, :], v_bank[0:ROWS, :]).then_inc(v_ok, 1)
            skewed(act, step, 1, 2)

        @block.vector
        def _(dve):
            def normalize_rows(g, k):
                dve.wait_ge(exp_ok, g + 1)
                nc.vector.reciprocal(tot[k][:, :], tot[k][:, :]).then_inc(recip_ok, 1)
                dve.wait_ge(recip_ok, g + 1)
                nc.vector.tensor_tensor(score[k][:, :, :], score[k][:, :, :], spread(tot[k][:, :], 2, ROWS),
                                        ALU.mult).then_inc(prob_ok, 1)

            def mask_scores(g, k):
                for j in range(2):
                    dve.wait_ge(score_done, 2 * g + j + 1)
                    nc.vector.tensor_tensor(score[k][:, 4 * j:4 * j + 4, :],
                                            s_bank[j][0:ROWS, 0:HALF].rearrange("p (h t) -> p h t", h=4),
                                            spread(mask[:, :], 1, 4), ALU.add).then_inc(masked, 1)
                dve.wait_ge(masked, 2 * g + 2)
                nc.vector.tensor_reduce(top[k][:, :], score[k][:, :, :], AX.X, ALU.max).then_inc(top_ok, 1)
                dve.wait_ge(top_ok, g + 1)
                nc.vector.tensor_scalar(shift[k][:, :], top[k][:, :], -scale, None, ALU.mult).then_inc(shift_ok, 1)

            def step(i, k):
                if live(i, -1):
                    normalize_rows(i - 1, 1 - k)
                if live(i, -2):
                    dve.wait_ge(flip_done, 2 * i - 2)
                    nc.vector.tensor_copy(prob_t[k][:, HALF:2 * HALF], t_bank[1][0:ROWS, 0:HALF]).then_inc(flip_d, 1)
                if live(i):
                    mask_scores(i, k)
                if live(i, 1):
                    dve.wait_ge(q_done, 2 * i + 4)
                    nc.vector.tensor_copy(q_t[1 - k][:, HALF:2 * HALF], q_bank[1][0:C, 0:HALF]).then_inc(q_d, 1)
                if live(i, -2):
                    dve.wait_ge(mix_done, i - 1)
                    row = hid[:, bass.ds(i - 2, 1), :].rearrange("p g c -> p (g c)")
                    nc.vector.tensor_tensor(row, row, o_bank[0:ROWS, 0:C], ALU.add).then_inc(hid_ok, 1)
            skewed(dve, step, 1, 2)


def product_keys(nc, xT, ident, side_w, table, kv_t):
    Q = 4
    QN = ENT // Q
    SIDE = KEYS // Q
    TURNS = ENT // BANK
    PARTS = ((0, 16, 0, 2), (0, 2, 2, 16), (2, 5, 2, 5))
    CAND = sum((a1 - a0) * (b1 - b0) for a0, a1, b0, b1 in PARTS)
    PICKS = 13
    with Scope(nc, "pk") as s:
        x_st, w_st = s.sb("x_st", [C, 128]), s.sb("w_st", [C, 128])
        sim_sel, sim_sum = s.sb("sim_sel", [128, 128]), s.sb("sim_sum", [128, 128])
        total = [s.sb(f"total{q}", [128, SIDE, KEYS]) for q in range(Q)]
        weight = [s.sb(f"weight{q}", [128, QN]) for q in range(Q)]
        turned = [s.sb(f"turned{i}", [128, BANK]) for i in range(4)]
        tab = s.sb("tab", [128, CHUNKS, 128])
        best = [s.sb(f"best{p}", [128, TOPK]) for p in range(2)]
        rest = [s.sb(f"rest{p}", [128, KEYS]) for p in range(2)]
        cand, cand2, chosen = s.sb("cand", [128, CAND]), s.sb("cand2", [128, CAND]), s.sb("chosen", [128, TOPK])
        cut, shift = s.sb("cut", [128, 1]), s.sb("shift", [128, 1])
        zpart, zinv = s.sb("zpart", [128, Q]), s.sb("zinv", [128, 1])
        kv_sb = s.sb("kv_sb", [128, 128])
        expo = [s.ctx.enter_context(nc.psum_tensor(f"pk_expo{i}", [128, QN], F32)) for i in range(2)]
        turn = [s.bank(f"turn{i}") for i in range(2)]
        out, misc = s.bank("out"), s.bank("misc")
        zero_ok, staged, sims_done, sel_ok, sum_in = (s.sem(n) for n in ("zero", "staged", "sims_done", "sel", "sum_in"))
        pool_sum, dve_sum, exp_ok, masked, cut_ok = (s.sem(n) for n in ("pool_sum", "dve_sum", "exp", "masked", "cut"))
        turn_done, turned_ok, mul_done = s.sem("turn_done"), s.sem("turned"), s.sem("mul_done")
        pick, z_ok, zinv_ok, kv_ok, flip_done, flip_out = (s.sem(n) for n in ("pick", "z", "zinv", "kv", "flip_done", "flip_out"))
        tab_in = [s.sem(f"tab_in{q}") for q in range(Q)]
        ready, shift_ok = s.sem("ready"), s.sem("shift")
        block = s.block()
        TURNED0, MUL0, MASKED0, TURN0 = 1 + LOAN, 3 + LOAN, 3 + LOAN, 6 + LOAN

        def sum_quarter(eng, q):
            return eng.tensor_tensor(total[q][:, :, :], spread(sim_sum[:, 0:KEYS], 1, SIDE),
                                     spread(sim_sum[:, KEYS + q * SIDE:KEYS + (q + 1) * SIDE], 2, KEYS), ALU.add)

        @block.sync
        def _(sp):
            per = CHUNKS // Q
            for q in range(Q):
                sp.dma_start(tab[:, q * per:(q + 1) * per, :], table[0, :, q * per:(q + 1) * per, :]).then_inc(tab_in[q], 16)
            with sp.Fori(1, HEADS) as h:
                for q in range(Q):
                    sp.wait_ge(mul_done, h * (TURNS * TILES) + (MUL0 - TURNS + 2 * q + 2))
                    sp.dma_start(tab[:, q * per:(q + 1) * per, :],
                                 table[bass.ds(h, 1), :, q * per:(q + 1) * per, :].rearrange("h p c n -> (h p) c n")).then_inc(tab_in[q], 16)

        @block.gpsimd
        def _(pool):
            nc.gpsimd.memset(kv_sb[:, :], 0.0).then_inc(zero_ok, 1)
            pool.sem_inc(pool_sum, LOAN)
            nc.gpsimd.tensor_copy(w_st[:, :], side_w[:, 0, :]).then_inc(ready, 1)
            nc.gpsimd.tensor_copy(x_st[:, :], xT[:, 0:128]).then_inc(staged, 1)

            def unit(u, at, head):
                pool.wait_ge(pool_sum, u * (Q - 1) + LOAN)
                pool.wait_ge(dve_sum, u + LOAN)
                pool.wait_ge(sel_ok, u + 1)
                if head is not None:
                    nc.gpsimd.tensor_copy(w_st[:, :], side_w[:, bass.ds(head, 1), :].rearrange("p h n -> p (h n)")).then_inc(ready, 1)
                nc.gpsimd.tensor_copy(x_st[:, :], xT[:, at]).then_inc(staged, 1)
                nc.gpsimd.tensor_copy(sim_sum[:, :], sim_sel[:, :]).then_inc(sum_in, 1)
                pool.wait_ge(sum_in, u + 1)
                for q in range(Q - 1):
                    pool.wait_ge(masked, u * Q + q + MASKED0 - 3)
                    sum_quarter(nc.gpsimd, q).then_inc(pool_sum, 1)

            with pool.Fori(0, HEADS) as h:
                with pool.Fori(0, TILES - 1) as t:
                    unit(h * TILES + t, bass.ds(t * 128 + 128, 128), None)
                unit(h * TILES + (TILES - 1), slice(0, 128), h + 1)

        @block.tensor
        def _(pe):
            pe.wait_ge(zero_ok, 1)
            pe.sem_inc(mul_done, MUL0)
            pe.sem_inc(turn_done, TURN0)
            pe.wait_ge(ready, 1)
            pe.wait_ge(staged, 1)
            nc.tensor.matmul(misc[:, 0:128], x_st[:, :], w_st[:, :], start=True, stop=True).then_inc(sims_done, 1)

            def turn_bank(u, k):
                if k % 2 == 0:
                    pe.wait_ge(masked, u * Q + (k // 2 + 1 + MASKED0))
                pe.wait_ge(turned_ok, u * TURNS + (k - 1 + TURNED0))
                for j in range(4):
                    at = ((4 * k + j) % (QN // 128)) * 128
                    last = nc.tensor.transpose(turn[k % 2][:, j * 128:(j + 1) * 128],
                                               weight[k // 2][:, at:at + 128], ident[:, :])
                last.then_inc(turn_done, 1)

            def multiply(u, h, k):
                if k == 0:
                    pe.wait_ge(kv_ok, u + LOAN)
                if k % 2 == 0:
                    pe.wait_ge(tab_in[k // 2], h * 16 + 16)
                pe.wait_ge(turned_ok, u * TURNS + (k + 1 + TURNED0))
                for j in range(4):
                    last = nc.tensor.matmul(out[:, 0:128], turned[k % 4][:, j * 128:(j + 1) * 128], tab[:, 4 * k + j, :],
                                            start=k == 0 and j == 0, stop=k == TURNS - 1 and j == 3)
                last.then_inc(mul_done, 1)

            def flip(u, sims=2):
                pe.wait_ge(kv_ok, u + LOAN)
                pe.wait_ge(sel_ok, u + sims)
                nc.tensor.transpose(misc[:, 128:256], kv_sb[:, :], ident[:, :]).then_inc(flip_done, 1)

            with pe.Fori(0, HEADS) as h:
                with pe.Fori(0, TILES) as t:
                    u = h * TILES + t
                    turn_bank(u, 0)
                    for k in range(TURNS):
                        if k + 1 < TURNS:
                            turn_bank(u, k + 1)
                        if k == 0:
                            pe.wait_ge(flip_out, u + LOAN)
                            pe.wait_ge(staged, u + 2)
                            pe.wait_ge(ready, h + 1)
                            nc.tensor.matmul(misc[:, 0:128], x_st[:, :], w_st[:, :], start=True, stop=True).then_inc(sims_done, 1)
                        multiply(u, h, k)
                        if k == 1:
                            flip(u)
            flip(UNITS, sims=1)

        @block.scalar
        def _(act):
            act.sem_inc(kv_ok, LOAN)
            act.sem_inc(flip_out, LOAN)
            act.sem_inc(turned_ok, TURNED0)

            def exp(u, q):
                if q < Q - 1:
                    act.wait_ge(pool_sum, u * (Q - 1) + (q + 1 + LOAN))
                else:
                    act.wait_ge(dve_sum, u + 1 + LOAN)
                act.wait_ge(shift_ok, u + 1)
                act.wait_ge(masked, u * Q + (q - 1 + MASKED0))
                nc.scalar.activation(expo[q % 2][:, :], total[q][:, :, :].rearrange("p j i -> p (j i)"), ACT.Exp,
                                     bias=shift[:, :]).then_inc(exp_ok, 1)

            def copy_turned(u, k):
                act.wait_ge(turn_done, u * TURNS + (k + 1 + TURN0))
                act.wait_ge(mul_done, u * TURNS + (k - 3 + MUL0))
                nc.scalar.copy(turned[k % 4][:, :], turn[k % 2][:, :]).then_inc(turned_ok, 1)

            def flipped(u):
                act.wait_ge(flip_done, u + 1)
                nc.scalar.copy(kv_t[:, bass.ds(u * 128, 128)], misc[:, 128:256]).then_inc(flip_out, 1)

            def unit(u, last):
                copy_turned(u, 0)
                copy_turned(u, 1)
                exp(u, 2)
                copy_turned(u, 2)
                flipped(u)
                copy_turned(u, 3)
                exp(u, 3)
                copy_turned(u, 4)
                copy_turned(u, 5)
                if not last:
                    exp(u + 1, 0)
                copy_turned(u, 6)
                if not last:
                    exp(u + 1, 1)
                copy_turned(u, 7)
                act.wait_ge(mul_done, u * TURNS + (TURNS + MUL0))
                act.wait_ge(zinv_ok, u + 1)
                act.wait_ge(flip_done, u + 1)
                nc.scalar.activation(kv_sb[:, :], out[:, 0:128], ACT.Copy, scale=zinv[:, 0:1]).then_inc(kv_ok, 1)

            exp(0, 0)
            exp(0, 1)
            with act.Fori(0, UNITS - 1) as u:
                unit(u, False)
            unit(UNITS - 1, True)
            flipped(UNITS)

        @block.vector
        def _(dve):
            dve.sem_inc(masked, MASKED0)
            dve.sem_inc(dve_sum, LOAN)

            own = Chain(dve, pick)
            side = [sim_sel[:, p * KEYS:(p + 1) * KEYS] for p in range(2)]

            def take_scores(v):
                dve.sem_clear(pick)
                own.n = 0
                dve.wait_ge(sum_in, v)
                dve.wait_ge(sims_done, v + 1)
                own.step(nc.vector.tensor_copy(sim_sel[:, :], misc[:, 0:128]))
                own.wait()
                dve.sem_inc(sel_ok, 1)

            def best_of_sides():
                for p in range(2):
                    own.step(nc.vector.max(best[p][:, 0:8], side[p]))
                own.wait()
                for p in range(2):
                    own.step(nc.vector.match_replace(rest[p][:, :], best[p][:, 0:8], side[p], NEG))
                own.wait()
                for p in range(2):
                    own.step(nc.vector.max(best[p][:, 8:16], rest[p][:, :]))

            def best_of_sums():
                own.wait()
                at = 0
                for a0, a1, b0, b1 in PARTS:
                    n = (a1 - a0) * (b1 - b0)
                    own.step(nc.vector.tensor_tensor(
                        cand[:, at:at + n].rearrange("p (b a) -> p b a", a=a1 - a0),
                        spread(best[0][:, a0:a1], 1, b1 - b0), spread(best[1][:, b0:b1], 2, a1 - a0), ALU.add))
                    at += n
                own.wait()
                own.step(nc.vector.max(chosen[:, 0:8], cand[:, :]))
                own.wait()
                own.step(nc.vector.match_replace(cand2[:, :], chosen[:, 0:8], cand[:, :], NEG))
                own.wait()
                own.step(nc.vector.max(chosen[:, 8:16], cand2[:, :]))
                assert own.n == PICKS

            def set_shift():
                dve.wait_ge(pick, PICKS)
                nc.vector.tensor_scalar(shift[:, :], chosen[:, 0:1], -1.0, None, ALU.mult).then_inc(shift_ok, 1)

            def set_cut():
                dve.wait_ge(pick, PICKS)
                nc.vector.tensor_copy(cut[:, :], chosen[:, 15:16]).then_inc(cut_ok, 1)

            def mask(u, q):
                dve.wait_ge(exp_ok, u * Q + (q + 1))
                dve.wait_ge(cut_ok, u + 1)
                dve.wait_ge(turn_done, u * TURNS + (2 * q - 6 + TURN0))
                nc.vector.scalar_tensor_tensor(weight[q][:, :], total[q][:, :, :].rearrange("p j i -> p (j i)"),
                                               cut[:, 0:1], expo[q % 2][:, :], ALU.is_ge, ALU.mult,
                                               accum_out=zpart[:, q:q + 1]).then_inc(masked, 1)

            dve.wait_ge(sims_done, 1)
            own.step(nc.vector.tensor_copy(sim_sel[:, :], misc[:, 0:128]))
            own.wait()
            dve.sem_inc(sel_ok, 1)
            best_of_sides()
            best_of_sums()
            set_shift()
            set_cut()
            with dve.Fori(0, UNITS) as u:
                mask(u, 0)
                dve.wait_ge(sum_in, u + 1)
                sum_quarter(nc.vector, 3).then_inc(dve_sum, 1)
                mask(u, 1)
                take_scores(u + 1)
                best_of_sides()
                mask(u, 2)
                best_of_sums()
                dve.wait_ge(exp_ok, u * Q + Q)
                set_shift()
                mask(u, 3)
                dve.wait_ge(masked, u * Q + (Q + MASKED0))
                set_cut()
                dve.wait_ge(kv_ok, u + LOAN)
                nc.vector.tensor_reduce(zinv[:, :], zpart[:, :], AX.X, ALU.add).then_inc(z_ok, 1)
                dve.wait_ge(z_ok, u + 1)
                nc.vector.reciprocal(zinv[:, :], zinv[:, :]).then_inc(zinv_ok, 1)


def clear(nc, tag, spots):
    with Scope(nc, tag) as s:
        block = s.block()

        @block.gpsimd
        def _(pool):
            for spot in spots:
                nc.gpsimd.memset(spot, 0.0)


def rotary_attention(nc, x, xT, ident, mask, wqkvT, woT, rope):
    NQ, NKV, HD = 4, 2, 16
    QK = (NQ + NKV) * HD
    with Scope(nc, "gqa") as s:
        def two(name, shape):
            return [s.sb(f"{name}{i}", shape) for i in range(2)]
        w_in, w_o = s.sb("w_in", [C, 128]), s.sb("w_o", [C, C])
        cos_sin = s.sb("cos_sin", [ROWS, 2, HD])
        x_g = two("x_g", [C, ROWS])
        part, turn = two("part", [ROWS, QK]), two("turn", [ROWS, QK])
        v_g = two("v_g", [ROWS, NKV * HD])
        q_t, k_t = two("q_t", [HD, NQ * ROWS]), two("k_t", [HD, NKV * ROWS])
        score, prob_t = two("score", [ROWS, NQ, ROWS]), two("prob_t", [ROWS, NQ * ROWS])
        top, tot = two("top", [ROWS, NQ]), two("tot", [ROWS, NQ])
        y, y_t = two("y", [ROWS, 128]), two("y_t", [C, ROWS])
        pad_ok = s.sem("pad")
        bank = [[s.bank(f"b{k}{n}") for n in range(3)] for k in range(2)]
        arrived, x_ok, qkv_done, part_ok, rope_ok, v_ok = (s.sem(n) for n in ("arrived", "x", "qkv", "part", "rope", "v"))
        flip_q, flip_k, q_ok, k_ok, score_done, masked = (s.sem(n) for n in ("flip_q", "flip_k", "q", "k", "score", "masked"))
        top_ok, centered, exp_ok, sum_ok, recip_ok = (s.sem(n) for n in ("top", "sub", "exp", "sum", "recip"))
        flip_p, p_ok, mix_done, y_ok, flip_y, yt_ok, out_done, x_new = (
            s.sem(n) for n in ("flip_p", "p", "mix", "y", "flip_y", "yt", "out", "x_new"))
        block = s.block()

        @block.sync
        def _(sp):
            for dst, src in ((w_in[:, :], wqkvT), (w_o[:, :], woT), (cos_sin[:, :, :], rope)):
                sp.dma_start(dst, src).then_inc(arrived, 16)

        @block.gpsimd
        def _(pool):
            for k in range(2):
                nc.gpsimd.memset(y[k][:, :], 0.0).then_inc(pad_ok, 1)
            with pool.Fori(0, GROUPS // 2) as i:
                for k in range(2):
                    pool.wait_ge(qkv_done, 2 * i + LOAN)
                    nc.gpsimd.tensor_copy(x_g[k][:, :], xT[:, bass.ds((2 * i + k) * ROWS, ROWS)]).then_inc(x_ok, 1)

        @block.tensor
        def _(pe):
            pe.sem_inc(qkv_done, LOAN)
            pe.wait_ge(arrived, 48)
            pe.wait_ge(pad_ok, 2)
            with pe.Fori(0, GROUPS // 2) as i:
                def turn_of(k):
                    return 2 * i + k + 1
                for k in range(2):
                    pe.wait_ge(x_ok, turn_of(k))
                    pe.wait_ge(x_new, 2 * i + LOAN)
                    nc.tensor.matmul(bank[k][0][0:ROWS, 0:128], x_g[k][:, :], w_in[:, :], start=True, stop=True).then_inc(qkv_done, 1)
                for k in range(2):
                    pe.wait_ge(rope_ok, turn_of(k))
                    for h in range(NQ):
                        last = nc.tensor.transpose(bank[k][1][0:HD, h * ROWS:(h + 1) * ROWS],
                                                   part[k][:, h * HD:(h + 1) * HD], ident[0:ROWS, 0:ROWS])
                    last.then_inc(flip_q, 1)
                    for h in range(NKV):
                        last = nc.tensor.transpose(bank[k][2][0:HD, h * ROWS:(h + 1) * ROWS],
                                                   part[k][:, (NQ + h) * HD:(NQ + h + 1) * HD], ident[0:ROWS, 0:ROWS])
                    last.then_inc(flip_k, 1)
                for k in range(2):
                    pe.wait_ge(q_ok, turn_of(k))
                    pe.wait_ge(k_ok, turn_of(k))
                    for h in range(NQ):
                        last = nc.tensor.matmul(bank[k][1][0:ROWS, h * ROWS:(h + 1) * ROWS], q_t[k][:, h * ROWS:(h + 1) * ROWS],
                                                k_t[k][:, (h // 2) * ROWS:(h // 2 + 1) * ROWS], start=True, stop=True)
                    last.then_inc(score_done, 1)
                for k in range(2):
                    pe.wait_ge(exp_ok, turn_of(k))
                    for h in range(NQ):
                        last = nc.tensor.transpose(bank[k][1][0:ROWS, h * ROWS:(h + 1) * ROWS], score[k][:, h, :],
                                                   ident[0:ROWS, 0:ROWS])
                    last.then_inc(flip_p, 1)
                for k in range(2):
                    pe.wait_ge(p_ok, turn_of(k))
                    for h in range(NQ):
                        last = nc.tensor.matmul(bank[k][0][0:ROWS, h * HD:(h + 1) * HD], prob_t[k][:, h * ROWS:(h + 1) * ROWS],
                                                v_g[k][:, (h // 2) * HD:(h // 2 + 1) * HD], start=True, stop=True)
                    last.then_inc(mix_done, 1)
                for k in range(2):
                    pe.wait_ge(y_ok, turn_of(k))
                    nc.tensor.transpose(bank[k][2][:, 0:ROWS], y[k][:, :], ident[0:ROWS, 0:ROWS]).then_inc(flip_y, 1)
                for k in range(2):
                    pe.wait_ge(yt_ok, turn_of(k))
                    nc.tensor.matmul(bank[k][0][0:ROWS, 0:C], y_t[k][:, :], w_o[:, :], start=True, stop=True).then_inc(out_done, 1)

        @block.scalar
        def _(act):
            with act.Fori(0, GROUPS // 2) as i:
                for k in range(2):
                    act.wait_ge(flip_q, 2 * i + k + 1)
                    nc.scalar.copy(q_t[k][:, :], bank[k][1][0:HD, 0:NQ * ROWS]).then_inc(q_ok, 1)
                for k in range(2):
                    act.wait_ge(centered, 2 * i + k + 1)
                    nc.scalar.activation(score[k][:, :, :], score[k][:, :, :], ACT.Exp, scale=HD ** -0.5).then_inc(exp_ok, 1)
                for k in range(2):
                    act.wait_ge(flip_p, 2 * i + k + 1)
                    nc.scalar.copy(prob_t[k][:, :], bank[k][1][0:ROWS, 0:NQ * ROWS]).then_inc(p_ok, 1)
                for k in range(2):
                    act.wait_ge(flip_y, 2 * i + k + 1)
                    nc.scalar.copy(y_t[k][:, :], bank[k][2][0:C, 0:ROWS]).then_inc(yt_ok, 1)

        @block.vector
        def _(dve):
            dve.sem_inc(x_new, LOAN)
            dve.wait_ge(arrived, 48)
            dve.wait_ge(pad_ok, 2)
            with dve.Fori(0, GROUPS // 2) as i:
                for k in range(2):
                    dve.wait_ge(qkv_done, 2 * i + (k + 1 + LOAN))
                    b = bank[k][0]
                    halves = [a[0:ROWS, 0:QK].rearrange("p (h s d) -> p h s d", s=2, d=HD // 2) for a in (b, turn[k])]
                    nc.vector.tensor_tensor(part[k][:, :].rearrange("p (h d) -> p h d", d=HD), b[0:ROWS, 0:QK].rearrange("p (h d) -> p h d", d=HD),
                                            spread(cos_sin[:, 0, :], 1, NQ + NKV), ALU.mult).then_inc(part_ok, 1)
                    for d in range(2):
                        nc.vector.tensor_tensor(halves[1][:, :, d, :], halves[0][:, :, 1 - d, :],
                                                spread(cos_sin[:, 1, d * 8:d * 8 + 8], 1, NQ + NKV), ALU.mult).then_inc(part_ok, 1)
                    nc.vector.tensor_copy(v_g[k][:, :], b[0:ROWS, QK:128]).then_inc(v_ok, 1)
                for k in range(2):
                    dve.wait_ge(part_ok, 6 * i + 3 * k + 3)
                    dve.wait_ge(v_ok, 2 * i + k + 1)
                    nc.vector.tensor_tensor(part[k][:, :], part[k][:, :], turn[k][:, :], ALU.add).then_inc(rope_ok, 1)
                for k in range(2):
                    dve.wait_ge(flip_k, 2 * i + k + 1)
                    nc.vector.tensor_copy(k_t[k][:, :], bank[k][2][0:HD, 0:NKV * ROWS]).then_inc(k_ok, 1)
                for k in range(2):
                    dve.wait_ge(score_done, 2 * i + k + 1)
                    nc.vector.tensor_tensor(score[k][:, :, :], bank[k][1][0:ROWS, 0:NQ * ROWS].rearrange("p (h t) -> p h t", h=NQ),
                                            spread(mask[:, :], 1, NQ), ALU.add).then_inc(masked, 1)
                for k in range(2):
                    dve.wait_ge(masked, 2 * i + k + 1)
                    nc.vector.tensor_reduce(top[k][:, :], score[k][:, :, :], AX.X, ALU.max).then_inc(top_ok, 1)
                for k in range(2):
                    dve.wait_ge(top_ok, 2 * i + k + 1)
                    nc.vector.tensor_tensor(score[k][:, :, :], score[k][:, :, :], spread(top[k][:, :], 2, ROWS),
                                            ALU.subtract).then_inc(centered, 1)
                for k in range(2):
                    dve.wait_ge(exp_ok, 2 * i + k + 1)
                    nc.vector.tensor_reduce(tot[k][:, :], score[k][:, :, :], AX.X, ALU.add).then_inc(sum_ok, 1)
                    dve.wait_ge(sum_ok, 2 * i + k + 1)
                    nc.vector.reciprocal(tot[k][:, :], tot[k][:, :]).then_inc(recip_ok, 1)
                for k in range(2):
                    dve.wait_ge(recip_ok, 2 * i + k + 1)
                    dve.wait_ge(mix_done, 2 * i + k + 1)
                    nc.vector.tensor_tensor(y[k][:, 0:C].rearrange("p (h d) -> p h d", h=NQ),
                                            bank[k][0][0:ROWS, 0:C].rearrange("p (h d) -> p h d", h=NQ),
                                            spread(tot[k][:, :], 2, HD), ALU.mult).then_inc(y_ok, 1)
                for k in range(2):
                    dve.wait_ge(out_done, 2 * i + k + 1)
                    row = x[:, bass.ds(2 * i + k, 1), :].rearrange("p g c -> p (g c)")
                    nc.vector.tensor_tensor(row, row, bank[k][0][0:ROWS, 0:C], ALU.add).then_inc(x_new, 1)


def gates(nc, xT, routerT, gate):
    with Scope(nc, "gate") as s:
        w = s.sb("w", [C, NEXP])
        prob, best = s.sb("prob", [ROWS, GROUPS, NEXP]), s.sb("best", [ROWS, GROUPS, 8])
        red = s.sb("red", [ROWS, GROUPS])
        logits = s.bank("logits")
        w_in, logits_done, centered, exp_ok, own_sem = (s.sem(n) for n in ("w_in", "logits", "sub", "exp", "own"))
        block = s.block()

        @block.sync
        def _(sp):
            sp.dma_start(w[:, :], routerT).then_inc(w_in, 16)

        @block.tensor
        def _(pe):
            pe.wait_ge(w_in, 16)
            for g in range(GROUPS):
                last = nc.tensor.matmul(logits[0:ROWS, g * NEXP:(g + 1) * NEXP], xT[:, g * ROWS:(g + 1) * ROWS], w[:, :],
                                        start=True, stop=True)
            last.then_inc(logits_done, 1)

        @block.scalar
        def _(act):
            act.wait_ge(centered, 1)
            nc.scalar.activation(prob[:, :, :], prob[:, :, :], ACT.Exp).then_inc(exp_ok, 1)

        @block.vector
        def _(dve):
            own = Chain(dve, own_sem)

            def then(ins):
                own.step(ins)
                own.wait()

            dve.wait_ge(logits_done, 1)
            then(nc.vector.tensor_reduce(red[:, :], logits[0:ROWS, 0:GROUPS * NEXP].rearrange("p (g e) -> p g e", g=GROUPS), AX.X, ALU.max))
            nc.vector.tensor_tensor(prob[:, :, :], logits[0:ROWS, 0:GROUPS * NEXP].rearrange("p (g e) -> p g e", g=GROUPS),
                                    spread(red[:, :], 2, NEXP), ALU.subtract).then_inc(centered, 1)
            dve.wait_ge(exp_ok, 1)
            then(nc.vector.tensor_reduce(red[:, :], prob[:, :, :], AX.X, ALU.add))
            then(nc.vector.reciprocal(red[:, :], red[:, :]))
            then(nc.vector.tensor_tensor(prob[:, :, :], prob[:, :, :], spread(red[:, :], 2, NEXP), ALU.mult))
            for g in range(GROUPS):
                own.step(nc.vector.max(best[:, g, :], prob[:, g, :]))
            own.wait()
            then(nc.vector.tensor_tensor(red[:, :], best[:, :, 0], best[:, :, 1], ALU.add))
            then(nc.vector.tensor_scalar(red[:, :], red[:, :], 1e-9, None, ALU.add))
            then(nc.vector.reciprocal(red[:, :], red[:, :]))
            then(nc.vector.tensor_tensor(gate[:, :, :], prob[:, :, :], best[:, :, 1:2].broadcast_to([ROWS, GROUPS, NEXP]), ALU.is_ge))
            then(nc.vector.tensor_tensor(gate[:, :, :], gate[:, :, :], prob[:, :, :], ALU.mult))
            nc.vector.tensor_tensor(gate[:, :, :], gate[:, :, :], spread(red[:, :], 2, NEXP), ALU.mult)


def experts(nc, hid, x, xT, gate, w1T, w3T, w2T):
    PAIR = 2 * ROWS
    HALVES = 2 * NEXP
    with Scope(nc, "moe") as s:
        w1, w3 = s.sb("w1", [C, NEXP * HID]), s.sb("w3", [C, NEXP * HID])
        w2 = s.sb("w2", [HH, HALVES, C])
        x_p = s.sb("x_p", [C, PAIR])
        silu = [s.sb(f"silu{i}", [HH, PAIR]) for i in range(3)]
        hidden = s.sb("hidden", [HH, HALVES, PAIR])
        gated = [s.sb(f"gated{i}", [ROWS, NEXP, C]) for i in range(2)]
        mixed = [s.sb(f"mixed{i}", [ROWS, C]) for i in range(2)]
        up = [s.bank(f"up{i}") for i in range(3)]
        down = [s.bank(f"down{i}") for i in range(2)]
        arrived, x_ok, up_done, silu_ok, hidden_ok = (s.sem(n) for n in ("arrived", "x", "up", "silu", "hidden"))
        down_done, gated_ok, mixed_ok, hid_x = s.sem("down"), s.sem("gated"), s.sem("mixed"), s.sem("hid_x")
        block = s.block()
        HIDDEN0 = 2 + LOAN

        @block.sync
        def _(sp):
            for dst, src in ((w1[:, :], w1T), (w3[:, :], w3T), (w2[:, :, :], w2T)):
                sp.dma_start(dst, src).then_inc(arrived, 16)

        @block.gpsimd
        def _(pool):
            with pool.Fori(0, GROUPS // 2) as i:
                pool.wait_ge(up_done, HALVES * i + LOAN)
                nc.gpsimd.tensor_copy(x_p[:, :], xT[:, bass.ds(i * PAIR, PAIR)]).then_inc(x_ok, 1)

        @block.tensor
        def _(pe):
            pe.sem_inc(up_done, LOAN)
            pe.sem_inc(down_done, LOAN)
            pe.wait_ge(arrived, 48)
            with pe.Fori(0, GROUPS // 2) as i:
                pe.wait_ge(x_ok, i + 1)
                for c in range(HALVES):
                    pe.wait_ge(hidden_ok, HALVES * i + (c - 2 + HIDDEN0))
                    nc.tensor.matmul(up[c % 3][0:HH, 0:PAIR], w1[:, c * HH:(c + 1) * HH], x_p[:, :], start=True, stop=True)
                    nc.tensor.matmul(up[c % 3][0:HH, 256:256 + PAIR], w3[:, c * HH:(c + 1) * HH], x_p[:, :],
                                     start=True, stop=True).then_inc(up_done, 1)
                pe.wait_ge(hidden_ok, HALVES * i + (HALVES + HIDDEN0))
                pe.wait_ge(gated_ok, 2 * i + LOAN)
                for k in range(2):
                    for c in range(HALVES):
                        last = nc.tensor.matmul(down[k][0:ROWS, (c // 2) * C:(c // 2 + 1) * C], hidden[:, c, k * ROWS:(k + 1) * ROWS],
                                                w2[:, c, :], start=c % 2 == 0, stop=c % 2 == 1)
                    last.then_inc(down_done, 1)

        @block.scalar
        def _(act):
            with act.Fori(0, GROUPS // 2) as i:
                for c in range(HALVES):
                    act.wait_ge(up_done, HALVES * i + (c + 1 + LOAN))
                    act.wait_ge(hidden_ok, HALVES * i + (c - 2 + HIDDEN0))
                    nc.scalar.activation(silu[c % 3][:, :], up[c % 3][0:HH, 0:PAIR], ACT.Silu).then_inc(silu_ok, 1)

        @block.vector
        def _(dve):
            dve.sem_inc(gated_ok, LOAN)
            dve.sem_inc(hidden_ok, HIDDEN0)
            nc.vector.tensor_tensor(hid[:, :, :], hid[:, :, :], x[:, :, :], ALU.add).then_inc(hid_x, 1)
            dve.wait_ge(hid_x, 1)
            with dve.Fori(0, GROUPS // 2) as i:
                dve.wait_ge(down_done, 2 * i + LOAN)
                for c in range(HALVES):
                    dve.wait_ge(silu_ok, HALVES * i + (c + 1))
                    nc.vector.tensor_tensor(hidden[:, c, :], silu[c % 3][:, :], up[c % 3][0:HH, 256:256 + PAIR],
                                            ALU.mult).then_inc(hidden_ok, 1)
                for k in range(2):
                    dve.wait_ge(down_done, 2 * i + (k + 1 + LOAN))
                    one = bass.ds(2 * i + k, 1)
                    nc.vector.tensor_tensor(gated[k][:, :, :], down[k][0:ROWS, :].rearrange("p (e c) -> p e c", e=NEXP),
                                            gate[:, one, :].rearrange("p o e -> p e o").broadcast_to([ROWS, NEXP, C]), ALU.mult).then_inc(gated_ok, 1)
                for k in range(2):
                    dve.wait_ge(gated_ok, 2 * i + (k + 1 + LOAN))
                    nc.vector.tensor_reduce(mixed[k][:, :], gated[k][:, :, :].rearrange("p e c -> p c e"), AX.X, ALU.add).then_inc(mixed_ok, 1)
                for k in range(2):
                    dve.wait_ge(mixed_ok, 2 * i + k + 1)
                    row = hid[:, bass.ds(2 * i + k, 1), :].rearrange("p g c -> p (g c)")
                    nc.vector.tensor_tensor(row, row, mixed[k][:, :], ALU.add)


def vision_tower(nc, x_img, cls_tok, tok_w, tok_b, a_wq, a_wk, a_wv, a_mlp, a_b, unmix,
                 ln1, ln2, wqkv, wo, router, w1, w2, w3, rope,
                 key_m, query_m, value_in, value_out, pk_w, pk_k, mem_wq, table, mem_wo, ident_in, mask_in, out):
    Scope.spent = []
    with Scope(nc, "all") as s:
        hid = s.sb("hid", [ROWS, GROUPS, C])
        x = s.sb("x", [ROWS, GROUPS, C])
        xT = s.sb("xT", [C, COLS])
        ident, mask = s.sb("ident", [128, 128]), s.sb("mask", [ROWS, ROWS])

        load(nc, "consts", [(ident[:, :], ident_in), (mask[:, :], mask_in)])
        embed(nc, hid, x_img, tok_w, cls_tok, tok_b)
        normalize(nc, "ln_a", hid, x, xT, ident, True, 1e-5)
        relu_attention(nc, hid, xT, ident, a_wq, a_wk, a_wv, a_mlp, a_b, unmix)
        normalize(nc, "ln_b", hid, x, xT, ident, True, 1e-5)
        with Scope(nc, "first") as f:
            scaled = f.sb("scaled", [ROWS, GROUPS, C])
            gate = f.sb("gate", [ROWS, GROUPS, NEXP])
            normalize(nc, "rms_a", x, scaled, xT, ident, False, 1e-6, ln1)
            rotary_attention(nc, x, xT, ident, mask, wqkv, wo, rope)
            normalize(nc, "rms_b", x, scaled, xT, ident, False, 1e-6, ln2)
            gates(nc, xT, router, gate)
            experts(nc, hid, x, xT, gate, w1, w3, w2)

        normalize(nc, "ln_c", hid, x, xT, ident, True, 1e-5)
        with Scope(nc, "second") as f:
            raw = [f.sb(f"raw{n}", [C, HEADS, C]) for n in range(4)]
            score_w, value_w = f.sb("score_w", [C, HEADS, C]), f.sb("value_w", [C, HEADS, C])
            load(nc, "raw", [(r[:, :, :], a) for r, a in zip(raw, (key_m, query_m, value_in, value_out))])
            merge(nc, "merge", [(raw[2 * m][:, h, :], raw[2 * m + 1][:, h, :]) for m in range(2) for h in range(HEADS)],
                  [w[:, :, :].rearrange("p h c -> p (h c)") for w in (score_w, value_w)])
            head_attention(nc, "mha", hid, xT, ident, mask, score_w, value_w, 1.0)

        normalize(nc, "ln_d", hid, x, xT, ident, True, 1e-5)
        with Scope(nc, "third") as f:
            kv_t = f.sb("kv_t", [128, KVT])
            with Scope(nc, "keys") as g:
                side_w = g.sb("side_w", [C, HEADS + 1, 128])
                a, b = g.sb("a", [32, 2 * HEADS, C]), g.sb("b", [32, 2 * HEADS, C])
                load(nc, "pk_in", [(a[:, :, :], pk_w), (b[:, :, :], pk_k)])
                clear(nc, "clear", [side_w[:, HEADS, :], kv_t[:, 128 + HEADS * PADT:]])
                merge(nc, "merge2", [(a[:, n, :], b[:, n, :]) for n in range(2 * HEADS)],
                      [side_w[:, 4 * m:4 * m + 4, :].rearrange("p h c -> p (h c)") for m in range(2)])
                product_keys(nc, xT, ident, side_w, table, kv_t)
            wq, wv = f.sb("wq", [C, HEADS, C]), f.sb("wv", [128, HEADS, C])
            clear(nc, "clear2", [wv[0:C, :, :]])
            load(nc, "wo", [(wq[:, :, :], mem_wq), (wv[C:128, :, :], mem_wo)])
            head_attention(nc, "mem", hid, xT, ident, mask, wq, wv, C ** -0.5, kv_t)
        load(nc, "store", [(out, hid[:, :, :])])


def _constants():
    mask = np.full((ROWS, ROWS), -1e30, np.float32)
    for m in range(PER):
        for i in range(TOK):
            mask[m * TOK + i, m * TOK:m * TOK + i + 1] = 0
    unmix = np.zeros((C, C), np.float32)
    for g in range(2):
        for d in range(32):
            unmix[g * 32 + d, d * 2 + g] = 1
    hd = 16
    inv = 1.0 / 10000.0 ** (np.arange(0, hd, 2, dtype=np.float32) / hd)
    angle = np.outer(np.arange(TOK, dtype=np.float32), inv)
    sin, cos = np.sin(angle), np.cos(angle)
    table = np.stack([np.concatenate([cos, cos], 1), np.concatenate([-sin, sin], 1)], 1)
    return {"unmix": unmix, "rope": np.tile(table, (PER, 1, 1)).astype(np.float32),
            "ident_in": np.eye(128, dtype=np.float32), "mask_in": mask}


def kernel(x, cls_tok, L0_tok_W, L0_tok_b, L0_attn_Wq, L0_attn_Wk, L0_attn_Wv, L0_attn_w_mlp, L0_attn_b_mlp,
           L0_ffn_ln1_w, L0_ffn_ln2_w, L0_ffn_wq, L0_ffn_wk, L0_ffn_wv, L0_ffn_wo, L0_ffn_router_w, L0_ffn_w1,
           L0_ffn_w2, L0_ffn_w3, L1_attn_key_matrices, L1_attn_query_matrices, L1_attn_value_in_matrices,
           L1_attn_value_out_matrices, L1_ffn_Wq_pk, L1_ffn_pk_keys, L1_ffn_Wq, L1_ffn_keys_table,
           L1_ffn_values_table, L1_ffn_Wo):
    import concourse.bacc as bacc
    from concourse.bass_utils import run_bass_kernel_spmd

    patches = np.asarray(x).reshape(IMAGES, 3, 6, 16, 6, 16).transpose(0, 2, 4, 1, 3, 5).reshape(IMAGES, 36, 768)
    tokens = np.zeros((GROUPS * PER, TOK, 768), np.float32)
    tokens[:IMAGES, 1:] = patches
    consts = _constants()
    table = np.concatenate([L1_ffn_keys_table, L1_ffn_values_table], 1)
    arrays = {
        "x_img": tokens.reshape(GROUPS, ROWS, KCH, 128).transpose(0, 3, 2, 1).reshape(GROUPS, 128, KCH * ROWS),
        "cls_tok": np.asarray(cls_tok).reshape(1, C),
        "tok_w": np.asarray(L0_tok_W).T.reshape(KCH, 128, C).transpose(1, 0, 2).reshape(128, KCH * C),
        "tok_b": L0_tok_b,
        "a_wq": np.asarray(L0_attn_Wq).T, "a_wk": np.asarray(L0_attn_Wk).T,
        "a_wv": np.asarray(L0_attn_Wv).reshape(32, 2, C).transpose(1, 0, 2).reshape(C, C).T,
        "a_mlp": L0_attn_w_mlp, "a_b": L0_attn_b_mlp, "unmix": consts["unmix"],
        "ln1": L0_ffn_ln1_w, "ln2": L0_ffn_ln2_w,
        "wqkv": np.concatenate([L0_ffn_wq, L0_ffn_wk, L0_ffn_wv]).T, "wo": np.asarray(L0_ffn_wo).T,
        "router": np.asarray(L0_ffn_router_w).T,
        "w1": np.asarray(L0_ffn_w1).transpose(2, 0, 1).reshape(C, NEXP * HID),
        "w2": np.asarray(L0_ffn_w2).reshape(NEXP, C, 2, HH).transpose(3, 0, 2, 1).reshape(HH, 2 * NEXP, C),
        "w3": np.asarray(L0_ffn_w3).transpose(2, 0, 1).reshape(C, NEXP * HID),
        "rope": consts["rope"],
        "key_m": np.asarray(L1_attn_key_matrices).transpose(2, 0, 1),
        "query_m": np.asarray(L1_attn_query_matrices).transpose(2, 0, 1),
        "value_in": np.asarray(L1_attn_value_in_matrices).transpose(2, 0, 1),
        "value_out": np.asarray(L1_attn_value_out_matrices).transpose(1, 0, 2),
        "pk_w": np.asarray(L1_ffn_Wq_pk).reshape(C, 2, HEADS, 32).transpose(3, 2, 1, 0).reshape(32, 2 * HEADS, C),
        "pk_k": np.asarray(L1_ffn_pk_keys).transpose(3, 2, 0, 1).reshape(32, 2 * HEADS, KEYS),
        "mem_wq": np.asarray(L1_ffn_Wq).reshape(C, HEADS, C),
        "table": table.reshape(HEADS, CHUNKS, 128, 128).transpose(0, 2, 1, 3),
        "mem_wo": np.asarray(L1_ffn_Wo).reshape(HEADS, C, C).transpose(1, 0, 2),
        "ident_in": consts["ident_in"], "mask_in": consts["mask_in"],
    }
    nc = bacc.Bacc("TRN2", target_bir_lowering=False, num_devices=1)
    arrays = {f"in_{n}": np.ascontiguousarray(a) for n, a in arrays.items()}
    args = {n[3:]: nc.dram_tensor(n, a.shape, mybir.dt.from_np(a.dtype), kind="ExternalInput").ap() for n, a in arrays.items()}
    out = nc.dram_tensor("out", (ROWS, GROUPS, C), F32, kind="ExternalOutput").ap()
    vision_tower(nc, **args, out=out)
    got = run_bass_kernel_spmd(nc, [arrays], core_ids=[0]).results[0]["out"]
    return got.transpose(1, 0, 2).reshape(GROUPS * PER, TOK, C)[:IMAGES]
```

```python
from contextlib import ExitStack

import numpy as np

import concourse.bass as bass
from concourse import mybir

F32 = mybir.dt.float32
ALU = mybir.AluOpType
ACT = mybir.ActivationFunctionType
AX = mybir.AxisListType

C = 64
IMAGES, TOK = 64, 37
PER = 3
ROWS = PER * TOK
GROUPS = 22
COLS = ROWS * GROUPS
KCH = 6
BANK = 512
NEXP, HID = 8, 170
REST = HID - 128
RESTS = ((0, 3), (3, 3), (6, 2))
HEADS = 8
KEYS = 64
TOPK = 16
ENT = KEYS * KEYS
CHUNKS = ENT // 128
TILES = -(-IMAGES * TOK // 128)
UNITS = HEADS * TILES
PADT = TILES * 128
KVT = 128 + HEADS * PADT + COLS
NEG = -3.0e38
LOAN = 1


class Scope:

    spent = []

    def __init__(self, nc, tag):
        self.nc, self.tag = nc, tag
        self.ctx, self.sem_ctx, self.sems, self.old = ExitStack(), ExitStack(), [], []

    def __enter__(self):
        return self

    def __exit__(self, *a):
        self.ctx.close()
        for ctx, _ in self.old:
            ctx.close()
        if self.sems:
            Scope.spent.append((self.sem_ctx, self.sems))

    def sb(self, name, shape, dt=F32):
        return self.ctx.enter_context(self.nc.sbuf_tensor(f"{self.tag}_{name}", shape, dt))

    def bank(self, name):
        return self.ctx.enter_context(self.nc.psum_tensor(f"{self.tag}_{name}", [128, BANK], F32))

    def sem(self, name):
        self.sems.append(self.sem_ctx.enter_context(self.nc.semaphore(f"{self.tag}_{name}")))
        return self.sems[-1]

    def block(self):
        block = self.ctx.enter_context(self.nc.Block())
        self.old, Scope.spent = Scope.spent, []

        @block.sync
        def _(sp):
            for _, sems in self.old:
                for sem in sems:
                    sp.sem_clear(sem)
        return block


class Chain:

    def __init__(self, eng, sem, base=0):
        self.eng, self.sem, self.base, self.n = eng, sem, base, 0

    def step(self, ins):
        ins.then_inc(self.sem, 1)
        self.n += 1

    def wait(self):
        self.eng.wait_ge(self.sem, self.base + self.n)


def spread(ap, axis, n):
    a = ap.unsqueeze(axis)
    shape = list(a.shape)
    shape[axis] = n
    return a.broadcast_to(shape)


def await_count(eng, sem, count):
    if not isinstance(count, int) or count > 0:
        eng.wait_ge(sem, count)


def embed(nc, hid, x_img, w_tokT, cls_tok, b_tok, ident, later, later_in, zeroed):
    PAIRS, COLS2 = GROUPS // 2, 2 * ROWS
    with Scope(nc, "tok") as s:
        patches = [s.sb(f"patches{p}", [128, KCH * COLS2]) for p in range(PAIRS)]
        w = s.sb("w", [128, KCH * C])
        add = s.sb("add", [ROWS, C])
        flat = [s.sb(f"flat{i}", [C, COLS2]) for i in range(2)]
        acc, turned = ([s.bank(f"{n}{i}") for i in range(2)] for n in ("acc", "turned"))
        w_in, bias_in, cls_in, zero_ok = (s.sem(n) for n in ("w_in", "bias_in", "cls_in", "zero"))
        patches_in = [s.sem(f"patches_in{p}") for p in range(PAIRS)]
        product_done, flat_ok, turned_done, row_done = (s.sem(n) for n in ("product_done", "flat", "turned_done", "row_done"))
        block = s.block()

        @block.sync
        def _(sp):
            sp.dma_start(w[:, :], w_tokT).then_inc(w_in, 16)
            for p in range(PAIRS):
                sp.dma_start(patches[p][:, :], x_img[p, :, :]).then_inc(patches_in[p], 16)
            for spot, source in later:
                sp.dma_start(spot, source).then_inc(later_in, 16)

        @block.gpsimd
        def _(pool):
            for n, spot in enumerate(zeroed):
                if n:
                    pool.wait_ge(zero_ok, n)
                nc.gpsimd.memset(spot, 0.0).then_inc(zero_ok, 1)

        @block.tensor
        def _(pe):
            def turn(p):
                pe.wait_ge(flat_ok, p + 1)
                await_count(pe, row_done, p - 1)
                for k in range(2):
                    last = nc.tensor.transpose(turned[p % 2][0:ROWS, k * C:(k + 1) * C],
                                               flat[p % 2][:, k * ROWS:(k + 1) * ROWS], ident[0:C, 0:C])
                last.then_inc(turned_done, 1)

            pe.wait_ge(w_in, 16)
            for p in range(PAIRS):
                pe.wait_ge(patches_in[p], 16)
                await_count(pe, flat_ok, p - 1)
                for c in range(KCH):
                    last = nc.tensor.matmul(acc[p % 2][0:C, 0:COLS2], w[:, c * C:(c + 1) * C],
                                            patches[p][:, c * COLS2:(c + 1) * COLS2], start=c == 0, stop=c == KCH - 1)
                last.then_inc(product_done, 1)
                if p > 0:
                    turn(p - 1)
            turn(PAIRS - 1)

        @block.scalar
        def _(act):
            act.dma_start(add[:, :], b_tok.rearrange("(o c) -> o c", o=1).broadcast_to([ROWS, C])).then_inc(bias_in, 16)
            act.wait_ge(bias_in, 16)
            for m in range(PER):
                act.dma_start(add[m * TOK:m * TOK + 1, :], cls_tok).then_inc(cls_in, 16)
            for p in range(PAIRS):
                act.wait_ge(product_done, p + 1)
                await_count(act, turned_done, p - 1)
                nc.scalar.copy(flat[p % 2][:, :], acc[p % 2][0:C, 0:COLS2]).then_inc(flat_ok, 1)

        @block.vector
        def _(dve):
            dve.wait_ge(bias_in, 16)
            dve.wait_ge(cls_in, 16 * PER)
            for p in range(PAIRS):
                dve.wait_ge(turned_done, p + 1)
                nc.vector.tensor_tensor(hid[:, 2 * p:2 * p + 2, :], turned[p % 2][0:ROWS, 0:2 * C].rearrange("p (g c) -> p g c", g=2),
                                        spread(add[:, :], 1, 2), ALU.add).then_inc(row_done, 1)


def normalize(nc, tag, src, dst, xT, ident, center, eps, weight=None, twice=False):
    width = 2 * C if twice else C
    with Scope(nc, tag) as s:
        row = [ROWS, GROUPS]
        work = s.sb("work", [ROWS, GROUPS, C])
        mean, power, rstd = s.sb("mean", row), s.sb("power", row), s.sb("rstd", row)
        flip = [s.bank(f"flip{i}") for i in range(6)]
        centered_ok, square_ok, power_ok, rstd_ok = (s.sem(n) for n in ("centered", "square", "power", "rstd"))
        out_ok, flip_ok, dve_own = s.sem("out"), s.sem("flip"), s.sem("dve_own")
        w_in = s.sem("w_in")
        xc = dst if center else src
        if weight is not None:
            wrow = s.sb("wrow", [ROWS, C])
        block = s.block()
        PARTS = ((0, 8), (8, 8), (16, 6))
        quads = [(n, min(4, GROUPS - 4 * n)) for n in range(6)]

        @block.sync
        def _(sp):
            if weight is not None:
                sp.dma_start(wrow[:, :], weight.rearrange("(o c) -> o c", o=1).broadcast_to([ROWS, C])).then_inc(w_in, 16)

        @block.vector
        def _(dve):
            own = Chain(dve, dve_own)
            part = [slice(g, g + n) for g, n in PARTS]
            if center:
                for p in part:
                    own.step(nc.vector.tensor_reduce(mean[:, p], src[:, p, :], AX.X, ALU.add))
                    own.wait()
                    own.step(nc.vector.tensor_scalar(mean[:, p], mean[:, p], 1.0 / C, None, ALU.mult))
                    own.wait()
                    nc.vector.tensor_tensor(dst[:, p, :], src[:, p, :], spread(mean[:, p], 2, C),
                                            ALU.subtract).then_inc(centered_ok, 1)
            for n, p in enumerate(part):
                dve.wait_ge(square_ok, n + 1)
                own.step(nc.vector.tensor_reduce(power[:, p], work[:, p, :], AX.X, ALU.add))
                own.wait()
                nc.vector.tensor_scalar(power[:, p], power[:, p], eps, None, ALU.add).then_inc(power_ok, 1)
            for n, p in enumerate(part):
                dve.wait_ge(rstd_ok, n + 1)
                own.step(nc.vector.reciprocal(rstd[:, p], rstd[:, p]))
                own.wait()
                if center:
                    dve.wait_ge(centered_ok, n + 1)
                last = nc.vector.tensor_tensor(dst[:, p, :], xc[:, p, :], spread(rstd[:, p], 2, C), ALU.mult)
                if weight is not None:
                    own.step(last)
                    own.wait()
                    dve.wait_ge(w_in, 16)
                    last = nc.vector.tensor_tensor(dst[:, p, :], dst[:, p, :], spread(wrow[:, :], 1, PARTS[n][1]), ALU.mult)
                last.then_inc(out_ok, 1)
            for n, m in quads[1::2]:
                dve.wait_ge(flip_ok, n + 1)
                nc.vector.tensor_copy(xT[0:width, 4 * n * ROWS:(4 * n + m) * ROWS], flip[n][0:width, 0:m * ROWS])

        @block.scalar
        def _(act):
            for n, (g, m) in enumerate(PARTS):
                if center:
                    act.wait_ge(centered_ok, n + 1)
                nc.scalar.activation(work[:, g:g + m, :], xc[:, g:g + m, :], ACT.Square, scale=C ** -0.5).then_inc(square_ok, 1)
            for n, (g, m) in enumerate(PARTS):
                act.wait_ge(power_ok, n + 1)
                nc.scalar.activation(rstd[:, g:g + m], power[:, g:g + m], ACT.Sqrt).then_inc(rstd_ok, 1)
            for n, m in quads[0::2]:
                act.wait_ge(flip_ok, n + 1)
                nc.scalar.copy(xT[0:width, 4 * n * ROWS:(4 * n + m) * ROWS], flip[n][0:width, 0:m * ROWS])

        @block.tensor
        def _(pe):
            for n, m in quads:
                pe.wait_ge(out_ok, n // 2 + 1)
                for j in range(m):
                    columns = slice(j * ROWS, (j + 1) * ROWS)
                    last = nc.tensor.transpose(flip[n][0:C, columns], dst[:, 4 * n + j, :], ident[0:ROWS, 0:ROWS])
                    if twice:
                        last = nc.tensor.matmul(flip[n][C:128, columns], dst[:, 4 * n + j, :], ident[0:ROWS, 0:ROWS],
                                                start=True, stop=True)
                last.then_inc(flip_ok, 1)


def relu_attention(nc, hid, xT, ident, wqT, wkT, wvT, w_mlp, b_mlp, unmix, later_in, later_count):
    HALF = IMAGES // 2
    D = 32
    SLOTS = 4
    OCT = IMAGES // 8
    with Scope(nc, "rat") as s:
        q, k = s.sb("q", [128, HALF, TOK]), s.sb("k", [128, HALF, TOK])
        w3 = s.sb("w3", [128, 3 * C])
        window = s.sb("window", [128, 252])
        b_sb = s.sb("b_sb", [1, 1])
        zrow = s.sb("zrow", [1, BANK])
        ones = s.sb("ones", [1, 128])
        brow = s.sb("brow", [1, BANK])
        wst = [s.sb(f"wst{i}", [128, 128]) for i in range(SLOTS)]
        diff = [s.sb(f"diff{i}", [128, TOK, TOK]) for i in range(SLOTS)]
        logit = s.sb("logit", [128, TOK, TOK])
        top, tot = s.sb("top", [128, TOK]), s.sb("tot", [128, TOK])
        prob_t = s.sb("prob_t", [128, TOK, 128])
        v8 = [s.sb(f"v8_{i}", [128, 9 * C]) for i in range(2)]
        out_t = s.sb("out_t", [128, COLS])
        unmix_sb = s.sb("unmix", [128, C])
        bank = [s.bank(f"b{i}") for i in range(8)]
        w_in, win_in, pad_ok, const_ok, b_ok = (s.sem(n) for n in ("w_in", "win_in", "pad", "const", "b"))
        qk_done, q_out, k_out = s.sem("qk_done"), s.sem("q_out"), s.sem("k_out")
        win_ok, diff_ok, relu_ok, pair_done = (s.sem(n) for n in ("win", "diff", "relu", "pair_done"))
        logits_done, logit_ok, own, exp_ok, prob_ok = (s.sem(n) for n in ("logits_done", "logit", "dve_own", "exp", "prob"))
        flip_ok, flip_a, flip_d = s.sem("flip"), s.sem("flip_a"), s.sem("flip_d")
        v_done, v8_ok, mix_done, mix_out = (s.sem(n) for n in ("v_done", "v8", "mix_done", "mix_out"))
        back_ok, centered = s.sem("back"), s.sem("sub")
        block = s.block()
        PARTS = ((0, 13), (13, 12), (25, 12))
        FLIPS = -(-TOK // 4)
        QUAD = 8 * TOK // 2
        before = [w3[C:128, :], unmix_sb[C:128, :], window[:, :]]
        after = [out_t[:, :], zrow[:, :], v8[0][:, :], v8[1][:, :], prob_t[:, :, :]]
        PADS = len(before) + len(after)

        @block.sync
        def _(sp):
            sp.dma_start(w3[0:C, 0:C], wqT).then_inc(w_in, 16)
            sp.dma_start(w3[0:C, C:2 * C], wkT).then_inc(w_in, 16)
            sp.dma_start(w3[0:C, 2 * C:3 * C], wvT).then_inc(w_in, 16)
            sp.dma_start(unmix_sb[0:C, :], unmix).then_inc(w_in, 16)
            sp.dma_start(b_sb[:, :], b_mlp.rearrange("(o c) -> o c", o=1)).then_inc(w_in, 16)
            sp.wait_ge(pad_ok, len(before))
            for m in range(4):
                sp.dma_start(window[m * D:(m + 1) * D, 124 + m:125 + m],
                             w_mlp.rearrange("(d o) -> d o", o=1)).then_inc(win_in, 16)
            sp.wait_ge(later_in, later_count)

        @block.gpsimd
        def _(pool):
            for n, spot in enumerate(before + after):
                if n:
                    pool.wait_ge(pad_ok, n)
                if n == len(before):
                    nc.gpsimd.memset(ones[:, :], 1.0).then_inc(const_ok, 1)
                    pool.wait_ge(const_ok, 1)
                nc.gpsimd.memset(spot, 0.0).then_inc(pad_ok, 1)
            pool.wait_ge(w_in, 80)
            pool.wait_ge(pad_ok, PADS)
            nc.gpsimd.tensor_scalar(brow[:, :], zrow[:, :], b_sb[0:1, 0:1], None, ALU.add).then_inc(b_ok, 1)
            pool.wait_ge(b_ok, 1)
            pool.wait_ge(win_in, 64)
            with pool.Fori(0, HALF // SLOTS) as i:
                for m in range(SLOTS):
                    at = pool.snap(i * (-4 * SLOTS) + (124 - 4 * m))
                    pool.wait_ge(pair_done, SLOTS * i + m + 1)
                    nc.gpsimd.tensor_copy(wst[m][:, :], window[:, bass.ds(at, 128)]).then_inc(win_ok, 1)

        @block.tensor
        def _(pe):
            pe.sem_inc(pair_done, SLOTS)
            pe.wait_ge(w_in, 80)
            pe.wait_ge(pad_ok, 1)
            for n in range(4):
                for j in range(2):
                    for hf in range(2):
                        at = (hf * 4 + n) * 8 * TOK
                        last = nc.tensor.matmul(bank[2 * n + j][C * hf:C * hf + C, 0:8 * TOK], w3[:, j * C:(j + 1) * C],
                                                xT[:, at:at + 8 * TOK], start=True, stop=True)
                last.then_inc(qk_done, 1)
            pe.wait_ge(pad_ok, PADS)
            pe.wait_ge(const_ok, 1)
            pe.wait_ge(q_out, 2)
            pe.wait_ge(k_out, 2)
            for b, (r, n) in enumerate(PARTS):
                nc.tensor.matmul(bank[b][:, 0:n * TOK], ones[:, :], zrow[:, 0:n * TOK], start=True, stop=False)
            with pe.Fori(0, HALF // SLOTS) as i:
                for m in range(SLOTS):
                    pe.wait_ge(win_ok, SLOTS * i + m + 1)
                    pe.wait_ge(relu_ok, SLOTS * i + m + 1)
                    for b, (r, n) in enumerate(PARTS):
                        last = nc.tensor.matmul(bank[b][:, 0:n * TOK], wst[m][:, :], diff[m][:, r:r + n, :],
                                                start=False, stop=False)
                    last.then_inc(pair_done, 1)
            pe.wait_ge(b_ok, 1)
            for b, (r, n) in enumerate(PARTS):
                nc.tensor.matmul(bank[b][:, 0:n * TOK], ones[:, :], brow[:, 0:n * TOK],
                                 start=False, stop=True).then_inc(logits_done, 1)

            def make_values(c):
                await_count(pe, v8_ok, c - 1)
                if c == 0:
                    pe.wait_ge(k_out, 4)
                for j in range(8):
                    at = (8 * c + j) * TOK
                    last = nc.tensor.matmul(bank[6 + c % 2][0:TOK, j * C:(j + 1) * C], xT[:, at:at + TOK],
                                            w3[:, 2 * C:3 * C], start=True, stop=True)
                last.then_inc(v_done, 1)

            make_values(0)
            make_values(1)
            for n in range(FLIPS):
                rows = range(4 * n, min(4 * n + 4, TOK))
                pe.wait_ge(prob_ok, 1 + sum(rows[-1] >= r for r, _ in PARTS[1:]))
                if n >= 3:
                    pe.wait_ge((flip_a, flip_d)[(n - 3) % 2], (n - 3) // 2 + 1)
                for r in rows:
                    last = nc.tensor.transpose(bank[3 + n % 3][0:TOK, (r % 4) * 128:(r % 4 + 1) * 128], logit[:, r, :],
                                               ident[:, :])
                last.then_inc(flip_ok, 1)
            pe.wait_ge(flip_a, FLIPS // 2)
            pe.wait_ge(flip_d, FLIPS // 2)
            pe.wait_ge(logit_ok, 3)
            for c in range(OCT):
                pe.wait_ge(v8_ok, c + 1)
                await_count(pe, mix_out, 4 * (c - 1))
                for j in range(8):
                    column = 4 * ((8 * c + j) % HALF) + 2 * (c // (OCT // 2))
                    last = nc.tensor.matmul(bank[2 * (c % 2) + j // 4][:, (j % 4) * 2 * TOK:(j % 4 + 1) * 2 * TOK],
                                            v8[c % 2][:, j * C:j * C + 128],
                                            prob_t[:, :, column:column + 2], start=True, stop=True)
                last.then_inc(mix_done, 1)
                if c + 2 < OCT:
                    make_values(c + 2)
            for g in range(GROUPS):
                if g % 8 == 0:
                    pe.wait_ge(mix_out, 4 * min(OCT, -(-(g + 8) * PER // 8)))
                last = nc.tensor.matmul(bank[4 + g // 8][0:ROWS, (g % 8) * C:(g % 8 + 1) * C],
                                        out_t[:, g * ROWS:(g + 1) * ROWS], unmix_sb[:, :], start=True, stop=True)
                if g % 8 == 7 or g == GROUPS - 1:
                    last.then_inc(back_ok, 1)

        @block.scalar
        def _(act):
            for n in range(4):
                act.wait_ge(qk_done, n + 1)
                nc.scalar.copy(q[:, n * 8:(n + 1) * 8, :].rearrange("p i t -> p (i t)"), bank[2 * n][:, 0:8 * TOK]).then_inc(q_out, 1)
            with act.Fori(0, HALF // SLOTS) as i:
                for m in range(SLOTS):
                    act.wait_ge(diff_ok, SLOTS * i + m + 1)
                    nc.scalar.activation(diff[m][:, :, :], diff[m][:, :, :], ACT.Relu).then_inc(relu_ok, 1)
            for b, (r, n) in enumerate(PARTS):
                act.wait_ge(logits_done, 3)
                nc.scalar.activation(logit[:, r:r + n, :].rearrange("p a b -> p (a b)"), bank[b][:, 0:n * TOK], ACT.Relu).then_inc(logit_ok, 1)
            for b, (r, n) in enumerate(PARTS):
                act.wait_ge(centered, b + 1)
                nc.scalar.activation(logit[:, r:r + n, :], logit[:, r:r + n, :], ACT.Exp).then_inc(exp_ok, 1)

            def take_values(c):
                act.wait_ge(v_done, c + 1)
                await_count(act, mix_done, c - 1)
                nc.scalar.copy(v8[c % 2][0:TOK, 0:8 * C], bank[6 + c % 2][0:TOK, :]).then_inc(v8_ok, 1)

            take_values(0)
            take_values(1)
            for n in range(0, FLIPS, 2):
                act.wait_ge(flip_ok, n + 1)
                m = min(4, TOK - 4 * n)
                nc.scalar.copy(prob_t[0:TOK, 4 * n:4 * n + m, :].rearrange("p a b -> p (a b)"),
                               bank[3 + n % 3][0:TOK, 0:128 * m]).then_inc(flip_a, 1)
            for c in range(2, OCT):
                take_values(c)

        @block.vector
        def _(dve):
            for n in range(4):
                dve.wait_ge(qk_done, n + 1)
                nc.vector.tensor_copy(k[:, n * 8:(n + 1) * 8, :].rearrange("p i t -> p (i t)"), bank[2 * n + 1][:, 0:8 * TOK]).then_inc(k_out, 1)
            dve.wait_ge(q_out, 4)
            dve.wait_ge(k_out, 4)
            with dve.Fori(0, HALF // SLOTS) as i:
                for m in range(SLOTS):
                    dve.wait_ge(pair_done, SLOTS * i + m + 1)
                    one = bass.ds(SLOTS * i + m, 1)
                    nc.vector.tensor_tensor(diff[m][:, :, :], q[:, one, :].rearrange("p o t -> p t o").broadcast_to([128, TOK, TOK]),
                                            k[:, one, :].broadcast_to([128, TOK, TOK]), ALU.subtract).then_inc(diff_ok, 1)
            chain = Chain(dve, own)
            part = [(logit[:, r:r + n, :], top[:, r:r + n], tot[:, r:r + n]) for r, n in PARTS]
            for b, (values, most, _) in enumerate(part):
                dve.wait_ge(logit_ok, b + 1)
                chain.step(nc.vector.tensor_reduce(most, values, AX.X, ALU.max))
                chain.wait()
                nc.vector.tensor_tensor(values, values, spread(most, 2, TOK), ALU.subtract).then_inc(centered, 1)
            for b, (values, _, total) in enumerate(part):
                dve.wait_ge(exp_ok, b + 1)
                chain.step(nc.vector.tensor_reduce(total, values, AX.X, ALU.add))
                chain.wait()
                chain.step(nc.vector.reciprocal(total, total))
                chain.wait()
                nc.vector.tensor_tensor(values, values, spread(total, 2, TOK), ALU.mult).then_inc(prob_ok, 1)
            for n in range(1, FLIPS, 2):
                dve.wait_ge(flip_ok, n + 1)
                m = min(4, TOK - 4 * n)
                nc.vector.tensor_copy(prob_t[0:TOK, 4 * n:4 * n + m, :].rearrange("p a b -> p (a b)"),
                                      bank[3 + n % 3][0:TOK, 0:128 * m]).then_inc(flip_d, 1)
            for c in range(OCT):
                dve.wait_ge(mix_done, c + 1)
                for h4 in range(2):
                    for g in range(2):
                        src = bank[2 * (c % 2) + h4][g * D:(g + 1) * D, 0:8 * TOK].rearrange("p (j t g) -> p j t g", j=4, g=2)
                        at = (2 * c + h4) * QUAD
                        nc.vector.tensor_copy(out_t[g * D:(g + 1) * D, at:at + QUAD].rearrange("p (j t) -> p j t", j=4),
                                              src[:, :, :, g]).then_inc(mix_out, 1)
            for n in range(3):
                m = min(8, GROUPS - 8 * n)
                dve.wait_ge(back_ok, n + 1)
                nc.vector.tensor_tensor(hid[:, 8 * n:8 * n + m, :].rearrange("p g c -> p (g c)"),
                                        hid[:, 8 * n:8 * n + m, :].rearrange("p g c -> p (g c)"),
                                        bank[4 + n][0:ROWS, 0:m * C], ALU.add)


def merge(nc, tag, pairs, spots):
    with Scope(nc, tag) as s:
        banks = [s.bank(f"m{i}") for i in range(-(-len(pairs) // 8))]
        bank_ok = s.sem("bank")
        block = s.block()

        @block.tensor
        def _(pe):
            for n, (left, right) in enumerate(pairs):
                last = nc.tensor.matmul(banks[n // 8][0:C, (n % 8) * C:(n % 8 + 1) * C], left, right, start=True, stop=True)
                if n % 8 == 7:
                    last.then_inc(bank_ok, 1)

        @block.vector
        def _(dve):
            for n, spot in enumerate(spots):
                dve.wait_ge(bank_ok, n + 1)
                nc.vector.tensor_copy(spot, banks[n][0:C, :])


def load(nc, tag, pairs):
    with Scope(nc, tag) as s:
        arrived = s.sem("arrived")
        block = s.block()

        @block.sync
        def _(sp):
            for dst, src in pairs:
                sp.dma_start(dst, src).then_inc(arrived, 16)
            sp.wait_ge(arrived, 16 * len(pairs))


def skewed(eng, step, before, after, n=GROUPS):
    lo, hi = after, n - before
    lo += lo % 2
    hi -= hi % 2
    for i in range(-before, lo):
        step(i, i % 2)
    with eng.Fori(0, (hi - lo) // 2) as j:
        for k in range(2):
            step(2 * j + (lo + k), k)
    for i in range(hi, n + after):
        step(i, i % 2)


def live(i, shift=0, n=GROUPS):
    return not isinstance(i, int) or 0 <= i + shift < n


def head_attention(nc, tag, hid, xT, ident, mask, wq, wv, scale, kv=None):
    HALF = 4 * ROWS
    NH = HEADS
    with Scope(nc, tag) as s:
        def two(name, shape):
            return [s.sb(f"{name}{i}", shape) for i in range(2)]
        x_g = two("x_g", [128, ROWS])
        q_t = two("q_t", [128, NH, ROWS])
        v_g = two("v_g", [ROWS, NH * C])
        score = two("score", [ROWS, NH, ROWS])
        prob_t = two("prob_t", [ROWS, NH * ROWS])
        top, shift, tot = two("top", [ROWS, NH]), two("shift", [ROWS, NH]), two("tot", [ROWS, NH])
        if kv is not None:
            kv_g = two("kv_g", [128, NH, ROWS])
        q_half = [[t[n * C:(n + 1) * C, :, :].rearrange("p (m n) t -> p n m t", n=2)[:, n, :, :] for n in range(2)] for t in q_t]
        s_bank, t_bank = ([s.bank(f"{n}{j}") for j in range(2)] for n in ("s", "t"))
        q_bank, v_bank, o_bank = s.bank("q"), s.bank("v"), s.bank("o")
        x_ok, kv_ok, q_done, v_done, q_a, q_d, v_ok = (s.sem(n) for n in ("x", "kv", "q_done", "v_done", "q_a", "q_d", "v"))
        score_done, masked, top_ok, shift_ok, exp_ok, prob_ok = (
            s.sem(n) for n in ("score_done", "masked", "top", "shift", "exp", "prob"))
        recip_ok, pad_ok = s.sem("recip"), s.sem("pad")
        flip_done, flip_a, flip_d, mix_done, hid_ok = (s.sem(n) for n in ("flip_done", "flip_a", "flip_d", "mix_done", "hid"))
        block = s.block()

        @block.gpsimd
        def _(pool):
            for k in range(2):
                nc.gpsimd.memset(q_t[k][:, :, :], 0.0).then_inc(pad_ok, 1)
            pool.wait_ge(pad_ok, 2)

            def step(g, k):
                if not live(g):
                    return
                await_count(pool, v_done, g - 1)
                nc.gpsimd.tensor_copy(x_g[k][:, :], xT[:, bass.ds(g * ROWS, ROWS)]).then_inc(x_ok, 1)
                if kv is not None:
                    nc.gpsimd.tensor_copy(
                        kv_g[k][:, :, :],
                        kv[:, bass.ds(g * ROWS + 128, NH * PADT)].rearrange("p (h t) -> p h t", h=NH)[:, :, 0:ROWS]).then_inc(kv_ok, 1)
            skewed(pool, step, 0, 2)

        @block.tensor
        def _(pe):
            def turn(g, k):
                await_count(pe, prob_ok, g + 1)
                await_count(pe, flip_a, g)
                await_count(pe, flip_d, g)
                for h in range(NH):
                    last = nc.tensor.transpose(t_bank[h // 4][0:ROWS, (h % 4) * ROWS:(h % 4 + 1) * ROWS],
                                               score[k][:, h, :], ident[0:ROWS, 0:ROWS])
                    if h % 4 == 3:
                        last.then_inc(flip_done, 1)

            def make_scores(g, k):
                if kv is not None:
                    await_count(pe, kv_ok, g + 1)
                await_count(pe, masked, 2 * g)
                await_count(pe, q_d, g + 1)
                await_count(pe, q_a, g + 1)
                for h in range(NH):
                    keys = x_g[k][:, :] if kv is None else kv_g[k][:, h, :]
                    last = nc.tensor.matmul(s_bank[h // 4][0:ROWS, (h % 4) * ROWS:(h % 4 + 1) * ROWS],
                                            q_t[k][:, h, :], keys, start=True, stop=True)
                    if h % 4 == 3:
                        last.then_inc(score_done, 1)

            def make_queries(g, k):
                await_count(pe, q_a, g)
                await_count(pe, q_d, g)
                await_count(pe, x_ok, g + 1)
                for m in range(NH // 2):
                    last = nc.tensor.matmul(q_bank[:, m * ROWS:(m + 1) * ROWS],
                                            wq[:, 2 * m:2 * m + 2, :].rearrange("p h c -> p (h c)"), x_g[k][:, :],
                                            start=True, stop=True)
                last.then_inc(q_done, 1)

            def mix(g, k):
                await_count(pe, hid_ok, g)
                await_count(pe, v_ok, g + 1)
                await_count(pe, flip_a, g + 1)
                await_count(pe, flip_d, g + 1)
                for h in range(NH):
                    last = nc.tensor.matmul(o_bank[0:ROWS, 0:C], prob_t[k][:, h * ROWS:(h + 1) * ROWS],
                                            v_g[k][:, h * C:(h + 1) * C], start=h == 0, stop=h == NH - 1)
                last.then_inc(mix_done, 1)

            def make_values(g, k):
                await_count(pe, v_ok, g)
                if kv is None:
                    nc.tensor.matmul(v_bank[0:ROWS, :], x_g[k][:, :], wv[:, :, :].rearrange("p h c -> p (h c)"),
                                     start=True, stop=True).then_inc(v_done, 1)
                else:
                    for h in range(NH):
                        last = nc.tensor.matmul(v_bank[0:ROWS, h * C:(h + 1) * C], kv_g[k][:, h, :], wv[:, h, :],
                                                start=True, stop=True)
                    last.then_inc(v_done, 1)

            def step(i, k):
                if live(i, -2):
                    turn(i - 2, k)
                if live(i):
                    make_scores(i, k)
                if live(i, 1):
                    make_queries(i + 1, 1 - k)
                if live(i, -2):
                    mix(i - 2, k)
                if live(i):
                    make_values(i, k)
            pe.wait_ge(pad_ok, 2)
            skewed(pe, step, 1, 2)

        @block.scalar
        def _(act):
            def step(i, k):
                if live(i, -2):
                    act.wait_ge(flip_done, 2 * i - 3)
                    nc.scalar.copy(prob_t[k][:, 0:HALF], t_bank[0][0:ROWS, 0:HALF]).then_inc(flip_a, 1)
                if live(i, 1):
                    act.wait_ge(q_done, i + 2)
                    nc.scalar.copy(q_half[1 - k][0], q_bank[0:C, 0:HALF].rearrange("p (m t) -> p m t", t=ROWS)).then_inc(q_a, 1)
                if live(i):
                    act.wait_ge(shift_ok, i + 1)
                    for h in range(NH):
                        last = nc.scalar.activation(score[k][:, h, :], score[k][:, h, :], ACT.Exp, scale=scale,
                                                    bias=shift[k][:, h:h + 1], accum_out=tot[k][:, h:h + 1])
                    last.then_inc(exp_ok, 1)
                    act.wait_ge(v_done, i + 1)
                    nc.scalar.copy(v_g[k][:, :], v_bank[0:ROWS, :]).then_inc(v_ok, 1)
            act.wait_ge(pad_ok, 2)
            skewed(act, step, 1, 2)

        @block.vector
        def _(dve):
            def normalize_rows(g, k):
                dve.wait_ge(exp_ok, g + 1)
                nc.vector.reciprocal(tot[k][:, :], tot[k][:, :]).then_inc(recip_ok, 1)
                dve.wait_ge(recip_ok, g + 1)
                nc.vector.tensor_tensor(score[k][:, :, :], score[k][:, :, :], spread(tot[k][:, :], 2, ROWS),
                                        ALU.mult).then_inc(prob_ok, 1)

            def mask_scores(g, k):
                for j in range(2):
                    dve.wait_ge(score_done, 2 * g + j + 1)
                    nc.vector.tensor_tensor(score[k][:, 4 * j:4 * j + 4, :],
                                            s_bank[j][0:ROWS, 0:HALF].rearrange("p (h t) -> p h t", h=4),
                                            spread(mask[:, :], 1, 4), ALU.add).then_inc(masked, 1)
                dve.wait_ge(masked, 2 * g + 2)
                nc.vector.tensor_reduce(top[k][:, :], score[k][:, :, :], AX.X, ALU.max).then_inc(top_ok, 1)
                dve.wait_ge(top_ok, g + 1)
                nc.vector.tensor_scalar(shift[k][:, :], top[k][:, :], -scale, None, ALU.mult).then_inc(shift_ok, 1)

            def step(i, k):
                if live(i, -2):
                    dve.wait_ge(flip_done, 2 * i - 2)
                    nc.vector.tensor_copy(prob_t[k][:, HALF:2 * HALF], t_bank[1][0:ROWS, 0:HALF]).then_inc(flip_d, 1)
                if live(i):
                    mask_scores(i, k)
                if live(i, -1):
                    normalize_rows(i - 1, 1 - k)
                if live(i, 1):
                    dve.wait_ge(q_done, i + 2)
                    nc.vector.tensor_copy(q_half[1 - k][1], q_bank[C:128, 0:HALF].rearrange("p (m t) -> p m t", t=ROWS)).then_inc(q_d, 1)
                if live(i, -2):
                    dve.wait_ge(mix_done, i - 1)
                    row = hid[:, bass.ds(i - 2, 1), :].rearrange("p g c -> p (g c)")
                    nc.vector.tensor_tensor(row, row, o_bank[0:ROWS, 0:C], ALU.add).then_inc(hid_ok, 1)
            dve.wait_ge(pad_ok, 2)
            skewed(dve, step, 1, 2)


def product_keys(nc, xT, ident, side_w, table, kv_t):
    Q = 4
    QN = ENT // Q
    SIDE = KEYS // Q
    TURNS = ENT // BANK
    PARTS = ((0, 16, 0, 2), (0, 2, 2, 16), (2, 5, 2, 5))
    CAND = sum((a1 - a0) * (b1 - b0) for a0, a1, b0, b1 in PARTS)
    PICKS = 13
    with Scope(nc, "pk") as s:
        x_st, w_st = s.sb("x_st", [C, 128]), s.sb("w_st", [C, 128])
        sim_sel, sim_sum = s.sb("sim_sel", [128, 128]), s.sb("sim_sum", [128, 128])
        total = [s.sb(f"total{q}", [128, SIDE, KEYS]) for q in range(Q)]
        weight = [s.sb(f"weight{q}", [128, QN]) for q in range(Q)]
        turned = [s.sb(f"turned{i}", [128, BANK]) for i in range(4)]
        tab = s.sb("tab", [128, CHUNKS, 128])
        best = [s.sb(f"best{p}", [128, TOPK]) for p in range(2)]
        rest = [s.sb(f"rest{p}", [128, KEYS]) for p in range(2)]
        cand, cand2, chosen = s.sb("cand", [128, CAND]), s.sb("cand2", [128, CAND]), s.sb("chosen", [128, TOPK])
        cut, shift = s.sb("cut", [128, 1]), s.sb("shift", [128, 1])
        zpart, zinv = s.sb("zpart", [128, Q]), s.sb("zinv", [128, 1])
        kv_sb = s.sb("kv_sb", [128, 128])
        expo = [s.ctx.enter_context(nc.psum_tensor(f"pk_expo{i}", [128, QN], F32)) for i in range(2)]
        turn = [s.bank(f"turn{i}") for i in range(2)]
        out, misc = s.bank("out"), s.bank("misc")
        zero_ok, staged, sims_done, sel_ok, sum_in = (s.sem(n) for n in ("zero", "staged", "sims_done", "sel", "sum_in"))
        pool_sum, exp_ok, masked, cut_ok = (s.sem(n) for n in ("pool_sum", "exp", "masked", "cut"))
        turn_done, turned_ok, mul_done = s.sem("turn_done"), s.sem("turned"), s.sem("mul_done")
        pick, z_ok, zinv_ok, kv_ok, flip_done, flip_out = (s.sem(n) for n in ("pick", "z", "zinv", "kv", "flip_done", "flip_out"))
        tab_in = [s.sem(f"tab_in{q}") for q in range(Q)]
        ready, shift_ok = s.sem("ready"), s.sem("shift")
        block = s.block()
        TURNED0, MUL0, MASKED0, TURN0 = 1 + LOAN, 3 + LOAN, 3 + LOAN, 6 + LOAN

        def sum_quarter(eng, q):
            return eng.tensor_tensor(total[q][:, :, :], spread(sim_sum[:, 0:KEYS], 1, SIDE),
                                     spread(sim_sum[:, KEYS + q * SIDE:KEYS + (q + 1) * SIDE], 2, KEYS), ALU.add)

        @block.sync
        def _(sp):
            per = CHUNKS // Q
            for q in range(Q):
                sp.dma_start(tab[:, q * per:(q + 1) * per, :], table[0, :, q * per:(q + 1) * per, :]).then_inc(tab_in[q], 16)
            with sp.Fori(1, HEADS) as h:
                for q in range(Q):
                    sp.wait_ge(mul_done, h * (TURNS * TILES) + (MUL0 - TURNS + 2 * q + 2))
                    sp.dma_start(tab[:, q * per:(q + 1) * per, :],
                                 table[bass.ds(h, 1), :, q * per:(q + 1) * per, :].rearrange("h p c n -> (h p) c n")).then_inc(tab_in[q], 16)

        @block.gpsimd
        def _(pool):
            nc.gpsimd.memset(kv_sb[:, :], 0.0).then_inc(zero_ok, 1)
            pool.sem_inc(pool_sum, LOAN)
            nc.gpsimd.tensor_copy(w_st[:, :], side_w[:, 0, :]).then_inc(ready, 1)
            nc.gpsimd.tensor_copy(x_st[:, :], xT[0:C, 0:128]).then_inc(staged, 1)
            nc.gpsimd.memset(kv_t[:, 128 + HEADS * PADT:], 0.0)

            def unit(u, at, head):
                pool.wait_ge(pool_sum, u * Q + LOAN)
                pool.wait_ge(sel_ok, u + 1)
                if head is not None:
                    nc.gpsimd.tensor_copy(w_st[:, :], side_w[:, bass.ds(head, 1), :].rearrange("p h n -> p (h n)")).then_inc(ready, 1)
                nc.gpsimd.tensor_copy(x_st[:, :], xT[0:C, at]).then_inc(staged, 1)
                nc.gpsimd.tensor_copy(sim_sum[:, :], sim_sel[:, :]).then_inc(sum_in, 1)
                pool.wait_ge(sum_in, u + 1)
                for q in range(Q):
                    pool.wait_ge(masked, u * Q + q + MASKED0 - 3)
                    sum_quarter(nc.gpsimd, q).then_inc(pool_sum, 1)

            with pool.Fori(0, HEADS) as h:
                with pool.Fori(0, TILES - 1) as t:
                    unit(h * TILES + t, bass.ds(t * 128 + 128, 128), None)
                unit(h * TILES + (TILES - 1), slice(0, 128), h + 1)

        @block.tensor
        def _(pe):
            pe.wait_ge(zero_ok, 1)
            pe.sem_inc(mul_done, MUL0)
            pe.sem_inc(turn_done, TURN0)
            pe.wait_ge(ready, 1)
            pe.wait_ge(staged, 1)
            nc.tensor.matmul(misc[:, 0:128], x_st[:, :], w_st[:, :], start=True, stop=True).then_inc(sims_done, 1)

            def turn_bank(u, k):
                if k % 2 == 0:
                    pe.wait_ge(masked, u * Q + (k // 2 + 1 + MASKED0))
                pe.wait_ge(turned_ok, u * TURNS + (k - 1 + TURNED0))
                for j in range(4):
                    at = ((4 * k + j) % (QN // 128)) * 128
                    last = nc.tensor.transpose(turn[k % 2][:, j * 128:(j + 1) * 128],
                                               weight[k // 2][:, at:at + 128], ident[:, :])
                last.then_inc(turn_done, 1)

            def multiply(u, h, k):
                if k == 0:
                    pe.wait_ge(kv_ok, u + LOAN)
                if k % 2 == 0:
                    pe.wait_ge(tab_in[k // 2], h * 16 + 16)
                pe.wait_ge(turned_ok, u * TURNS + (k + 1 + TURNED0))
                for j in range(4):
                    last = nc.tensor.matmul(out[:, 0:128], turned[k % 4][:, j * 128:(j + 1) * 128], tab[:, 4 * k + j, :],
                                            start=k == 0 and j == 0, stop=k == TURNS - 1 and j == 3)
                last.then_inc(mul_done, 1)

            def flip(u, sims=2):
                pe.wait_ge(kv_ok, u + LOAN)
                pe.wait_ge(sel_ok, u + sims)
                nc.tensor.transpose(misc[:, 128:256], kv_sb[:, :], ident[:, :]).then_inc(flip_done, 1)

            def unit(u, h, last=False):
                for k in range(TURNS):
                    if k + 1 < TURNS:
                        turn_bank(u, k + 1)
                    elif not last:
                        turn_bank(u + 1, 0)
                    if k == 0:
                        pe.wait_ge(flip_out, u + LOAN)
                        pe.wait_ge(staged, u + 2)
                        pe.wait_ge(ready, h + 1)
                        nc.tensor.matmul(misc[:, 0:128], x_st[:, :], w_st[:, :], start=True, stop=True).then_inc(sims_done, 1)
                    multiply(u, h, k)
                    if k == 1:
                        flip(u)

            turn_bank(0, 0)
            with pe.Fori(0, HEADS - 1) as h:
                with pe.Fori(0, TILES) as t:
                    unit(h * TILES + t, h)
            with pe.Fori(0, TILES - 1) as t:
                unit((HEADS - 1) * TILES + t, HEADS - 1)
            unit(UNITS - 1, HEADS - 1, last=True)
            flip(UNITS, sims=1)

        @block.scalar
        def _(act):
            act.sem_inc(kv_ok, LOAN)
            act.sem_inc(flip_out, LOAN)
            act.sem_inc(turned_ok, TURNED0)

            def exp(u, q):
                act.wait_ge(pool_sum, u * Q + (q + 1 + LOAN))
                act.wait_ge(shift_ok, u + 1)
                act.wait_ge(masked, u * Q + (q - 1 + MASKED0))
                nc.scalar.activation(expo[q % 2][:, :], total[q][:, :, :].rearrange("p j i -> p (j i)"), ACT.Exp,
                                     bias=shift[:, :]).then_inc(exp_ok, 1)

            def copy_turned(u, k):
                act.wait_ge(turn_done, u * TURNS + (k + 1 + TURN0))
                act.wait_ge(mul_done, u * TURNS + (k - 3 + MUL0))
                nc.scalar.copy(turned[k % 4][:, :], turn[k % 2][:, :]).then_inc(turned_ok, 1)

            def flipped(u):
                act.wait_ge(flip_done, u + 1)
                nc.scalar.copy(kv_t[:, bass.ds(u * 128, 128)], misc[:, 128:256]).then_inc(flip_out, 1)

            def unit(u, last):
                copy_turned(u, 1)
                exp(u, 2)
                copy_turned(u, 2)
                flipped(u)
                copy_turned(u, 3)
                exp(u, 3)
                copy_turned(u, 4)
                if not last:
                    exp(u + 1, 0)
                copy_turned(u, 5)
                copy_turned(u, 6)
                if not last:
                    exp(u + 1, 1)
                copy_turned(u, 7)
                if not last:
                    copy_turned(u + 1, 0)
                act.wait_ge(mul_done, u * TURNS + (TURNS + MUL0))
                act.wait_ge(zinv_ok, u + 1)
                act.wait_ge(flip_done, u + 1)
                nc.scalar.activation(kv_sb[:, :], out[:, 0:128], ACT.Copy, scale=zinv[:, 0:1]).then_inc(kv_ok, 1)

            exp(0, 0)
            exp(0, 1)
            copy_turned(0, 0)
            with act.Fori(0, UNITS - 1) as u:
                unit(u, False)
            unit(UNITS - 1, True)
            flipped(UNITS)

        @block.vector
        def _(dve):
            dve.sem_inc(masked, MASKED0)

            own = Chain(dve, pick)
            side = [sim_sel[:, p * KEYS:(p + 1) * KEYS] for p in range(2)]

            def take_scores(v):
                dve.sem_clear(pick)
                own.n = 0
                dve.wait_ge(sum_in, v)
                dve.wait_ge(sims_done, v + 1)
                own.step(nc.vector.tensor_copy(sim_sel[:, :], misc[:, 0:128]))
                own.wait()
                dve.sem_inc(sel_ok, 1)

            def best_of_sides():
                for p in range(2):
                    own.step(nc.vector.max(best[p][:, 0:8], side[p]))
                own.wait()
                for p in range(2):
                    own.step(nc.vector.match_replace(rest[p][:, :], best[p][:, 0:8], side[p], NEG))
                own.wait()
                for p in range(2):
                    own.step(nc.vector.max(best[p][:, 8:16], rest[p][:, :]))

            def best_of_sums():
                own.wait()
                at = 0
                for a0, a1, b0, b1 in PARTS:
                    n = (a1 - a0) * (b1 - b0)
                    own.step(nc.vector.tensor_tensor(
                        cand[:, at:at + n].rearrange("p (b a) -> p b a", a=a1 - a0),
                        spread(best[0][:, a0:a1], 1, b1 - b0), spread(best[1][:, b0:b1], 2, a1 - a0), ALU.add))
                    at += n
                own.wait()
                own.step(nc.vector.max(chosen[:, 0:8], cand[:, :]))
                own.wait()
                own.step(nc.vector.match_replace(cand2[:, :], chosen[:, 0:8], cand[:, :], NEG))
                own.wait()
                own.step(nc.vector.max(chosen[:, 8:16], cand2[:, :]))
                assert own.n == PICKS

            def set_shift():
                dve.wait_ge(pick, PICKS)
                nc.vector.tensor_scalar(shift[:, :], chosen[:, 0:1], -1.0, None, ALU.mult).then_inc(shift_ok, 1)

            def set_cut():
                dve.wait_ge(pick, PICKS)
                nc.vector.tensor_copy(cut[:, :], chosen[:, 15:16]).then_inc(cut_ok, 1)

            def mask(u, q):
                dve.wait_ge(exp_ok, u * Q + (q + 1))
                dve.wait_ge(cut_ok, u + 1)
                dve.wait_ge(turn_done, u * TURNS + (2 * q - 6 + TURN0))
                nc.vector.scalar_tensor_tensor(weight[q][:, :], total[q][:, :, :].rearrange("p j i -> p (j i)"),
                                               cut[:, 0:1], expo[q % 2][:, :], ALU.is_ge, ALU.mult,
                                               accum_out=zpart[:, q:q + 1]).then_inc(masked, 1)

            dve.wait_ge(sims_done, 1)
            own.step(nc.vector.tensor_copy(sim_sel[:, :], misc[:, 0:128]))
            own.wait()
            dve.sem_inc(sel_ok, 1)
            best_of_sides()
            best_of_sums()
            set_shift()
            set_cut()
            with dve.Fori(0, UNITS) as u:
                mask(u, 0)
                mask(u, 1)
                take_scores(u + 1)
                best_of_sides()
                mask(u, 2)
                best_of_sums()
                dve.wait_ge(exp_ok, u * Q + Q)
                set_shift()
                mask(u, 3)
                dve.wait_ge(masked, u * Q + (Q + MASKED0))
                set_cut()
                dve.wait_ge(kv_ok, u + LOAN)
                nc.vector.tensor_reduce(zinv[:, :], zpart[:, :], AX.X, ALU.add).then_inc(z_ok, 1)
                dve.wait_ge(z_ok, u + 1)
                nc.vector.reciprocal(zinv[:, :], zinv[:, :]).then_inc(zinv_ok, 1)


def rotary_attention(nc, x, xT, ident, mask, w_in, w_o, cos_sin):
    NQ, NKV, HD = 4, 2, 16
    QK, VD = (NQ + NKV) * HD, NKV * HD
    with Scope(nc, "gqa") as s:
        def two(name, shape):
            return [s.sb(f"{name}{i}", shape) for i in range(2)]
        x_g = two("x_g", [128, ROWS])
        part, turned = two("part", [ROWS, QK]), two("turned", [ROWS, QK])
        v_all, v_g = s.sb("v_all", [ROWS, GROUPS, VD]), two("v_g", [ROWS, VD])
        q_t, k_t = two("q_t", [128, NQ * ROWS]), two("k_t", [128, NKV * ROWS])
        score, prob_t = two("score", [ROWS, NQ, ROWS]), two("prob_t", [ROWS, NQ * ROWS])
        top, shift, tot, inv = (two(n, [ROWS, NQ]) for n in ("top", "shift", "tot", "inv"))
        y, y_t = two("y", [ROWS, 128]), two("y_t", [128, ROWS])
        qkv_bank, q_bank, k_bank, s_bank, p_bank, m_bank, y_bank, o_bank = (
            s.bank(n) for n in ("qkv", "q", "k", "s", "p", "m", "y", "o"))
        pad_ok, x_ok, qkv_done, part_ok, rope_ok, v_ok, vg_ok = (
            s.sem(n) for n in ("pad", "x", "qkv_done", "part", "rope", "v", "vg"))
        flip_q, flip_k, q_ok, k_ok, score_done, masked = (s.sem(n) for n in ("flip_q", "flip_k", "q_ok", "k_ok", "score", "masked"))
        top_ok, shift_ok, exp_ok, inv_ok = (s.sem(n) for n in ("top", "shift", "exp", "inv"))
        flip_p, p_ok, mix_done, y_ok, flip_y, yt_ok, out_done, x_new = (
            s.sem(n) for n in ("flip_p", "p_ok", "mix", "y_ok", "flip_y", "yt", "out", "x_new"))
        block = s.block()
        padded = [*q_t, *k_t, *y]
        PADS = len(padded)

        @block.gpsimd
        def _(pool):
            for spot in padded:
                nc.gpsimd.memset(spot[:, :], 0.0).then_inc(pad_ok, 1)
            pool.wait_ge(pad_ok, PADS)

            def step(j, k):
                if live(j):
                    await_count(pool, qkv_done, j - 1)
                    nc.gpsimd.tensor_copy(x_g[k][:, :], xT[:, bass.ds(j * ROWS, ROWS)]).then_inc(x_ok, 1)
                if live(j, -3):
                    pool.wait_ge(v_ok, j - 2)
                    await_count(pool, mix_done, j - 4)
                    nc.gpsimd.tensor_copy(v_g[1 - k][:, :], v_all[:, bass.ds(j - 3, 1), :].rearrange("p g c -> p (g c)")).then_inc(vg_ok, 1)
            skewed(pool, step, 0, 5)

        @block.tensor
        def _(pe):
            def project(g, k):
                pe.wait_ge(x_ok, g + 1)
                await_count(pe, part_ok, 3 * g)
                await_count(pe, v_ok, g)
                nc.tensor.matmul(qkv_bank[0:ROWS, 0:128], x_g[k][:, :], w_in[:, :], start=True, stop=True).then_inc(qkv_done, 1)

            def turn_rotated(g, k):
                pe.wait_ge(rope_ok, g + 1)
                await_count(pe, q_ok, g)
                await_count(pe, k_ok, g)
                for h in range(NQ):
                    last = nc.tensor.transpose(q_bank[0:HD, h * ROWS:(h + 1) * ROWS],
                                               part[k][:, h * HD:(h + 1) * HD], ident[0:ROWS, 0:ROWS])
                last.then_inc(flip_q, 1)
                for h in range(NKV):
                    last = nc.tensor.transpose(k_bank[0:HD, h * ROWS:(h + 1) * ROWS],
                                               part[k][:, (NQ + h) * HD:(NQ + h + 1) * HD], ident[0:ROWS, 0:ROWS])
                last.then_inc(flip_k, 1)

            def make_scores(g, k):
                pe.wait_ge(q_ok, g + 1)
                pe.wait_ge(k_ok, g + 1)
                await_count(pe, masked, g)
                for h in range(NQ):
                    last = nc.tensor.matmul(s_bank[0:ROWS, h * ROWS:(h + 1) * ROWS], q_t[k][:, h * ROWS:(h + 1) * ROWS],
                                            k_t[k][:, (h // 2) * ROWS:(h // 2 + 1) * ROWS], start=True, stop=True)
                last.then_inc(score_done, 1)

            def turn_probabilities(g, k):
                pe.wait_ge(exp_ok, g + 1)
                await_count(pe, p_ok, g)
                for h in range(NQ):
                    last = nc.tensor.transpose(p_bank[0:ROWS, h * ROWS:(h + 1) * ROWS], score[k][:, h, :],
                                               ident[0:ROWS, 0:ROWS])
                last.then_inc(flip_p, 1)

            def mix(g, k):
                pe.wait_ge(vg_ok, g + 1)
                await_count(pe, y_ok, g)
                pe.wait_ge(p_ok, g + 1)
                for h in range(NQ):
                    last = nc.tensor.matmul(m_bank[0:ROWS, h * HD:(h + 1) * HD], prob_t[k][:, h * ROWS:(h + 1) * ROWS],
                                            v_g[k][:, (h // 2) * HD:(h // 2 + 1) * HD], start=True, stop=True)
                last.then_inc(mix_done, 1)

            def turn_mixed(g, k):
                await_count(pe, yt_ok, g)
                pe.wait_ge(y_ok, g + 1)
                nc.tensor.transpose(y_bank[:, 0:ROWS], y[k][:, :], ident[0:ROWS, 0:ROWS]).then_inc(flip_y, 1)

            def make_output(g, k):
                await_count(pe, x_new, g)
                pe.wait_ge(yt_ok, g + 1)
                nc.tensor.matmul(o_bank[0:ROWS, 0:C], y_t[k][:, :], w_o[:, :], start=True, stop=True).then_inc(out_done, 1)

            def step(i, k):
                if live(i):
                    make_scores(i, k)
                if live(i, 1):
                    turn_rotated(i + 1, 1 - k)
                if live(i, -2):
                    mix(i - 2, k)
                if live(i, -3):
                    make_output(i - 3, 1 - k)
                if live(i, 2):
                    project(i + 2, k)
                if live(i, -1):
                    turn_probabilities(i - 1, 1 - k)
                if live(i, -2):
                    turn_mixed(i - 2, k)

            pe.wait_ge(pad_ok, PADS)
            skewed(pe, step, 2, 3)

        @block.scalar
        def _(act):
            def step(i, k):
                if live(i, 1):
                    act.wait_ge(flip_q, i + 2)
                    nc.scalar.copy(q_t[1 - k][0:HD, :], q_bank[0:HD, 0:NQ * ROWS]).then_inc(q_ok, 1)
                if live(i):
                    act.wait_ge(shift_ok, i + 1)
                    for h in range(NQ):
                        last = nc.scalar.activation(score[k][:, h, :], score[k][:, h, :], ACT.Exp, scale=HD ** -0.5,
                                                    bias=shift[k][:, h:h + 1], accum_out=tot[k][:, h:h + 1])
                    last.then_inc(exp_ok, 1)
                if live(i, -1):
                    act.wait_ge(flip_p, i)
                    nc.scalar.copy(prob_t[1 - k][:, :], p_bank[0:ROWS, 0:NQ * ROWS]).then_inc(p_ok, 1)
                if live(i, -2):
                    act.wait_ge(flip_y, i - 1)
                    nc.scalar.copy(y_t[k][:, :], y_bank[:, 0:ROWS]).then_inc(yt_ok, 1)

            act.wait_ge(pad_ok, PADS)
            skewed(act, step, 2, 3)

        @block.vector
        def _(dve):
            def rotate(g, k):
                dve.wait_ge(qkv_done, g + 1)
                b = qkv_bank[0:ROWS, 0:QK]
                halves = [a.rearrange("p (h s d) -> p h s d", s=2, d=HD // 2) for a in (b, turned[k][:, :])]
                nc.vector.tensor_tensor(part[k][:, :].rearrange("p (h d) -> p h d", d=HD), b.rearrange("p (h d) -> p h d", d=HD),
                                        spread(cos_sin[:, 0, :], 1, NQ + NKV), ALU.mult).then_inc(part_ok, 1)
                for d in range(2):
                    nc.vector.tensor_tensor(halves[1][:, :, d, :], halves[0][:, :, 1 - d, :],
                                            spread(cos_sin[:, 1, d * 8:d * 8 + 8], 1, NQ + NKV), ALU.mult).then_inc(part_ok, 1)
                nc.vector.tensor_copy(v_all[:, bass.ds(g, 1), :].rearrange("p g c -> p (g c)"),
                                      qkv_bank[0:ROWS, QK:QK + VD]).then_inc(v_ok, 1)
                dve.wait_ge(part_ok, 3 * g + 3)
                nc.vector.tensor_tensor(part[k][:, :], part[k][:, :], turned[k][:, :], ALU.add).then_inc(rope_ok, 1)

            def mask_scores(g, k):
                dve.wait_ge(score_done, g + 1)
                nc.vector.tensor_tensor(score[k][:, :, :], s_bank[0:ROWS, 0:NQ * ROWS].rearrange("p (h t) -> p h t", h=NQ),
                                        spread(mask[:, :], 1, NQ), ALU.add).then_inc(masked, 1)
                dve.wait_ge(masked, g + 1)
                nc.vector.tensor_reduce(top[k][:, :], score[k][:, :, :], AX.X, ALU.max).then_inc(top_ok, 1)
                dve.wait_ge(top_ok, g + 1)
                nc.vector.tensor_scalar(shift[k][:, :], top[k][:, :], -HD ** -0.5, None, ALU.mult).then_inc(shift_ok, 1)

            def add_output(g):
                dve.wait_ge(out_done, g + 1)
                row = x[:, bass.ds(g, 1), :].rearrange("p g c -> p (g c)")
                nc.vector.tensor_tensor(row, row, o_bank[0:ROWS, 0:C], ALU.add).then_inc(x_new, 1)

            def scale_mixed(g, k):
                dve.wait_ge(inv_ok, g + 1)
                dve.wait_ge(mix_done, g + 1)
                nc.vector.tensor_tensor(y[k][:, 0:C].rearrange("p (h d) -> p h d", h=NQ),
                                        m_bank[0:ROWS, 0:C].rearrange("p (h d) -> p h d", h=NQ),
                                        spread(inv[k][:, :], 2, HD), ALU.mult).then_inc(y_ok, 1)

            def step(i, k):
                if live(i):
                    mask_scores(i, k)
                if live(i, -2):
                    scale_mixed(i - 2, k)
                if live(i, 1):
                    dve.wait_ge(flip_k, i + 2)
                    nc.vector.tensor_copy(k_t[1 - k][0:HD, :], k_bank[0:HD, 0:NKV * ROWS]).then_inc(k_ok, 1)
                if live(i, 2):
                    rotate(i + 2, k)
                if live(i, -3):
                    add_output(i - 3)
                if live(i, -1):
                    dve.wait_ge(exp_ok, i)
                    nc.vector.reciprocal(inv[1 - k][:, :], tot[1 - k][:, :]).then_inc(inv_ok, 1)

            dve.wait_ge(pad_ok, PADS)
            skewed(dve, step, 2, 3)


def gates(nc, xT, w, gate):
    with Scope(nc, "gate") as s:
        prob, best = s.sb("prob", [ROWS, GROUPS, NEXP]), s.sb("best", [ROWS, GROUPS, 8])
        red = s.sb("red", [ROWS, GROUPS])
        logits = s.bank("logits")
        logits_done, centered, exp_ok, own_sem = (s.sem(n) for n in ("logits", "sub", "exp", "own"))
        block = s.block()

        @block.tensor
        def _(pe):
            for g in range(GROUPS):
                last = nc.tensor.matmul(logits[0:ROWS, g * NEXP:(g + 1) * NEXP], xT[0:C, g * ROWS:(g + 1) * ROWS], w[:, :],
                                        start=True, stop=True)
            last.then_inc(logits_done, 1)

        @block.scalar
        def _(act):
            act.wait_ge(centered, 1)
            nc.scalar.activation(prob[:, :, :], prob[:, :, :], ACT.Exp).then_inc(exp_ok, 1)

        @block.vector
        def _(dve):
            own = Chain(dve, own_sem)

            def then(ins):
                own.step(ins)
                own.wait()

            dve.wait_ge(logits_done, 1)
            then(nc.vector.tensor_reduce(red[:, :], logits[0:ROWS, 0:GROUPS * NEXP].rearrange("p (g e) -> p g e", g=GROUPS), AX.X, ALU.max))
            nc.vector.tensor_tensor(prob[:, :, :], logits[0:ROWS, 0:GROUPS * NEXP].rearrange("p (g e) -> p g e", g=GROUPS),
                                    spread(red[:, :], 2, NEXP), ALU.subtract).then_inc(centered, 1)
            dve.wait_ge(exp_ok, 1)
            then(nc.vector.tensor_reduce(red[:, :], prob[:, :, :], AX.X, ALU.add))
            then(nc.vector.reciprocal(red[:, :], red[:, :]))
            then(nc.vector.tensor_tensor(prob[:, :, :], prob[:, :, :], spread(red[:, :], 2, NEXP), ALU.mult))
            for g in range(GROUPS):
                own.step(nc.vector.max(best[:, g, :], prob[:, g, :]))
            own.wait()
            then(nc.vector.tensor_tensor(red[:, :], best[:, :, 0], best[:, :, 1], ALU.add))
            then(nc.vector.tensor_scalar(red[:, :], red[:, :], 1e-9, None, ALU.add))
            then(nc.vector.reciprocal(red[:, :], red[:, :]))
            then(nc.vector.tensor_tensor(gate[:, :, :], prob[:, :, :], best[:, :, 1:2].broadcast_to([ROWS, GROUPS, NEXP]), ALU.is_ge))
            then(nc.vector.tensor_tensor(gate[:, :, :], gate[:, :, :], prob[:, :, :], ALU.mult))
            nc.vector.tensor_tensor(gate[:, :, :], gate[:, :, :], spread(red[:, :], 2, NEXP), ALU.mult)


def experts(nc, hid, x, xT, gate, w1, w3, w2, w2_rest):
    PAIR = 2 * ROWS
    PAIRS = GROUPS // 2
    rows = [128] * NEXP + [n * REST for _, n in RESTS]
    starts = [sum(rows[:c]) for c in range(len(rows))]
    HC = len(rows)

    def freed(i, c):
        return HC * i + (c - 2 if c < HC % 4 else c - 3)

    with Scope(nc, "moe") as s:
        x_p = [s.sb(f"x_p{i}", [128, PAIR]) for i in range(2)]
        silu = [s.sb(f"silu{i}", [128, PAIR]) for i in range(4)]
        hidden = [s.sb(f"hidden{i}", [128, HC, PAIR]) for i in range(2)]
        gated = [s.sb(f"gated{i}", [ROWS, NEXP, C]) for i in range(2)]
        mixed = [s.sb(f"mixed{i}", [ROWS, C]) for i in range(2)]
        up = [s.bank(f"up{i}") for i in range(4)]
        down = [s.bank(f"down{i}") for i in range(2)]
        x_ok, up_done, silu_ok, hidden_ok = (s.sem(n) for n in ("x", "up", "silu", "hidden"))
        down_done, gated_ok, mixed_ok, hid_x = s.sem("down"), s.sem("gated"), s.sem("mixed"), s.sem("hid_x")
        block = s.block()

        @block.gpsimd
        def _(pool):
            def step(i, k):
                if live(i, 0, PAIRS):
                    await_count(pool, up_done, HC * (i - 1))
                    nc.gpsimd.tensor_copy(x_p[k][:, :], xT[:, bass.ds(i * PAIR, PAIR)]).then_inc(x_ok, 1)
            skewed(pool, step, 0, 2, PAIRS)

        @block.tensor
        def _(pe):
            def step(i, k):
                if live(i, 0, PAIRS):
                    pe.wait_ge(x_ok, i + 1)
                    for c, m in enumerate(rows):
                        await_count(pe, hidden_ok, freed(i, c))
                        for at, w in ((0, w1), (256, w3)):
                            last = nc.tensor.matmul(up[c % 4][0:m, at:at + PAIR], w[:, starts[c]:starts[c] + m], x_p[k][:, :],
                                                    start=True, stop=True)
                        last.then_inc(up_done, 1)
                if live(i, -1, PAIRS):
                    pe.wait_ge(hidden_ok, HC * i)
                    await_count(pe, gated_ok, 2 * (i - 1))
                    for n in range(2):
                        for c in range(NEXP):
                            nc.tensor.matmul(down[n][0:ROWS, c * C:(c + 1) * C], hidden[1 - k][:, c, n * ROWS:(n + 1) * ROWS],
                                             w2[:, c, :], start=c == 0, stop=False)
                        for c, (e, m) in enumerate(RESTS):
                            last = nc.tensor.matmul(down[n][0:ROWS, e * C:(e + m) * C],
                                                    hidden[1 - k][0:m * REST, NEXP + c, n * ROWS:(n + 1) * ROWS],
                                                    w2_rest[0:m * REST, c, 0:m, :], start=False, stop=c == len(RESTS) - 1)
                        last.then_inc(down_done, 1)
            skewed(pe, step, 0, 2, PAIRS)

        @block.scalar
        def _(act):
            def step(i, k):
                if live(i, 0, PAIRS):
                    for c, m in enumerate(rows):
                        act.wait_ge(up_done, HC * i + (c + 1))
                        await_count(act, hidden_ok, freed(i, c))
                        nc.scalar.activation(silu[c % 4][0:m, :], up[c % 4][0:m, 0:PAIR], ACT.Silu).then_inc(silu_ok, 1)
            skewed(act, step, 0, 2, PAIRS)

        @block.vector
        def _(dve):
            nc.vector.tensor_tensor(hid[:, :, :], hid[:, :, :], x[:, :, :], ALU.add).then_inc(hid_x, 1)
            dve.wait_ge(hid_x, 1)

            def add_outputs(i):
                for n in range(2):
                    dve.wait_ge(down_done, 2 * i + (n + 1))
                    one = bass.ds(2 * i + n, 1)
                    nc.vector.tensor_tensor(gated[n][:, :, :], down[n][0:ROWS, :].rearrange("p (e c) -> p e c", e=NEXP),
                                            gate[:, one, :].rearrange("p o e -> p e o").broadcast_to([ROWS, NEXP, C]), ALU.mult).then_inc(gated_ok, 1)
                for n in range(2):
                    dve.wait_ge(gated_ok, 2 * i + (n + 1))
                    nc.vector.tensor_reduce(mixed[n][:, :], gated[n][:, :, :].rearrange("p e c -> p c e"), AX.X, ALU.add).then_inc(mixed_ok, 1)
                for n in range(2):
                    dve.wait_ge(mixed_ok, 2 * i + n + 1)
                    row = hid[:, bass.ds(2 * i + n, 1), :].rearrange("p g c -> p (g c)")
                    nc.vector.tensor_tensor(row, row, mixed[n][:, :], ALU.add)

            def step(i, k):
                for c, m in enumerate(rows):
                    if c == HC // 2 and live(i, -2, PAIRS):
                        add_outputs(i - 2)
                    if live(i, 0, PAIRS):
                        if c == 0:
                            await_count(dve, down_done, 2 * (i - 1))
                        dve.wait_ge(silu_ok, HC * i + (c + 1))
                        nc.vector.tensor_tensor(hidden[k][0:m, c, :], silu[c % 4][0:m, :], up[c % 4][0:m, 256:256 + PAIR],
                                                ALU.mult).then_inc(hidden_ok, 1)
            skewed(dve, step, 0, 2, PAIRS)


def by_parity(a, odd):
    return a.rearrange("p (m n) c -> p n m c", n=2)[:, odd, :, :]


def vision_tower(nc, x_img, cls_tok, tok_w, tok_b, a_wq, a_wk, a_wv, a_mlp, a_b, unmix,
                 ln1, ln2, wqkv, wo, router, w1, w2, w2_rest, w3, rope,
                 key_m, query_m, value_in, value_out, pk_w, pk_k, mem_wq, table, mem_wo, ident_in, mask_in, out):
    Scope.spent = []
    with Scope(nc, "all") as s:
        hid = s.sb("hid", [ROWS, GROUPS, C])
        x = s.sb("x", [ROWS, GROUPS, C])
        xT = s.sb("xT", [128, COLS])
        ident, mask = s.sb("ident", [128, 128]), s.sb("mask", [ROWS, ROWS])

        side_w = s.sb("side_w", [C, HEADS + 1, 128])
        wq, wv = s.sb("wq", [128, HEADS, C]), s.sb("wv", [128, HEADS, C])
        later_in = s.sem("later_in")

        with Scope(nc, "early") as f:
            w_in, w_o, cos_sin = f.sb("w_in", [128, 128]), f.sb("w_o", [128, C]), f.sb("cos_sin", [ROWS, 2, 16])
            router_w = f.sb("router_w", [C, NEXP])
            up_w = [f.sb(f"up_w{n}", [128, NEXP * HID]) for n in range(2)]
            down_w, down_rest = f.sb("down_w", [128, NEXP, C]), f.sb("down_rest", [3 * REST, len(RESTS), 3, C])
            raw = [f.sb(f"raw{n}", [C, HEADS, C]) for n in range(4)]
            a, b = f.sb("a", [32, 2 * HEADS, C]), f.sb("b", [32, 2 * HEADS, C])
            score_w, value_w = f.sb("score_w", [128, HEADS, C]), f.sb("value_w", [128, HEADS, C])
            later = [(w_in[0:C, :], wqkv), (w_o[0:C, :], wo), (cos_sin[:, :, :], rope), (router_w[:, :], router),
                     (up_w[0][0:C, :], w1), (up_w[1][0:C, :], w3), (down_w[:, :, :], w2), (down_rest[:, :, :, :], w2_rest),
                     *((r[:, :, :], m) for r, m in zip(raw, (key_m, query_m, value_in, value_out))),
                     (a[:, :, :], pk_w), (b[:, :, :], pk_k), (wq[0:C, :, :], mem_wq),
                     (by_parity(wv[C:128, :, :], 0), by_parity(mem_wo, 0)), (by_parity(wv[0:C, :, :], 1), by_parity(mem_wo, 1))]
            zeroed = [xT[C:128, :], w_in[C:128, :], w_o[C:128, :], up_w[0][C:128, :], up_w[1][C:128, :],
                      score_w[C:128, :, :], value_w[C:128, :, :], side_w[:, HEADS, :], wq[C:128, :, :],
                      by_parity(wv[0:C, :, :], 0), by_parity(wv[C:128, :, :], 1)]

            load(nc, "consts", [(ident[:, :], ident_in), (mask[:, :], mask_in)])
            embed(nc, hid, x_img, tok_w, cls_tok, tok_b, ident, later, later_in, zeroed)
            normalize(nc, "ln_a", hid, x, xT, ident, True, 1e-5)
            relu_attention(nc, hid, xT, ident, a_wq, a_wk, a_wv, a_mlp, a_b, unmix, later_in, 16 * len(later))
            normalize(nc, "ln_b", hid, x, xT, ident, True, 1e-5)
            with Scope(nc, "first") as g:
                scaled = g.sb("scaled", [ROWS, GROUPS, C])
                gate = g.sb("gate", [ROWS, GROUPS, NEXP])
                normalize(nc, "rms_a", x, scaled, xT, ident, False, 1e-6, ln1)
                rotary_attention(nc, x, xT, ident, mask, w_in, w_o, cos_sin)
                normalize(nc, "rms_b", x, scaled, xT, ident, False, 1e-6, ln2)
                gates(nc, xT, router_w, gate)
                experts(nc, hid, x, xT, gate, up_w[0], up_w[1], down_w, down_rest)

            merge(nc, "merge",
                  [(raw[2 * m][:, h, :], raw[2 * m + 1][:, h, :]) for m in range(2) for h in range(HEADS)]
                  + [(a[:, n, :], b[:, n, :]) for n in range(2 * HEADS)],
                  [w[0:C, :, :].rearrange("p h c -> p (h c)") for w in (score_w, value_w)]
                  + [side_w[:, 4 * m:4 * m + 4, :].rearrange("p h c -> p (h c)") for m in range(2)])
            normalize(nc, "ln_c", hid, x, xT, ident, True, 1e-5, twice=True)
            head_attention(nc, "mha", hid, xT, ident, mask, score_w, value_w, 1.0)

        normalize(nc, "ln_d", hid, x, xT, ident, True, 1e-5)
        with Scope(nc, "memory") as f:
            kv_t = f.sb("kv_t", [128, KVT])
            product_keys(nc, xT, ident, side_w, table, kv_t)
            head_attention(nc, "mem", hid, xT, ident, mask, wq, wv, C ** -0.5, kv_t)
        load(nc, "store", [(out, hid[:, :, :])])


def _constants():
    mask = np.full((ROWS, ROWS), -1e30, np.float32)
    for m in range(PER):
        for i in range(TOK):
            mask[m * TOK + i, m * TOK:m * TOK + i + 1] = 0
    unmix = np.zeros((C, C), np.float32)
    for g in range(2):
        for d in range(32):
            unmix[g * 32 + d, d * 2 + g] = 1
    hd = 16
    inv = 1.0 / 10000.0 ** (np.arange(0, hd, 2, dtype=np.float32) / hd)
    angle = np.outer(np.arange(TOK, dtype=np.float32), inv)
    sin, cos = np.sin(angle), np.cos(angle)
    table = np.stack([np.concatenate([cos, cos], 1), np.concatenate([-sin, sin], 1)], 1)
    return {"unmix": unmix, "rope": np.tile(table, (PER, 1, 1)).astype(np.float32),
            "ident_in": np.eye(128, dtype=np.float32), "mask_in": mask}


def kernel(x, cls_tok, L0_tok_W, L0_tok_b, L0_attn_Wq, L0_attn_Wk, L0_attn_Wv, L0_attn_w_mlp, L0_attn_b_mlp,
           L0_ffn_ln1_w, L0_ffn_ln2_w, L0_ffn_wq, L0_ffn_wk, L0_ffn_wv, L0_ffn_wo, L0_ffn_router_w, L0_ffn_w1,
           L0_ffn_w2, L0_ffn_w3, L1_attn_key_matrices, L1_attn_query_matrices, L1_attn_value_in_matrices,
           L1_attn_value_out_matrices, L1_ffn_Wq_pk, L1_ffn_pk_keys, L1_ffn_Wq, L1_ffn_keys_table,
           L1_ffn_values_table, L1_ffn_Wo):
    import concourse.bacc as bacc
    from concourse.bass_utils import run_bass_kernel_spmd

    patches = np.asarray(x).reshape(IMAGES, 3, 6, 16, 6, 16).transpose(0, 2, 4, 1, 3, 5).reshape(IMAGES, 36, 768)
    tokens = np.zeros((GROUPS * PER, TOK, 768), np.float32)
    tokens[:IMAGES, 1:] = patches
    consts = _constants()
    sides = [np.asarray(t).reshape(HEADS, ENT, C) for t in (L1_ffn_keys_table, L1_ffn_values_table)]
    table = np.concatenate([np.concatenate([sides[h % 2][h], sides[1 - h % 2][h]], 1) for h in range(HEADS)])
    def chunked(w):
        w = np.asarray(w).transpose(2, 0, 1)
        return np.concatenate([w[:, :, :128].reshape(C, -1), w[:, :, 128:].reshape(C, -1)], 1)
    down = np.asarray(L0_ffn_w2)
    down_rest = np.zeros((3 * REST, len(RESTS), 3, C), np.float32)
    for c, (first, n) in enumerate(RESTS):
        for e in range(n):
            down_rest[e * REST:(e + 1) * REST, c, e] = down[first + e, :, 128:].T
    arrays = {
        "x_img": tokens.reshape(GROUPS // 2, 2 * ROWS, KCH, 128).transpose(0, 3, 2, 1).reshape(GROUPS // 2, 128, KCH * 2 * ROWS),
        "cls_tok": np.asarray(cls_tok).reshape(1, C),
        "tok_w": np.asarray(L0_tok_W).T.reshape(KCH, 128, C).transpose(1, 0, 2).reshape(128, KCH * C),
        "tok_b": L0_tok_b,
        "a_wq": np.asarray(L0_attn_Wq).T, "a_wk": np.asarray(L0_attn_Wk).T,
        "a_wv": np.asarray(L0_attn_Wv).reshape(32, 2, C).transpose(1, 0, 2).reshape(C, C).T,
        "a_mlp": L0_attn_w_mlp, "a_b": L0_attn_b_mlp, "unmix": consts["unmix"],
        "ln1": L0_ffn_ln1_w, "ln2": L0_ffn_ln2_w,
        "wqkv": np.concatenate([L0_ffn_wq, L0_ffn_wk, L0_ffn_wv]).T, "wo": np.asarray(L0_ffn_wo).T,
        "router": np.asarray(L0_ffn_router_w).T,
        "w1": chunked(L0_ffn_w1), "w3": chunked(L0_ffn_w3),
        "w2": down[:, :, :128].transpose(2, 0, 1), "w2_rest": down_rest,
        "rope": consts["rope"],
        "key_m": np.asarray(L1_attn_key_matrices).transpose(2, 0, 1),
        "query_m": np.asarray(L1_attn_query_matrices).transpose(2, 0, 1),
        "value_in": np.asarray(L1_attn_value_in_matrices).transpose(2, 0, 1),
        "value_out": np.asarray(L1_attn_value_out_matrices).transpose(1, 0, 2),
        "pk_w": np.asarray(L1_ffn_Wq_pk).reshape(C, 2, HEADS, 32).transpose(3, 2, 1, 0).reshape(32, 2 * HEADS, C),
        "pk_k": np.asarray(L1_ffn_pk_keys).transpose(3, 2, 0, 1).reshape(32, 2 * HEADS, KEYS),
        "mem_wq": np.asarray(L1_ffn_Wq).reshape(C, HEADS, C),
        "table": table.reshape(HEADS, CHUNKS, 128, 128).transpose(0, 2, 1, 3),
        "mem_wo": np.asarray(L1_ffn_Wo).reshape(HEADS, C, C).transpose(1, 0, 2),
        "ident_in": consts["ident_in"], "mask_in": consts["mask_in"],
    }
    nc = bacc.Bacc("TRN2", target_bir_lowering=False, num_devices=1)
    arrays = {f"in_{n}": np.ascontiguousarray(a) for n, a in arrays.items()}
    args = {n[3:]: nc.dram_tensor(n, a.shape, mybir.dt.from_np(a.dtype), kind="ExternalInput").ap() for n, a in arrays.items()}
    out = nc.dram_tensor("out", (ROWS, GROUPS, C), F32, kind="ExternalOutput").ap()
    vision_tower(nc, **args, out=out)
    got = run_bass_kernel_spmd(nc, [arrays], core_ids=[0]).results[0]["out"]
    return got.transpose(1, 0, 2).reshape(GROUPS * PER, TOK, C)[:IMAGES]
```
